# Optimizing a Trainium2 kernel written in Bass

```python
import numpy as np
import jax
import jax.numpy as jnp

def _softmax(x, axis=-1):
    return jax.nn.softmax(x, axis=axis)

def _gelu(x):
    return jax.nn.gelu(x, approximate=True)

def _silu(x):
    return jax.nn.silu(x)

def _sigmoid(x):
    return jax.nn.sigmoid(x)

def _layernorm(x, axis=-1, eps=1e-05):
    m = jnp.mean(x, axis=axis, keepdims=True)
    v = jnp.var(x, axis=axis, keepdims=True)
    return (x - m) / jnp.sqrt(v + eps)

def _scatter_add(tgt, idx, src, axis=0):
    return tgt.at[idx].add(src)

def _segment_sum(src, seg, n):
    return jax.ops.segment_sum(src, seg, n)
kernel_name = 'mk_vit_tower_d2_tok_img768_r4_ed369b'

def setup_inputs(seed: int=0):
    np.random.seed(seed)
    _w = jnp.asarray

    def _rec_inputs():
        import jax
        import jax.numpy as jnp
        _rk = jax.random.key(seed)
        x = 7.57192e-06 + 1.00007 * jax.random.normal(jax.random.fold_in(_rk, 1), (64, 224, 224, 3), jnp.float32)
        return x
    x = _rec_inputs()

    def _L0_tok_setup():
        import jax, jax.numpy as jnp
        import numpy as np
        IMG = 224
        P = 16
        HP = P // 2
        D = 192
        C_IN = 3
        B = 64

        def _crop_shift_pad(images, oh, ow):
            th = IMG - HP
            tw = IMG - HP
            out = jnp.zeros_like(images)
            return out.at[:, oh:oh + th, ow:ow + tw, :].set(images[:, oh:oh + th, ow:ow + tw, :])
        key = jax.random.key(seed)
        k1, k2 = jax.random.split(key, 2)
        images = jax.random.normal(k1, (B, IMG, IMG, C_IN), dtype=jnp.float32)
        pvs = P * P * C_IN * 5
        W = jax.random.normal(k2, (pvs, D), dtype=jnp.float32) * 0.02
        b = jnp.zeros((D,), dtype=jnp.float32)
        return {'images': images, 'W': W, 'b': b}
    _L0_tok_all = _L0_tok_setup()
    _L0_tok_in = {k: v for k, v in _L0_tok_all.items() if k in ('W', 'b')}
    del _L0_tok_all

    def _L0_attn_setup():
        import jax, jax.numpy as jnp
        import numpy as np
        N_HEADS = 12
        key = jax.random.key(seed)
        k1, k2, k3 = jax.random.split(key, 3)
        B, S, W = (8, 256, 192)
        x = jax.random.normal(k1, (B, S, W), dtype=jnp.float32)
        w_qkv = jax.random.normal(k2, (W, 3 * W), dtype=jnp.float32) * W ** (-0.5)
        w_out = jax.random.normal(k3, (W, W), dtype=jnp.float32) * W ** (-0.5)
        return {'x': x, 'w_qkv': w_qkv, 'w_out': w_out}
    _L0_attn_all = _L0_attn_setup()
    _L0_attn_in = {k: v for k, v in _L0_attn_all.items() if k in ('w_qkv', 'w_out')}
    del _L0_attn_all

    def _L0_ffn_setup():
        import jax, jax.numpy as jnp
        import numpy as np
        DIM = 192
        H = 12
        HD = 64
        SHARED = 2
        ROUTED = 2
        E_ROUTED = H - SHARED
        LN_EPS = 1e-05

        def _layernorm(x, w, b):
            m = x.mean(-1, keepdims=True)
            v = ((x - m) ** 2).mean(-1, keepdims=True)
            return (x - m) * jax.lax.rsqrt(v + LN_EPS) * w + b
        key = jax.random.key(seed)
        ks = jax.random.split(key, 12)
        B, N = (4, 512)
        s = 0.02
        return {'x': jax.random.normal(ks[0], (B, N, DIM), jnp.float32), 'qkv_w': jax.random.normal(ks[1], (DIM, 3 * H * HD), jnp.float32) * s, 'qkv_b': jnp.zeros((3 * H * HD,), jnp.float32), 'q_norm_w': jnp.ones((HD,), jnp.float32), 'q_norm_b': jnp.zeros((HD,), jnp.float32), 'k_norm_w': jnp.ones((HD,), jnp.float32), 'k_norm_b': jnp.zeros((HD,), jnp.float32), 'wg_w': jax.random.normal(ks[2], (DIM, E_ROUTED), jnp.float32) * s, 'wg0_w': jax.random.normal(ks[3], (DIM, 2), jnp.float32) * s, 'wg1_w': jax.random.normal(ks[4], (DIM, SHARED), jnp.float32) * s, 'proj_w': jax.random.normal(ks[5], (H * HD, DIM), jnp.float32) * s, 'proj_b': jnp.zeros((DIM,), jnp.float32)}
    _L0_ffn_all = _L0_ffn_setup()
    _L0_ffn_in = {k: v for k, v in _L0_ffn_all.items() if k in ('qkv_w', 'qkv_b', 'q_norm_w', 'q_norm_b', 'k_norm_w', 'k_norm_b', 'wg_w', 'wg0_w', 'wg1_w', 'proj_w', 'proj_b')}
    del _L0_ffn_all

    def _L1_attn_setup():
        import jax, jax.numpy as jnp
        import numpy as np
        B, N, C = (2, 1024, 192)
        H = 12
        HD = C // H
        THETA = 10000.0

        def _rope_tables(n, hd, dtype):
            inv = 1.0 / THETA ** (jnp.arange(0, hd, 2, dtype=jnp.float32) / hd)
            freqs = jnp.arange(n, dtype=jnp.float32)[:, None] * inv[None, :]
            cos = jnp.concatenate([jnp.cos(freqs), jnp.cos(freqs)], axis=-1).astype(dtype)
            sin = jnp.concatenate([jnp.sin(freqs), jnp.sin(freqs)], axis=-1).astype(dtype)
            return (cos, sin)

        def _rotate_half(x):
            x1, x2 = (x[..., :x.shape[-1] // 2], x[..., x.shape[-1] // 2:])
            return jnp.concatenate([-x2, x1], axis=-1)
        key = jax.random.key(seed)
        k1, k2, k3 = jax.random.split(key, 3)
        x = jax.random.normal(k1, (B, N, C), dtype=jnp.float32)
        w_qkv = jax.random.normal(k2, (3 * C, C), dtype=jnp.float32) * C ** (-0.5)
        b_qkv = jnp.zeros((3 * C,), dtype=jnp.float32)
        w_proj = jax.random.normal(k3, (C, C), dtype=jnp.float32) * C ** (-0.5)
        b_proj = jnp.zeros((C,), dtype=jnp.float32)
        return {'x': x, 'w_qkv': w_qkv, 'b_qkv': b_qkv, 'w_proj': w_proj, 'b_proj': b_proj}
    _L1_attn_all = _L1_attn_setup()
    _L1_attn_in = {k: v for k, v in _L1_attn_all.items() if k in ('w_qkv', 'b_qkv', 'w_proj', 'b_proj')}
    del _L1_attn_all

    def _L1_ffn_setup():
        import jax, jax.numpy as jnp
        import numpy as np
        B, T, C = (4, 512, 192)
        E, K = (8, 2)

        def _mlp(x, wfc, wproj):
            h = jnp.square(jax.nn.relu(x @ wfc))
            return h @ wproj
        key = jax.random.key(seed)
        ks = jax.random.split(key, 6)
        s = 0.02
        return {'x': jax.random.normal(ks[0], (B, T, C), jnp.float32), 'w_fc_sh': jax.random.normal(ks[1], (C, C), jnp.float32) * s, 'w_proj_sh': jax.random.normal(ks[2], (C, C), jnp.float32) * s, 'w1': jax.random.normal(ks[3], (E, C, C), jnp.float32) * s, 'w2': jax.random.normal(ks[4], (E, C, C), jnp.float32) * s, 'router_w': jax.random.normal(ks[5], (E, C), jnp.float32) * s, 'balance_bias': jnp.zeros((E,), jnp.float32)}
    _L1_ffn_all = _L1_ffn_setup()
    _L1_ffn_in = {k: v for k, v in _L1_ffn_all.items() if k in ('w_fc_sh', 'w_proj_sh', 'w1', 'w2', 'router_w', 'balance_bias')}
    del _L1_ffn_all
    return {'x': x, 'L0_tok_W': _L0_tok_in['W'], 'L0_tok_b': _L0_tok_in['b'], 'L0_attn_w_qkv': _L0_attn_in['w_qkv'], 'L0_attn_w_out': _L0_attn_in['w_out'], 'L0_ffn_qkv_w': _L0_ffn_in['qkv_w'], 'L0_ffn_qkv_b': _L0_ffn_in['qkv_b'], 'L0_ffn_q_norm_w': _L0_ffn_in['q_norm_w'], 'L0_ffn_q_norm_b': _L0_ffn_in['q_norm_b'], 'L0_ffn_k_norm_w': _L0_ffn_in['k_norm_w'], 'L0_ffn_k_norm_b': _L0_ffn_in['k_norm_b'], 'L0_ffn_wg_w': _L0_ffn_in['wg_w'], 'L0_ffn_wg0_w': _L0_ffn_in['wg0_w'], 'L0_ffn_wg1_w': _L0_ffn_in['wg1_w'], 'L0_ffn_proj_w': _L0_ffn_in['proj_w'], 'L0_ffn_proj_b': _L0_ffn_in['proj_b'], 'L1_attn_w_qkv': _L1_attn_in['w_qkv'], 'L1_attn_b_qkv': _L1_attn_in['b_qkv'], 'L1_attn_w_proj': _L1_attn_in['w_proj'], 'L1_attn_b_proj': _L1_attn_in['b_proj'], 'L1_ffn_w_fc_sh': _L1_ffn_in['w_fc_sh'], 'L1_ffn_w_proj_sh': _L1_ffn_in['w_proj_sh'], 'L1_ffn_w1': _L1_ffn_in['w1'], 'L1_ffn_w2': _L1_ffn_in['w2'], 'L1_ffn_router_w': _L1_ffn_in['router_w'], 'L1_ffn_balance_bias': _L1_ffn_in['balance_bias']}

def reference(x, L0_tok_W, L0_tok_b, L0_attn_w_qkv, L0_attn_w_out, L0_ffn_qkv_w, L0_ffn_qkv_b, L0_ffn_q_norm_w, L0_ffn_q_norm_b, L0_ffn_k_norm_w, L0_ffn_k_norm_b, L0_ffn_wg_w, L0_ffn_wg0_w, L0_ffn_wg1_w, L0_ffn_proj_w, L0_ffn_proj_b, L1_attn_w_qkv, L1_attn_b_qkv, L1_attn_w_proj, L1_attn_b_proj, L1_ffn_w_fc_sh, L1_ffn_w_proj_sh, L1_ffn_w1, L1_ffn_w2, L1_ffn_router_w, L1_ffn_balance_bias):
    import jax
    import jax.numpy as jnp

    def _L0_tok_ref(images, W, b):
        import jax, jax.numpy as jnp
        import numpy as np
        IMG = 224
        P = 16
        HP = P // 2
        D = 192
        C_IN = 3
        B = 64

        def _crop_shift_pad(images, oh, ow):
            th = IMG - HP
            tw = IMG - HP
            out = jnp.zeros_like(images)
            return out.at[:, oh:oh + th, ow:ow + tw, :].set(images[:, oh:oh + th, ow:ow + tw, :])
        offsets = [(0, 0), (HP, 0), (0, HP), (HP, HP)]
        concat = jnp.concatenate([images] + [_crop_shift_pad(images, oh, ow) for oh, ow in offsets], axis=-1)
        Bn, _, _, C = concat.shape
        g = IMG // P
        x = concat.reshape(Bn, g, P, g, P, C)
        x = x.transpose(0, 1, 3, 2, 4, 5).reshape(Bn, g * g, P * P * C)
        return x @ W + b

    def _L0_attn_ref(x, w_qkv, w_out):
        import jax, jax.numpy as jnp
        import numpy as np
        N_HEADS = 12
        B, S, W = x.shape
        H = N_HEADS
        D = W // H
        scale = W ** (-0.5)
        qkv = x @ w_qkv
        q, k, v = jnp.split(qkv, 3, axis=2)
        q = q.reshape(B, S, H, D)
        k = k.reshape(B, S, H, D)
        attn_score = jnp.einsum('binh,bjnh->bijn', q, k) * scale
        attn_weight = jax.nn.softmax(attn_score, axis=2)
        out = jnp.einsum('bijn,bjnh->binh', attn_weight, k)
        out = out.reshape(B, S, W)
        return out @ w_out

    def _L0_ffn_ref(x, qkv_w, qkv_b, q_norm_w, q_norm_b, k_norm_w, k_norm_b, wg_w, wg0_w, wg1_w, proj_w, proj_b):
        import jax, jax.numpy as jnp
        import numpy as np
        DIM = 192
        H = 12
        HD = 64
        SHARED = 2
        ROUTED = 2
        E_ROUTED = H - SHARED
        LN_EPS = 1e-05

        def _layernorm(x, w, b):
            m = x.mean(-1, keepdims=True)
            v = ((x - m) ** 2).mean(-1, keepdims=True)
            return (x - m) * jax.lax.rsqrt(v + LN_EPS) * w + b
        B, N, C = x.shape
        scale = HD ** (-0.5)
        gates = jax.nn.softmax(x @ wg_w, axis=-1)
        _, idx = jax.lax.top_k(gates, ROUTED)
        mask = jax.nn.one_hot(idx, E_ROUTED, dtype=gates.dtype).sum(-2)
        rg = gates * mask
        denom = jnp.clip(rg.sum(-1, keepdims=True), jnp.finfo(rg.dtype).eps, None)
        routed_gates = rg / denom * ROUTED
        qkv = (x @ qkv_w + qkv_b).reshape(B, N, 3, H, HD)
        qkv = jnp.transpose(qkv, (2, 0, 3, 1, 4))
        q, k, v = (qkv[0], qkv[1], qkv[2])
        q = _layernorm(q, q_norm_w, q_norm_b)
        k = _layernorm(k, k_norm_w, k_norm_b)
        attn = jax.nn.softmax(jnp.einsum('bhqd,bhkd->bhqk', q * scale, k), axis=-1)
        o = jnp.einsum('bhqk,bhkd->bhqd', attn, v)
        o = jnp.transpose(o, (0, 2, 1, 3))
        shared_gates = jax.nn.softmax(x @ wg1_w, axis=-1) * SHARED
        w0 = jax.nn.softmax(x @ wg0_w, axis=-1) * 2.0
        shared_gates = w0[..., 0:1] * shared_gates
        routed_gates = w0[..., 1:2] * routed_gates
        masked_gates = jnp.concatenate([shared_gates, routed_gates], axis=-1)
        o = (masked_gates[..., None] * o).reshape(B, N, H * HD)
        return o @ proj_w + proj_b

    def _L1_attn_ref(x, w_qkv, b_qkv, w_proj, b_proj):
        import jax, jax.numpy as jnp
        import numpy as np
        B, N, C = (2, 1024, 192)
        H = 12
        HD = C // H
        THETA = 10000.0

        def _rope_tables(n, hd, dtype):
            inv = 1.0 / THETA ** (jnp.arange(0, hd, 2, dtype=jnp.float32) / hd)
            freqs = jnp.arange(n, dtype=jnp.float32)[:, None] * inv[None, :]
            cos = jnp.concatenate([jnp.cos(freqs), jnp.cos(freqs)], axis=-1).astype(dtype)
            sin = jnp.concatenate([jnp.sin(freqs), jnp.sin(freqs)], axis=-1).astype(dtype)
            return (cos, sin)

        def _rotate_half(x):
            x1, x2 = (x[..., :x.shape[-1] // 2], x[..., x.shape[-1] // 2:])
            return jnp.concatenate([-x2, x1], axis=-1)
        b, n, c = x.shape
        scale = HD ** (-0.5)
        qkv = jnp.einsum('bnc,dc->bnd', x, w_qkv) + b_qkv
        qkv = qkv.reshape(b, n, 3, H, HD).transpose(2, 0, 3, 1, 4)
        q, k, v = (qkv[0], qkv[1], qkv[2])
        cos, sin = _rope_tables(n, HD, x.dtype)
        q = q * cos + _rotate_half(q) * sin
        k = k * cos + _rotate_half(k) * sin
        attn = jnp.einsum('bhqd,bhkd->bhqk', q, k) * scale
        attn = jax.nn.softmax(attn, axis=-1)
        out = jnp.einsum('bhqk,bhkd->bhqd', attn, v)
        out = out.transpose(0, 2, 1, 3).reshape(b, n, c)
        return jnp.einsum('bnc,dc->bnd', out, w_proj) + b_proj

    def _L1_ffn_ref(x, w_fc_sh, w_proj_sh, w1, w2, router_w, balance_bias):
        import jax, jax.numpy as jnp
        import numpy as np
        B, T, C = (4, 512, 192)
        E, K = (8, 2)

        def _mlp(x, wfc, wproj):
            h = jnp.square(jax.nn.relu(x @ wfc))
            return h @ wproj
        Bx, Tx, Cx = x.shape
        shared = _mlp(x, w_fc_sh, w_proj_sh)
        xf = x.reshape(-1, Cx)
        logits = xf.astype(jnp.float32) @ router_w.T
        scores = jax.nn.sigmoid(logits)
        _, idx = jax.lax.top_k(scores + balance_bias, K)
        tw = jnp.take_along_axis(scores, idx, axis=-1)
        tw = tw / (tw.sum(-1, keepdims=True) + 1e-20)
        combine = (jax.nn.one_hot(idx, E, dtype=tw.dtype) * tw[..., None]).sum(1)
        h = jnp.square(jax.nn.relu(jnp.einsum('nc,ech->neh', xf, w1)))
        y = jnp.einsum('neh,ehc->nec', h, w2)
        routed = jnp.einsum('nec,ne->nc', y, combine)
        return shared + routed.reshape(Bx, Tx, Cx)
    h = _L0_tok_ref(x, L0_tok_W, L0_tok_b)
    h = h + _L0_attn_ref(_layernorm(h, axis=-1), L0_attn_w_qkv, L0_attn_w_out)
    h = h + _L0_ffn_ref(_layernorm(h, axis=-1), L0_ffn_qkv_w, L0_ffn_qkv_b, L0_ffn_q_norm_w, L0_ffn_q_norm_b, L0_ffn_k_norm_w, L0_ffn_k_norm_b, L0_ffn_wg_w, L0_ffn_wg0_w, L0_ffn_wg1_w, L0_ffn_proj_w, L0_ffn_proj_b)
    h = h + _L1_attn_ref(_layernorm(h, axis=-1), L1_attn_w_qkv, L1_attn_b_qkv, L1_attn_w_proj, L1_attn_b_proj)
    h = h + _L1_ffn_ref(_layernorm(h, axis=-1), L1_ffn_w_fc_sh, L1_ffn_w_proj_sh, L1_ffn_w1, L1_ffn_w2, L1_ffn_router_w, L1_ffn_balance_bias)
    return h

_drawn_inputs = setup_inputs


def setup_inputs(seed=0):
    import zlib

    import numpy as np

    out = dict(_drawn_inputs(seed))
    spreads = {'L0_tok_b': (0.0, 0.1),
     'L0_ffn_qkv_b': (0.0, 0.1),
     'L0_ffn_q_norm_w': (1.0, 0.6),
     'L0_ffn_q_norm_b': (0.0, 0.8),
     'L0_ffn_k_norm_w': (1.0, 0.6),
     'L0_ffn_k_norm_b': (0.0, 0.8),
     'L0_ffn_proj_b': (0.0, 0.1),
     'L1_attn_b_qkv': (0.0, 0.1),
     'L1_attn_b_proj': (0.0, 0.1),
     'L1_ffn_balance_bias': (0.0, 0.537)}
    factors = {'L0_ffn_qkv_w': 3.606,
     'L0_ffn_wg_w': 3.008,
     'L0_ffn_wg0_w': 8.0,
     'L0_ffn_wg1_w': 8.0,
     'L1_ffn_w_fc_sh': 2.974,
     'L1_ffn_w_proj_sh': 2.776,
     'L1_ffn_w1': 4.167,
     'L1_ffn_w2': 3.842,
     'L1_ffn_router_w': 6.079}
    for name, (base, spread) in spreads.items():
        noise = np.random.default_rng([zlib.crc32(name.encode()), seed]).standard_normal(out[name].shape)
        drawn = base * np.exp(spread * noise) if base else spread * noise
        out[name] = jnp.asarray(drawn.astype(out[name].dtype))
    for name, factor in factors.items():
        out[name] = (out[name] * factor).astype(out[name].dtype)
    return out
```

```python
from contextlib import ExitStack

import concourse.bass as bass
from concourse import mybir

F32 = mybir.dt.float32
F32R = mybir.dt.float32r
U32 = mybir.dt.uint32
ALU = mybir.AluOpType
ACT = mybir.ActivationFunctionType
AX = mybir.AxisListType

IMAGES = 64
STEPS = 32
D = 192
TOK = 196
HALF = 98
IMS = 2
TT = IMS * TOK
NT = TT // HALF
NH = 12
EPS = 1e-5
GRID = 14
KC = 6

CLASSES = [("mid", "mid"), ("first", "mid"), ("last", "mid"), ("mid", "first"), ("mid", "last"),
           ("first", "first"), ("first", "last"), ("last", "first"), ("last", "last")]
MID_TILES = 72

C_A0QK, C_A1QK, C_A1V, C_F0QK = 0, 384, 768, 960
C_F0V = C_F0QK + 2 * NH * 64
NV0, NV1 = 384, 398
C_RT = C_F0V + NV0 + NV1
C_W1 = C_RT + 8
MOE_M = 14
NCOL = C_W1 + MOE_M * 128
K_W2, K_PJ, K_O0, K_O1 = 0, 14, 20, 23
NK = 26
SELROWS = 92


def token_classes():
    span = {"first": [0], "mid": list(range(1, GRID - 1)), "last": [GRID - 1]}
    cls = [[(i, j) for i in span[r] for j in span[c]] for r, c in CLASSES]
    return cls, sum(cls, [])


def edge_tiles():
    return [c for c in (1, 2, 3, 4) for k in range(6)] + [5, 6, 7, 8]


def crop_rows(c, k):
    r, q = CLASSES[c]
    quadrants = [[(0, 128, 0, 1), (0, 64, 1, 2)], [(64, 128, 1, 2), (0, 128, 2, 3)],
                 [(0, 128, 3, 4), (0, 64, 4, 5)], [(64, 128, 4, 5), (0, 128, 5, 6)]]
    kept = []
    for n, parts in enumerate(quadrants):
        low, right = n // 2, n % 2
        rows = not (low and r == "last") if k in (1, 3) else not (not low and r == "first")
        cols = not (right and q == "last") if k in (1, 2) else not (not right and q == "first")
        if rows and cols:
            kept += parts
    return [(0, 128, 0, KC)] if len(kept) == 8 else kept


def w32(ap):
    return ap.bitcast(F32)


class Signal:

    def __init__(self, sem, per):
        self.sem, self.per = sem, per

    def wait(self, e, it, k=None):
        e.wait_ge(self.sem, it * self.per + (self.per if k is None else k))


class Banks:

    def __init__(self, banks, filled, stages):
        self.banks, self.filled = banks, filled
        self.first, self.readers = {}, []
        for name, n, signal, count in stages:
            self.first[name] = len(self.readers)
            self.readers += [(signal, count(k)) for k in range(n)]
        self.total = len(self.readers)

    def claim(self, pe, it, stage, k):
        n = self.first[stage] + k
        if n >= len(self.banks):
            signal, count = self.readers[n - len(self.banks)]
            signal.wait(pe, it, count)
        return self.banks[n % len(self.banks)]

    def fill(self, ins):
        ins.then_inc(self.filled, 1)

    def wait(self, e, it, stage, k):
        e.wait_ge(self.filled, it * self.total + self.first[stage] + k + 1)
        return self.banks[(self.first[stage] + k) % len(self.banks)]


def setup_and_patches(nc, a, w, h0):
    with ExitStack() as ctx:
        def sb(name, shape, dt=F32):
            return ctx.enter_context(nc.sbuf_tensor(name, shape, dt))

        def sem(name):
            return ctx.enter_context(nc.semaphore(name))

        cuts = [0, 480, C_F0QK, C_F0QK + 768, C_F0V, C_RT, C_RT + 776, C_RT + 1544, NCOL]
        blocks = [("cols", c0, c1) for c0, c1 in zip(cuts, cuts[1:])]
        blocks += [("groups", g, min(g + 4, NK)) for g in range(0, NK, 4)]
        is_qk = [k == "cols" and C_F0QK <= c0 < C_F0V for k, c0, c1 in blocks]

        stage = sb("stage", [128, 2, 2, 784])
        headsum = sb("headsum", [128, 2, 12])
        wtok = sb("wtok", [128, 5, KC, D])
        weff = sb("weff", [128, KC, D])
        weffH = sb("weffH", [128, 2, KC, D], F32R)
        weffL = sb("weffL", [128, 2, KC, D], F32R)
        tokb = sb("tokb", [128, D])
        blockmean = sb("blockmean", [128, 128])
        qkb_in = sb("qkb_in", [128, 12])
        sel_in = sb("sel_in", [SELROWS, MOE_M * 128])
        px = sb("px", [128, 4, KC * 128])
        pxH = sb("pxH", [128, 2, KC * 128], F32R)
        pxL = sb("pxL", [128, 2, KC * 128], F32R)
        tok = sb("tok", [128, 2, D])
        ps = [ctx.enter_context(nc.psum_tensor(f"ps_tok{i}", [128, 512], F32)) for i in range(2)]
        ps_mean = ctx.enter_context(nc.psum_tensor("ps_mean", [128, 512], F32))

        wtok_in = sem("wtok_in")
        const_in = sem("const_in")
        stage_in = [sem("stage_in0"), sem("stage_in1")]
        centred = sem("centred")
        split_h = sem("split_h")
        split_l = sem("split_l")
        meaned = sem("meaned")
        small = sem("small")
        summed = sem("summed")
        weff_h = sem("weff_h")
        weff_l = sem("weff_l")
        px_in = [sem(f"px_in{i}") for i in range(4)]
        px_h = sem("px_h")
        px_l = sem("px_l")
        tok_ps = sem("tok_ps")
        tok_sb = sem("tok_sb")
        tok_out = [sem("tok_out0"), sem("tok_out1")]

        edges = edge_tiles()
        total = MID_TILES + len(edges)
        WHOLE = total - 4
        first_of = {c: MID_TILES + edges.index(c) for c in range(1, 9)}
        first_of[0] = 0
        ends, s = [], 0
        for c in range(len(CLASSES)):
            s += 1 + sum(len(crop_rows(c, k)) for k in range(1, 5))
            ends.append(s)

        block = ctx.enter_context(nc.Block())

        def since(e, sem_, v):
            if not isinstance(v, int) or v > 0:
                e.wait_ge(sem_, v)

        def all_tiles(e, body):
            for u in range(4):
                body(u, u)
            with e.Fori(1, MID_TILES // 4) as r:
                for u in range(4):
                    body(4 * r + u, u)
            for t in range(MID_TILES, total):
                body(t, t % 4)

        def rounds(t, u):
            return 4 * (t - u) + 16 if not isinstance(t, int) else 16 * (t // 4 + 1)

        @block.sync
        def _(sp):
            sp.dma_start(wtok[:, :, :, :], a["tokW"]).then_inc(wtok_in, 16)
            sp.dma_start(tokb[:, :], a["tokb"]).then_inc(wtok_in, 16)
            for t in range(4):
                sp.dma_start(px[:, t, :], a["px"][t]).then_inc(px_in[t], 16)
            for dst, name in ((blockmean, "blockmean"), (qkb_in, "qkb"), (sel_in, "sel"), (w["ident"], "ident"),
                              (w["sumcol"], "sumcol"), (w["cos"], "cos"), (w["sin"], "sin"),
                              (w["a1qkb"], "a1qkb"), (w["f0n"], "f0n"), (w["f0vb"], "f0vb"),
                              (w["a1vb"], "a1vb"), (w["f0pb"], "f0pb"), (w["bal"], "bal"), (w["iota"], "iota")):
                sp.dma_start(dst[:, :], a[name]).then_inc(const_in, 16)

            def load(t, u):
                sp.wait_ge(px_l, t - 3)
                sp.dma_start(px[:, u, :], a["px"][bass.ds(t, 1), :, :].rearrange("o p n -> (o p) n")
                             ).then_inc(px_in[u], 16)

            def store(t, u, rows):
                sp.wait_ge(tok_sb, t + 1)
                sp.dma_start(h0[bass.ds(128 * t if rows == 128 else 128 * WHOLE + 64 * (t - WHOLE), rows), :],
                             tok[0:rows, u % 2, :]).then_inc(tok_out[u % 2], 16)

            with sp.Fori(1, MID_TILES // 4) as r:
                for u in range(4):
                    load(4 * r + u, u)
                    store(4 * r + (u - 4), u, 128)
            for t in range(MID_TILES, total + 4):
                if t < total:
                    load(t, t % 4)
                store(t - 4, t % 4, 128 if t - 4 < WHOLE else 64)
            for u in range(2):
                sp.wait_ge(tok_out[u], 16 * (total // 2))
            sp.wait_ge(const_in, 16 * 14)

        @block.gpsimd
        def _(pool):
            def stage_block(i):
                if i < len(blocks):
                    kind, c0, c1 = blocks[i]
                    if kind == "cols":
                        for part, name in enumerate(("WA", "WB")):
                            pool.dma_start(stage[:, i % 2, part, 0:c1 - c0], a[name][:, c0:c1]
                                           ).then_inc(stage_in[i % 2], 16)
                    else:
                        pool.dma_start(stage[:, i % 2, 0, 0:(c1 - c0) * D], a["WK"][:, c0 * D:c1 * D]
                                       ).then_inc(stage_in[i % 2], 16)

            def class_weights(c):
                n = ends[c - 1] if c else 0
                if c:
                    pool.wait_ge(weff_h, c)
                    pool.wait_ge(weff_l, c)
                nc.gpsimd.tensor_copy(weff[:, :, :], wtok[:, 0, :, :]).then_inc(summed, 1)
                n += 1
                for k in range(1, 5):
                    for p0, p1, k0, k1 in crop_rows(c, k):
                        pool.wait_ge(summed, n)
                        nc.gpsimd.tensor_tensor(weff[p0:p1, k0:k1, :], weff[p0:p1, k0:k1, :],
                                                wtok[p0:p1, k, k0:k1, :], ALU.add).then_inc(summed, 1)
                        n += 1
                pool.wait_ge(weff_h, c + 1)
                nc.gpsimd.tensor_tensor(weffL[:, c % 2, :, :], weff[:, :, :],
                                        w32(weffH[:, c % 2, :, :]), ALU.subtract).then_inc(weff_l, 1)

            stage_block(0)
            stage_block(1)
            pool.wait_ge(wtok_in, 32)
            class_weights(0)
            for i, (kind, c0, c1) in enumerate(blocks):
                pool.wait_ge(split_h, i + 1)
                if kind == "cols":
                    n = c1 - c0
                    nc.gpsimd.tensor_tensor(w["Al"][:, c0:c1], stage[:, i % 2, 0, 0:n],
                                            w32(w["A"][:, c0:c1]), ALU.subtract).then_inc(split_l, 1)
                    pool.wait_ge(split_l, 2 * i + 1)
                    nc.gpsimd.tensor_tensor(w["B"][64:128, c0:c1], stage[64:128, i % 2, 1, 0:n],
                                            w32(w["B"][64:128, c0:c1]), ALU.subtract).then_inc(split_l, 1)
                else:
                    n = (c1 - c0) * D
                    nc.gpsimd.tensor_tensor(w["Kl"][:, c0 * D:c1 * D], stage[:, i % 2, 0, 0:n],
                                            w32(w["Kh"][:, c0 * D:c1 * D]), ALU.subtract).then_inc(split_l, 2)
                pool.wait_ge(split_l, 2 * i + 2)
                stage_block(i + 2)
            for c in range(1, len(CLASSES)):
                class_weights(c)

        @block.scalar
        def _(act):
            def weights_h(c):
                act.wait_ge(summed, ends[c])
                if c >= 2:
                    act.wait_ge(tok_ps, first_of[c - 1])
                nc.scalar.copy(weffH[:, c % 2, :, :], weff[:, :, :]).then_inc(weff_h, 1)

            def pixels_h(t, u):
                if isinstance(t, int) and t >= MID_TILES and t - 1 in [first_of[c] for c in range(1, 8)]:
                    weights_h(1 + [first_of[c] for c in range(1, 9)].index(t - 1) + 1)
                act.wait_ge(px_in[u], rounds(t, u))
                since(act, tok_ps, t - 1)
                nc.scalar.copy(pxH[:, u % 2, :], px[:, u, :]).then_inc(px_h, 1)

            weights_h(0)
            for i, (kind, c0, c1) in enumerate(blocks):
                if kind == "cols":
                    act.wait_ge(stage_in[i % 2], 32 * (i // 2 + 1))
                else:
                    n_cols = [len([b for b in blocks if b[0] == "cols"][p::2]) for p in range(2)][i % 2]
                    act.wait_ge(stage_in[i % 2], 32 * n_cols + 16 * (i // 2 + 1 - n_cols))
                if is_qk[i]:
                    act.wait_ge(centred, 3 * sum(is_qk[:i + 1]))
                n = c1 - c0
                if kind == "cols":
                    nc.scalar.copy(w["A"][:, c0:c1], stage[:, i % 2, 0, 0:n])
                    nc.scalar.copy(w["B"][:, c0:c1], stage[:, i % 2, 1, 0:n]).then_inc(split_h, 1)
                else:
                    nc.scalar.copy(w["Kh"][:, c0 * D:c1 * D], stage[:, i % 2, 0, 0:n * D]).then_inc(split_h, 1)
            weights_h(1)
            all_tiles(act, pixels_h)

        @block.vector
        def _(dve):
            n = 0
            for i in range(len(blocks)):
                if is_qk[i]:
                    part = stage[:, i % 2, :, 0:768].rearrange("p x (h d) -> p x h d", d=64)
                    dve.wait_ge(stage_in[i % 2], 32 * (i // 2 + 1))
                    since(dve, centred, n)
                    nc.vector.tensor_reduce(headsum[:, :, :], part, AX.X, ALU.add).then_inc(centred, 1)
                    dve.wait_ge(centred, n + 1)
                    nc.vector.tensor_scalar(headsum[:, :, :], headsum[:, :, :], 1.0 / 64, None,
                                            ALU.mult).then_inc(centred, 1)
                    dve.wait_ge(centred, n + 2)
                    nc.vector.tensor_tensor(part, part, headsum[:, :, :].unsqueeze(3).to_broadcast([128, 2, 12, 64]),
                                            ALU.subtract).then_inc(centred, 1)
                    n += 3
            dve.wait_ge(const_in, 16 * 14)
            nc.vector.tensor_copy(w["sel"][:, :, :].rearrange("p m n -> p (m n)"), sel_in[:, :]).then_inc(small, 1)
            dve.wait_ge(meaned, 1)
            nc.vector.tensor_tensor(w["f0qkb"][:, :], qkb_in[:, :], ps_mean[:, 0:12], ALU.subtract).then_inc(small, 1)

            def tile(t, u):
                dve.wait_ge(px_h, t + 1)
                nc.vector.tensor_tensor(pxL[:, u % 2, :], px[:, u, :], w32(pxH[:, u % 2, :]),
                                        ALU.subtract).then_inc(px_l, 1)
                dve.wait_ge(tok_ps, t + 1)
                since(dve, tok_out[u % 2], 8 * t - 8 * (u % 2))
                nc.vector.tensor_tensor(tok[:, u % 2, :], ps[u % 2][:, 0:D], tokb[:, :], ALU.add).then_inc(tok_sb, 1)

            all_tiles(dve, tile)

        @block.tensor
        def _(pe):
            pe.wait_ge(const_in, 16 * 14)
            nc.tensor.matmul(ps_mean[:, 0:12], blockmean[:, :], qkb_in[:, :], start=True, stop=True).then_inc(meaned, 1)

            def tile(t, u):
                c = 0 if not isinstance(t, int) or t < MID_TILES else edges[t - MID_TILES]
                if isinstance(t, int) and t == first_of[c]:
                    pe.wait_ge(weff_l, c + 1)
                pe.wait_ge(px_h, t + 1)
                since(pe, tok_sb, t - 1)
                out = ps[u % 2][:, 0:D]
                for k in range(KC):
                    x = pxH[:, u % 2, 128 * k:128 * k + 128]
                    nc.tensor.matmul(out, x, weffH[:, c % 2, k, :], start=(k == 0), stop=False)
                    nc.tensor.matmul(out, x, weffL[:, c % 2, k, :], start=False, stop=False)
                pe.wait_ge(px_l, t + 1)
                for k in range(KC):
                    last = nc.tensor.matmul(out, pxL[:, u % 2, 128 * k:128 * k + 128], weffH[:, c % 2, k, :],
                                            start=False, stop=(k == KC - 1))
                last.then_inc(tok_ps, 1)

            all_tiles(pe, tile)


def layers(nc, a, w, h0, out):
    with ExitStack() as ctx:
        def sb(name, shape, dt=F32):
            return ctx.enter_context(nc.sbuf_tensor(name, shape, dt))

        def sem(name):
            return ctx.enter_context(nc.semaphore(name))

        def signal(name, per):
            return Signal(sem(name), per)

        hin = sb("hin", [HALF, NT, D])
        h = sb("h", [HALF, NT, D])
        bnst = sb("bnst", [HALF, NT, 6])
        bnmv = sb("bnmv", [HALF, NT, 2])
        vareps = sb("vareps", [HALF, NT])
        rstd = sb("rstd", [HALF, NT])
        mhalf = sb("mhalf", [HALF, 1])
        eps = sb("eps", [HALF, 1])
        xA = sb("xA", [128, 2, TT], F32R)
        xB = sb("xB", [128, 2, TT], F32R)
        qs = sb("qs", [66, NH, TT], F32R)
        ks = sb("ks", [66, NH, TT], F32R)
        vf = sb("vf", [HALF, NT, 6, 3, 64])
        va = vf[:, :, :, 0:3:2, 0:32]
        P = 6
        work = sb("work", [128, P, TT])
        probs = work[0:HALF, :, :]
        qc = work
        mx = sb("mx", [HALF, NT, NH])
        rh = sb("rh", [128, 3, TT], F32R)
        rl = sb("rl", [128, 3, TT], F32R)
        sa = sb("sa", [128, 3, TT])
        sc = sb("sc", [128, 3, TT])
        qvar = sc[0:12, 0, :]
        xn = sa[0:HALF, :, :].rearrange("p a n -> p (a n)")[:, 0:NT * 256].rearrange("p (t c) -> p t c", c=256)
        rowH = sb("rowH", [SELROWS, TT], F32R)
        lg = sb("lg", [HALF, NT, 14])
        gmax = sb("gmax", [HALF, NT, 3])
        gsum = sb("gsum", [HALF, NT, 3])
        top8 = sb("top8", [HALF, NT, 8])
        idx8 = sb("idx8", [HALF, NT, 8], U32)
        idxf = sb("idxf", [HALF, NT, 8])
        hot = sb("hot", [HALF, NT, 10])
        hot2 = sb("hot2", [HALF, NT, 10])
        gm = sb("gm", [HALF, NT, NH])
        cm = sb("cm", [HALF, NT, 28])

        banks = [ctx.enter_context(nc.psum_tensor(f"ps{i}", [128, 512], F32)) for i in range(8)]
        ready = sem("ready")
        held = sem("held")
        h_in = sem("h_in")
        h_out = sem("h_out")
        subs = ("a0", "f0", "a1", "f1")
        stats = {s: signal(s + "_stats", 8) for s in subs}
        vare = {s: signal(s + "_vare", 1) for s in subs}
        rstds = {s: signal(s + "_rstd", 1) for s in subs}
        normed = {s: signal(s + "_normed", 8) for s in subs}
        xh = {s: signal(s + "_xh", 2) for s in subs}
        xl = {s: signal(s + "_xl", 2) for s in subs}
        resid = {"a0": signal("a0_resid", 4), "f0": signal("f0_resid", 8), "a1": signal("a1_resid", 4),
                 "f1": signal("f1_resid", 4)}
        at = ("a0", "a1")
        st_h = {s: signal(s + "_st_h", 3) for s in at}
        st_l = {s: signal(s + "_st_l", 3) for s in at}
        stack = {s: signal(s + "_stack", 96 * 16) for s in at}
        ones = {s: signal(s + "_ones", 1) for s in at}
        va_in = {s: signal(s + "_va", 2) for s in at}
        maxes = {s: signal(s + "_maxes", 24) for s in at}
        nm = {s: signal(s + "_nm", 1) for s in at}
        nmrow = {s: signal(s + "_nmrow", NH * 16) for s in at}
        exps = {s: signal(s + "_exps", 24) for s in at}
        pvs = {s: signal(s + "_pvs", 3) for s in at}
        dens = {s: signal(s + "_dens", 6) for s in at}
        quot = {s: signal(s + "_quot", 3) for s in at}
        on_h = {s: signal(s + "_on_h", 3) for s in at}
        on_l = {s: signal(s + "_on_l", 3) for s in at}
        rope_b = signal("rope_b", 3)
        rope_s = signal("rope_s", 3)
        rope_p = signal("rope_p", 3)
        rope_c = signal("rope_c", 3)
        rope_u = signal("rope_u", 3)
        a1_bias = signal("a1_bias", 3)
        h_bias = signal("h_bias", 4)
        f_v = signal("f_v", 12)
        f_gate = signal("f_gate", 28)
        f_gexp = signal("f_gexp", 1)
        f_row = signal("f_row", 4)
        f_qc = signal("f_qc", 12)
        f_sq = signal("f_sq", 12)
        f_squ = signal("f_squ", 10)
        f_var = signal("f_var", 2)
        f_rs = signal("f_rs", 2)
        f_rsr = signal("f_rsr", 4)
        f_t = signal("f_t", 12)
        f_u = signal("f_u", 12)
        f_h = signal("f_h", 36)
        f_l = signal("f_l", 24)
        f_max = signal("f_max", 24)
        f_nm = signal("f_nm", 2)
        f_nmrow = signal("f_nmrow", NH * 16)
        f_exp = signal("f_exp", 24)
        f_den = signal("f_den", 12)
        f_quot = signal("f_quot", 12)
        f_on = signal("f_on", 6)
        f_onh = signal("f_onh", 6)
        f_onl = signal("f_onl", 6)
        m_exp = signal("m_exp", 1)
        m_gate = signal("m_gate", 21)
        m_row = signal("m_row", 2)
        m_relu = signal("m_relu", MOE_M)
        m_c = signal("m_c", MOE_M)
        m_hid = signal("m_hid", MOE_M)
        m_h = signal("m_h", MOE_M)
        m_l = signal("m_l", MOE_M)
        m_used = signal("m_used", MOE_M - 1)

        ident, sel, sumcol = w["ident"], w["sel"], w["sumcol"]
        NREADY = 8

        def attention_fills(s):
            qk = st_l["a0"] if s == "a0" else rope_b
            return [(s + "_x", 2, xl[s], lambda k: k + 1), (s + "_qk", 3, qk, lambda k: k + 1),
                    (s + "_v", 2, va_in[s], lambda k: k + 1), (s + "_S1", 24, maxes[s], lambda k: k + 1),
                    (s + "_mx", 1, nm[s], lambda k: 1), (s + "_S2", 24, exps[s], lambda k: k + 1)]

        def after(n):
            return lambda k: n + k + 1

        s_fills = attention_fills("a0")
        s_fills += [("f0_x", 2, xl["f0"], after(0)), ("f0_v", 8, f_v, lambda k: 3 * (k // 2) + 1 + 2 * (k % 2))]
        for s in range(2):
            s_fills += [(f"f0_qk{s}", 6, f_qc, after(6 * s)), (f"f0_var{s}", 1, f_var, after(s)),
                        (f"f0_rs{s}", 6, f_t, after(6 * s)), (f"f0_S1{s}", 12, f_max, after(12 * s)),
                        (f"f0_mx{s}", 1, f_nm, after(s)), (f"f0_S2{s}", 12, f_exp, after(12 * s)),
                        (f"f0_g{s}", 1, f_row, after(2 * s + 1)), (f"f0_gb{s}", 3, f_on, after(3 * s))]
        s_fills += attention_fills("a1")
        s_fills += [("f1_x", 2, xl["f1"], after(0)), ("f1_r", 1, m_exp, after(0)), ("f1_c", 1, m_row, after(1))]
        for m in range(MOE_M):
            s_fills += [(f"f1_h{m}", 1, m_relu, after(m)), (f"f1_cb{m}", 1, m_c, after(m))]
        c_fills = [("a0_pv", 3, quot["a0"], after(0)), ("a0_out", 4, resid["a0"], after(0))]
        for s in range(2):
            c_fills += [(f"f0_pv{s}", 6, f_quot, after(6 * s)), (f"f0_out{s}", 4, resid["f0"], after(4 * s))]
        c_fills += [("a1_pv", 3, quot["a1"], after(0)), ("a1_out", 4, resid["a1"], after(0)),
                    ("f1_y", 4, resid["f1"], after(0))]
        S = Banks(banks[:4], sem("s_filled"), s_fills)
        C = Banks(banks[4:], sem("c_filled"), c_fills)

        def tok(t):
            return slice(HALF * t, HALF * t + HALF)

        def img(im):
            return slice(TOK * im, TOK * im + TOK)

        block = ctx.enter_context(nc.Block())

        @block.sync
        def _(sp):
            def load(it):
                for half in range(2):
                    sp.dma_start(hin[:, half:NT:2, :],
                                 h0v[half][:, bass.ds(IMS * it, IMS), :]).then_inc(h_in, 16)

            h0v = [h0[IMAGES * HALF * half:IMAGES * HALF * (half + 1), :].rearrange("(p b) d -> p b d", b=IMAGES)
                   for half in range(2)]

            def attention(it, s):
                for m in range(3):
                    st_h[s].wait(sp, it, m + 1)
                    st_l[s].wait(sp, it, m + 1)
                    for n in range(8):
                        dst, head = (qs, 8 * m + n) if 8 * m + n < NH else (ks, 8 * m + n - NH)
                        rows = (0, 16, 32, 48) if dst is qs else (0, 32, 16, 48)
                        for part, at_row in zip((rh, rh, rl, rl), rows):
                            sp.dma_start(w32(dst[at_row:at_row + 16, head, :]),
                                         w32(part[16 * n:16 * n + 16, m, :])).then_inc(stack[s].sem, 16)
                nm[s].wait(sp, it)
                for n in range(NH):
                    sp.dma_start(w32(qs[65:66, n, :]), w32(rowH[n:n + 1, :])).then_inc(nmrow[s].sem, 16)

            def body(it, more):
                attention(it, "a0")
                for s in range(2):
                    f_nm.wait(sp, it, s + 1)
                    for n in range(6):
                        sp.dma_start(w32(qs[65:66, 6 + n, :]), w32(rowH[n:n + 1, :])).then_inc(f_nmrow.sem, 16)
                attention(it, "a1")
                if more:
                    resid["a0"].wait(sp, it)
                    load(it + 1)
                resid["f1"].wait(sp, it)
                sp.dma_start(out[bass.ds(it, 1)].rearrange("o p t d -> (o p) t d"), h[:, :, :]).then_inc(h_out, 16)

            load(0)
            if STEPS > 1:
                with sp.Fori(0, STEPS - 1) as it:
                    body(it, True)
            body(STEPS - 1, False)
            sp.wait_ge(h_out, 16 * STEPS)

        @block.gpsimd
        def _(pool):
            constant = [(mhalf[:, :], -0.5), (eps[:, :], EPS), (w32(qs[64:66, :, :]), 0.0), (w32(ks[64:66, :, :]), 1.0),
                        (vf[:, :, :, 1, :], 1.0), (w32(rowH[:, :]), 0.0), (cm[:, :, 24:27], 1.0),
                        (cm[:, :, 27:28], 0.0)]
            for n, (to, value) in enumerate(constant):
                nc.gpsimd.memset(to, value).then_inc(ready, 1)
                pool.wait_ge(ready, n + 1)

            def rstd_of_tokens(it, s):
                stats[s].wait(pool, it)
                nc.gpsimd.tensor_tensor(vareps[:, :], bnmv[:, :, 1], eps[:, :].to_broadcast([HALF, NT]), ALU.add).then_inc(vare[s].sem, 1)
                vare[s].wait(pool, it)
                nc.gpsimd.tensor_tensor(rstd[:, :], vareps[:, :], mhalf[:, :].to_broadcast([HALF, NT]), ALU.pow).then_inc(rstds[s].sem, 1)

            def low(out_, full, high):
                return nc.gpsimd.tensor_tensor(out_, full, w32(high), ALU.subtract)

            def ones_beside_values(it, s):
                for t in range(NT):
                    ins = nc.gpsimd.memset(va[:, t, :, :, 16:32], 1.0)
                ins.then_inc(ones[s].sem, 1)

            def outputs(it, s):
                for g in range(3):
                    quot[s].wait(pool, it, g + 1)
                    if s == "a1":
                        nc.gpsimd.tensor_tensor(sc[:, g, :], sc[:, g, :], w["a1vb"][:, g:g + 1]
                                                .to_broadcast([128, TT]), ALU.add).then_inc(a1_bias.sem, 1)
                    on_h[s].wait(pool, it, g + 1)
                    low(rl[:, g, :], sc[:, g, :], rh[:, g, :]).then_inc(on_l[s].sem, 1)

            def body(it):
                rstd_of_tokens(it, "a0")
                ones_beside_values(it, "a0")
                outputs(it, "a0")

                rstd_of_tokens(it, "f0")
                normed["f0"].wait(pool, it)
                for t in range(NT):
                    nc.gpsimd.tensor_tensor(h[:, t, :], h[:, t, :], w["f0pb"][:, :], ALU.add).then_inc(h_bias.sem, 1)
                for s in range(2):
                    for i in range(6):
                        f_qc.wait(pool, it, 6 * s + i + 1)
                        if i >= 3:
                            f_squ.wait(pool, it, 6 * s + i - 2)
                        nc.gpsimd.tensor_tensor(sa[:, i % 3, :], qc[:, i, :], qc[:, i, :],
                                                ALU.mult).then_inc(f_sq.sem, 1)
                    f_var.wait(pool, it, s + 1)
                    nc.gpsimd.tensor_tensor(qvar, qvar, mhalf[0:12, :].to_broadcast([12, TT]), ALU.pow).then_inc(f_rs.sem, 1)
                    f_rsr.wait(pool, it, 2 * s + 1)
                    low(rowH[64:76, :], qvar, rowH[0:12, :]).then_inc(f_rsr.sem, 1)
                    for i in range(6):
                        dst = qs if i < 3 else ks
                        for x in range(2):
                            hd = 2 * (i % 3) + x
                            f_h.wait(pool, it, 18 * s + 3 * i + 1 + 2 * x)
                            high = dst[0:64, hd, :] if x == 0 else rh[64:128, i % 3, :]
                            low(dst[0:64, 6 + hd, :], qc[64 * x:64 * x + 64, i, :], high).then_inc(f_l.sem, 1)
                    for i in range(3):
                        f_onh.wait(pool, it, 3 * s + i + 1)
                        low(rl[:, i, :], sc[:, i, :], rh[:, i, :]).then_inc(f_onl.sem, 1)

                rstd_of_tokens(it, "a1")
                ones_beside_values(it, "a1")
                for m in range(3):
                    rope_s.wait(pool, it, m + 1)
                    for im in range(IMS):
                        ins = nc.gpsimd.tensor_tensor(sa[:, m, img(im)], sa[:, m, img(im)], w["cos"][:, :], ALU.mult)
                    ins.then_inc(rope_c.sem, 1)
                    rope_c.wait(pool, it, m + 1)
                    rope_p.wait(pool, it, m + 1)
                    nc.gpsimd.tensor_tensor(sc[:, m, :], sa[:, m, :], sc[:, m, :], ALU.add).then_inc(rope_u.sem, 1)
                    st_h["a1"].wait(pool, it, m + 1)
                    low(rl[:, m, :], sc[:, m, :], rh[:, m, :]).then_inc(st_l["a1"].sem, 1)
                outputs(it, "a1")

                rstd_of_tokens(it, "f1")
                for m in range(MOE_M):
                    m_c.wait(pool, it, m + 1)
                    nc.gpsimd.tensor_tensor(sc[:, m % 3, :], sc[:, m % 3, :], sa[:, m % 3, :], ALU.mult
                                            ).then_inc(m_hid.sem, 1)
                    m_h.wait(pool, it, m + 1)
                    low(rl[:, m % 3, :], sc[:, m % 3, :], rh[:, m % 3, :]).then_inc(m_l.sem, 1)

            with pool.Fori(0, STEPS) as it:
                body(it)

        @block.scalar
        def _(act):
            def copy(out_, in_, scale=1.0):
                return nc.scalar.activation(out_, in_, ACT.Copy, scale=scale)

            def turned(it, s):
                for k, x in enumerate((xA, xB)):
                    bank = S.wait(act, it, s + "_x", k)
                    copy(x[:, 0, :], bank[:, 0:TT]).then_inc(xh[s].sem, 1)

            def attention(it, s, scale):
                for m in range(3):
                    bank = S.wait(act, it, s + "_qk", m)
                    if s == "a0":
                        copy(rh[:, m, :], bank[:, 0:TT]).then_inc(st_h[s].sem, 1)
                    else:
                        ins = nc.scalar.activation(sa[:, m, :], bank[:, 0:TT], ACT.Identity,
                                                   bias=w["a1qkb"][:, m:m + 1])
                        ins.then_inc(rope_b.sem, 1)
                if s == "a1":
                    for m in range(3):
                        rope_u.wait(act, it, m + 1)
                        copy(rh[:, m, :], sc[:, m, :]).then_inc(st_h[s].sem, 1)
                for k in range(2):
                    bank = S.wait(act, it, s + "_v", k)
                    for x in range(2):
                        ins = copy(va[:, 2 * k + x, :, :, 0:16],
                                   bank[0:HALF, D * x:D * x + D].rearrange("p (a b d) -> p a b d", a=6, d=16))
                    ins.then_inc(va_in[s].sem, 1)
                bank = S.wait(act, it, s + "_mx", 0)
                ins = copy(rowH[0:NH, :], bank[0:NH, 0:TT], scale=-1.0)
                ins.then_inc(nm[s].sem, 1)

                def outputs_h(g):
                    if s == "a1":
                        a1_bias.wait(act, it, g + 1)
                    else:
                        quot[s].wait(act, it, g + 1)
                    copy(rh[:, g, :], sc[:, g, :]).then_inc(on_h[s].sem, 1)

                for n in range(24):
                    bank = S.wait(act, it, s + "_S2", n)
                    if n >= P:
                        b = (n - P) // 4
                        if b % 2:
                            C.wait(act, it, s + "_pv", b // 2)
                        else:
                            pvs[s].wait(act, it, b // 2 + 1)
                    ins = nc.scalar.activation(probs[:, n % P, :], bank[0:HALF, 0:TT], ACT.Exp, scale=scale)
                    ins.then_inc(exps[s].sem, 1)
                    if n in (15, 23):
                        outputs_h(n // 8 - 1)
                outputs_h(2)

            def body(it):
                turned(it, "a0")
                attention(it, "a0", float(D) ** -0.5)

                turned(it, "f0")
                for t in range(NT):
                    for k in range(2):
                        bank = S.wait(act, it, "f0_v", 2 * t + k)
                        copy(vf[:, t, 3 * k:3 * k + 3, 0:3:2, :],
                             bank[0:HALF, 0:384].rearrange("p (a x d) -> p a x d", a=3, d=64)).then_inc(f_v.sem, 1)
                        if k == 1:
                            copy(lg[:, t, :], bank[0:HALF, 384:398]).then_inc(f_v.sem, 1)
                f_gate.wait(act, it, 4)
                nc.scalar.activation(lg[:, :, :], lg[:, :, :], ACT.Exp).then_inc(f_gexp.sem, 1)
                for s in range(2):
                    for i in range(6):
                        bank = S.wait(act, it, f"f0_qk{s}", i)
                        tile = 3 * s + i % 3 + (6 if i >= 3 else 0)
                        ins = nc.scalar.activation(qc[:, i, :], bank[:, 0:TT], ACT.Identity,
                                                   bias=w["f0qkb"][:, tile:tile + 1])
                        ins.then_inc(f_qc.sem, 1)
                    f_rs.wait(act, it, s + 1)
                    copy(rowH[0:12, :], qvar).then_inc(f_rsr.sem, 1)
                    for i in range(6):
                        f_u.wait(act, it, 6 * s + i + 1)
                        dst = qs if i < 3 else ks
                        for x in range(2):
                            copy(dst[0:64, 2 * (i % 3) + x, :], qc[64 * x:64 * x + 64, i, :]).then_inc(f_h.sem, 1)
                        if i >= 3:
                            f_l.wait(act, it, 12 * s + 2 * i - 4)
                        copy(rh[64:128, i % 3, :], qc[64:128, i, :]).then_inc(f_h.sem, 1)
                    bank = S.wait(act, it, f"f0_mx{s}", 0)
                    copy(rowH[0:6, :], bank[0:6, 0:TT], scale=-1.0).then_inc(f_nm.sem, 1)

                    for n in range(12):
                        bank = S.wait(act, it, f"f0_S2{s}", n)
                        if n >= P:
                            C.wait(act, it, f"f0_pv{s}", (n - P) // 2)
                        nc.scalar.activation(probs[:, n % P, :], bank[0:HALF, 0:TT], ACT.Exp, scale=0.125
                                             ).then_inc(f_exp.sem, 1)
                    bank = S.wait(act, it, f"f0_g{s}", 0)
                    copy(rowH[0:12, :], bank[0:12, 0:TT]).then_inc(f_row.sem, 1)
                    for i in range(3):
                        f_on.wait(act, it, 3 * s + i + 1)
                        copy(rh[:, i, :], sc[:, i, :]).then_inc(f_onh.sem, 1)

                turned(it, "a1")
                attention(it, "a1", 16.0 ** -0.5)

                turned(it, "f1")
                bank = S.wait(act, it, "f1_r", 0)
                nc.scalar.activation(lg[:, :, 0:8], bank[0:HALF, 0:NT * 8].rearrange("p (t e) -> p t e", e=8),
                                     ACT.Exp, scale=-1.0).then_inc(m_exp.sem, 1)
                bank = S.wait(act, it, "f1_c", 0)
                copy(rowH[0:28, :], bank[0:28, 0:TT]).then_inc(m_row.sem, 1)

                def relu(m):
                    bank_ = S.wait(act, it, f"f1_h{m}", 0)
                    if m >= 3:
                        m_hid.wait(act, it, m - 2)
                    nc.scalar.activation(sa[:, m % 3, :], bank_[:, 0:TT], ACT.Relu).then_inc(m_relu.sem, 1)

                relu(0)
                for m in range(MOE_M):
                    if m + 1 < MOE_M:
                        relu(m + 1)
                    m_hid.wait(act, it, m + 1)
                    if m >= 3:
                        m_used.wait(act, it, m - 2)
                    copy(rh[:, m % 3, :], sc[:, m % 3, :]).then_inc(m_h.sem, 1)

            with act.Fori(0, STEPS) as it:
                body(it)

        @block.vector
        def _(dve):
            tt = nc.vector.tensor_tensor

            def hold(e):
                e.sem_inc(held, 1)

            def low(out_, full, high):
                return tt(out_, full, w32(high), ALU.subtract)

            def normalise(it, s, src):
                for t in range(NT):
                    nc.vector.bn_stats(bnst[:, t, :], src[:, t, :]).then_inc(stats[s].sem, 1)
                for t in range(NT):
                    stats[s].wait(dve, it, t + 1)
                    hold(dve)
                    nc.vector.bn_aggr(bnmv[:, t, :], bnst[:, t, :]).then_inc(stats[s].sem, 1)
                rstds[s].wait(dve, it)
                for t in range(NT):
                    for d0, s0, n in ((0, 0, D), (D, 128, 256 - D)):
                        nc.vector.tensor_scalar(xn[:, t, d0:d0 + n], src[:, t, s0:s0 + n], bnmv[:, t, 0:1],
                                                rstd[:, t:t + 1], ALU.subtract, ALU.mult).then_inc(normed[s].sem, 1)
                for k, x in enumerate((xA, xB)):
                    bank = S.wait(dve, it, s + "_x", k)
                    xh[s].wait(dve, it, k + 1)
                    low(x[:, 1, :], bank[:, 0:TT], x[:, 0, :]).then_inc(xl[s].sem, 1)

            def largest(bank, t0, head):
                return nc.vector.tensor_reduce(mx[:, t0:t0 + 2, head], bank[0:HALF, 0:TT]
                                               .rearrange("p (t k) -> p t k", t=2), AX.X, ALU.max)

            def add_up(it, s, stage, src, n0=0):
                for t in range(NT):
                    bank = C.wait(dve, it, stage, t)
                    tt(h[:, t, :], src[:, t, :], bank[0:HALF, 0:D], ALU.add).then_inc(resid[s].sem, 1)

            def attention(it, s):
                if s == "a0":
                    for m in range(3):
                        bank = S.wait(dve, it, "a0_qk", m)
                        st_h[s].wait(dve, it, m + 1)
                        low(rl[:, m, :], bank[:, 0:TT], rh[:, m, :]).then_inc(st_l[s].sem, 1)
                else:
                    swap = [(i // 16) * 16 + (i + 8) % 16 for i in range(32)]
                    for m in range(3):
                        rope_b.wait(dve, it, m + 1)
                        hold(dve)
                        nc.vector.stream_shuffle(sc[:, m, :], sa[:, m, :], swap).then_inc(rope_s.sem, 1)
                    for m in range(3):
                        rope_s.wait(dve, it, m + 1)
                        for im in range(IMS):
                            ins = tt(sc[:, m, img(im)], sc[:, m, img(im)], w["sin"][:, :], ALU.mult)
                        ins.then_inc(rope_p.sem, 1)
                for n in range(24):
                    bank = S.wait(dve, it, s + "_S1", n)
                    largest(bank, 2 * (n % 2), n // 2).then_inc(maxes[s].sem, 1)
                to_all = [16 + i % 16 for i in range(32)]
                for g in range(3):
                    bank = C.wait(dve, it, s + "_pv", g)
                    hold(dve)
                    nc.vector.stream_shuffle(sa[:, g, :], bank[:, 0:TT], to_all).then_inc(dens[s].sem, 1)
                    dens[s].wait(dve, it, 2 * g + 1)
                    nc.vector.reciprocal(sa[:, g, :], sa[:, g, :]).then_inc(dens[s].sem, 1)
                    dens[s].wait(dve, it, 2 * g + 2)
                    tt(sc[:, g, :], bank[:, 0:TT], sa[:, g, :], ALU.mult).then_inc(quot[s].sem, 1)

            def gates(it):
                n = [0]

                def step(ins, last=True, alone=False):
                    n[0] += 1
                    ins.then_inc(f_gate.sem, 1)
                    if last:
                        f_gate.wait(dve, it, n[0])
                    if alone:
                        hold(dve)

                pairs = lg[:, :, 10:14].rearrange("p t (a b) -> p t a b", b=2)
                f_v.wait(dve, it)
                step(nc.vector.tensor_reduce(gmax[:, :, 0], lg[:, :, 0:10], AX.X, ALU.max), False)
                step(nc.vector.tensor_reduce(gmax[:, :, 1:3], pairs, AX.X, ALU.max))
                step(tt(lg[:, :, 0:10], lg[:, :, 0:10], gmax[:, :, 0:1].to_broadcast([HALF, NT, 10]),
                        ALU.subtract), False)
                step(tt(pairs, pairs, gmax[:, :, 1:3].unsqueeze(3).to_broadcast([HALF, NT, 2, 2]), ALU.subtract))
                f_gexp.wait(dve, it)
                step(nc.vector.tensor_reduce(gsum[:, :, 0], lg[:, :, 0:10], AX.X, ALU.add), False)
                step(nc.vector.tensor_reduce(gsum[:, :, 1:3], pairs, AX.X, ALU.add))
                step(nc.vector.reciprocal(gsum[:, :, :], gsum[:, :, :]))
                step(tt(lg[:, :, 0:10], lg[:, :, 0:10], gsum[:, :, 0:1].to_broadcast([HALF, NT, 10]),
                        ALU.mult), False)
                step(tt(pairs, pairs, gsum[:, :, 1:3].unsqueeze(3).to_broadcast([HALF, NT, 2, 2]), ALU.mult),
                     alone=True)
                top_two(step, lg, 10)
                step(tt(hot[:, :, :], hot[:, :, :], lg[:, :, 0:10], ALU.mult))
                step(nc.vector.tensor_reduce(gsum[:, :, 0], hot[:, :, :], AX.X, ALU.add))
                step(nc.vector.tensor_scalar(gsum[:, :, 0], gsum[:, :, 0], 2.0 ** -23, None, ALU.max))
                step(nc.vector.reciprocal(gsum[:, :, 0], gsum[:, :, 0]))
                step(tt(hot[:, :, :], hot[:, :, :], gsum[:, :, 0:1].to_broadcast([HALF, NT, 10]), ALU.mult))
                step(nc.vector.scalar_tensor_tensor(gm[:, :, 2:12], hot[:, :, :], 4.0,
                                                    lg[:, :, 11:12].to_broadcast([HALF, NT, 10]),
                                                    ALU.mult, ALU.mult), False)
                step(nc.vector.scalar_tensor_tensor(gm[:, :, 0:2], lg[:, :, 12:14], 4.0,
                                                    lg[:, :, 10:11].to_broadcast([HALF, NT, 2]),
                                                    ALU.mult, ALU.mult), False)
                assert n[0] == f_gate.per, n

            def top_two(step, src, n):
                for t in range(NT):
                    step(nc.vector.max(top8[:, t, :], src[:, t, 0:n]), t == NT - 1, t == NT - 1)
                for t in range(NT):
                    step(nc.vector.max_index(idx8[:, t, :], top8[:, t, :], src[:, t, 0:n]), t == NT - 1)
                step(nc.vector.tensor_copy(idxf[:, :, 0:2], idx8[:, :, 0:2]))
                iota = w["iota"][:, 0:n].unsqueeze(1).to_broadcast([HALF, NT, n])
                for k, dst in enumerate((hot, hot2)):
                    step(tt(dst[:, :, 0:n], iota, idxf[:, :, k:k + 1].to_broadcast([HALF, NT, n]), ALU.is_equal),
                         k == 1)
                step(tt(hot[:, :, 0:n], hot[:, :, 0:n], hot2[:, :, 0:n], ALU.add))

            def router(it):
                n = [0]

                def step(ins, last=True, alone=False):
                    n[0] += 1
                    ins.then_inc(m_gate.sem, 1)
                    if last:
                        m_gate.wait(dve, it, n[0])
                    if alone:
                        hold(dve)

                m_exp.wait(dve, it)
                score = lg[:, :, 0:8]
                step(nc.vector.tensor_scalar(score, score, 1.0, None, ALU.add))
                step(nc.vector.reciprocal(score, score))
                step(tt(hot[:, :, 0:8], score, w["bal"][:, :].unsqueeze(1).to_broadcast([HALF, NT, 8]), ALU.add),
                     alone=True)
                top_two(step, hot, 8)
                step(tt(hot[:, :, 0:8], hot[:, :, 0:8], score, ALU.mult))
                step(nc.vector.tensor_reduce(gsum[:, :, 0], hot[:, :, 0:8], AX.X, ALU.add))
                step(nc.vector.tensor_scalar(gsum[:, :, 0], gsum[:, :, 0], 1e-20, None, ALU.add))
                step(nc.vector.reciprocal(gsum[:, :, 0], gsum[:, :, 0]))
                step(tt(hot[:, :, 0:8], hot[:, :, 0:8], gsum[:, :, 0:1].to_broadcast([HALF, NT, 8]), ALU.mult))
                step(nc.vector.tensor_copy(cm[:, :, 0:24].rearrange("p t (e r) -> p t e r", r=3),
                                           hot[:, :, 0:8].unsqueeze(3).to_broadcast([HALF, NT, 8, 3])), False)
                assert n[0] == m_gate.per, n

            def body(it):
                dve.wait_ge(h_in, 32 * it + 32)
                normalise(it, "a0", hin)
                attention(it, "a0")
                dve.wait_ge(h_out, 16 * it)
                add_up(it, "a0", "a0_out", hin)

                resid["a0"].wait(dve, it)
                normalise(it, "f0", h)
                gates(it)
                for s in range(2):
                    bank = S.wait(dve, it, f"f0_var{s}", 0)
                    nc.vector.tensor_scalar(qvar, bank[0:12, 0:TT], EPS, None, ALU.add).then_inc(f_var.sem, 1)
                    for i in range(6):
                        bank = S.wait(dve, it, f"f0_rs{s}", i)
                        f_qc.wait(dve, it, 6 * s + i + 1)
                        tt(qc[:, i, :], qc[:, i, :], bank[:, 0:TT], ALU.mult).then_inc(f_t.sem, 1)
                        f_t.wait(dve, it, 6 * s + i + 1)
                        k = 2 * (i // 3)
                        nc.vector.tensor_scalar(qc[:, i, :], qc[:, i, :], w["f0n"][:, k:k + 1],
                                                w["f0n"][:, k + 1:k + 2], ALU.mult, ALU.add).then_inc(f_u.sem, 1)
                    for n in range(12):
                        bank = S.wait(dve, it, f"f0_S1{s}", n)
                        largest(bank, 2 * (n % 2), 6 * s + n // 2).then_inc(f_max.sem, 1)
                    for hd in range(6):
                        x, i = hd % 2, hd // 2
                        bank = C.wait(dve, it, f"f0_pv{s}", hd)
                        r, other = slice(64 * x, 64 * x + 64), slice(64 - 64 * x, 128 - 64 * x)
                        nc.vector.reciprocal(sa[r, i, :], bank[other, 0:TT]).then_inc(f_den.sem, 1)
                        f_den.wait(dve, it, 6 * s + hd + 1)
                        tt(sc[r, i, :], bank[r, 0:TT], sa[r, i, :], ALU.mult).then_inc(f_quot.sem, 1)
                    bank = S.wait(dve, it, f"f0_g{s}", 0)
                    f_row.wait(dve, it, 2 * s + 1)
                    low(rowH[64:76, :], bank[0:12, 0:TT], rowH[0:12, :]).then_inc(f_row.sem, 1)
                    f_quot.wait(dve, it, 6 * s + 6)
                    for i in range(3):
                        bank = S.wait(dve, it, f"f0_gb{s}", i)
                        nc.vector.scalar_tensor_tensor(sc[:, i, :], sc[:, i, :], w["f0vb"][:, 3 * s + i:3 * s + i + 1],
                                                       bank[:, 0:TT], ALU.add, ALU.mult).then_inc(f_on.sem, 1)
                    if s == 0:
                        h_bias.wait(dve, it)
                    else:
                        resid["f0"].wait(dve, it, 4)
                    add_up(it, "f0", f"f0_out{s}", h)

                resid["f0"].wait(dve, it)
                normalise(it, "a1", h)
                attention(it, "a1")
                add_up(it, "a1", "a1_out", h)

                resid["a1"].wait(dve, it)
                normalise(it, "f1", h)
                router(it)
                bank = S.wait(dve, it, "f1_c", 0)
                m_row.wait(dve, it, 1)
                low(rowH[64:92, :], bank[0:28, 0:TT], rowH[0:28, :]).then_inc(m_row.sem, 1)
                for m in range(MOE_M):
                    bank = S.wait(dve, it, f"f1_cb{m}", 0)
                    m_relu.wait(dve, it, m + 1)
                    if m >= 3:
                        m_l.wait(dve, it, m - 2)
                    tt(sc[:, m % 3, :], sa[:, m % 3, :], bank[:, 0:TT], ALU.mult).then_inc(m_c.sem, 1)
                add_up(it, "f1", "f1_y", h)

            dve.wait_ge(ready, NREADY)
            with dve.Fori(0, STEPS) as it:
                body(it)

        @block.tensor
        def _(pe):
            def mm(out_, lhs, rhs, first, last):
                return nc.tensor.matmul(out_, lhs, rhs, start=first, stop=last, skip_group_check=True)

            def features(out_, c0):
                c = slice(c0, c0 + 128)
                mm(out_, w["A"][:, c], xA[:, 0, :], True, False)
                mm(out_, w["A"][:, c], xA[:, 1, :], False, False)
                mm(out_, w["Al"][:, c], xA[:, 0, :], False, False)
                mm(out_, w["B"][:, c], xB[:, 0, :], False, False)
                return mm(out_, w["B"][:, c], xB[:, 1, :], False, True)

            def rows(out_, t, c0, n):
                c = slice(c0, c0 + n)
                mm(out_, xA[:, 0, tok(t)], w["A"][:, c], True, False)
                mm(out_, xA[:, 0, tok(t)], w["Al"][:, c], False, False)
                mm(out_, xA[:, 1, tok(t)], w["A"][:, c], False, False)
                mm(out_, xB[:, 0, tok(t)], w["B"][:, c], False, False)
                return mm(out_, xB[:, 1, tok(t)], w["B"][:, c], False, True)

            def turn_tokens(it, s):
                normed[s].wait(pe, it)
                for k in range(2):
                    bank = S.claim(pe, it, s + "_x", k)
                    for t in range(NT):
                        last = nc.tensor.transpose(bank[:, tok(t)], xn[:, t, 128 * k:128 * k + 128],
                                                   ident[0:HALF, 0:HALF])
                    S.fill(last)

            def turn_rows(it, stage, src, n):
                bank = S.claim(pe, it, stage, 0)
                for t in range(NT):
                    last = nc.tensor.transpose(bank[0:n, tok(t)], src[:, t, :], ident[0:HALF, 0:HALF])
                S.fill(last)

            def project(it, stage, group, n, h_sig, h_of):
                for t in range(NT):
                    bank = C.claim(pe, it, stage, t)[0:HALF, 0:D]
                    for g in range(n):
                        if t == 0:
                            h_sig.wait(pe, it, h_of(g))
                        c = slice((group + g) * D, (group + g + 1) * D)
                        mm(bank, rh[:, g, tok(t)], w["Kh"][:, c], g == 0, False)
                        mm(bank, rh[:, g, tok(t)], w["Kl"][:, c], False, False)
                        last = mm(bank, rl[:, g, tok(t)], w["Kh"][:, c], False, g == n - 1)
                    C.fill(last)

            def attention(it, s, c_qk, c_v, group):
                turn_tokens(it, s)
                xl[s].wait(pe, it)
                for m in range(3):
                    bank = S.claim(pe, it, s + "_qk", m)
                    S.fill(features(bank[:, 0:TT], c_qk + 128 * m))
                for k in range(2):
                    bank = S.claim(pe, it, s + "_v", k)
                    for x in range(2):
                        last = rows(bank[0:HALF, D * x:D * x + D], 2 * k + x, c_v, D)
                    S.fill(last)
                stack[s].wait(pe, it)
                for n in range(24):
                    head, im = n // 2, n % 2
                    bank = S.claim(pe, it, s + "_S1", n)
                    for x in range(2):
                        last = mm(bank[0:HALF, TOK * x:TOK * x + TOK], qs[0:65, head, tok(2 * im + x)],
                                  ks[0:65, head, img(im)], True, True)
                    S.fill(last)
                maxes[s].wait(pe, it)
                turn_rows(it, s + "_mx", mx, NH)
                nmrow[s].wait(pe, it)

                def scores(b):
                    for j in range(4):
                        head, im = 4 * (b // 2) + j, b % 2
                        bank = S.claim(pe, it, s + "_S2", 4 * b + j)
                        for x in range(2):
                            last = mm(bank[0:HALF, TOK * x:TOK * x + TOK], ks[0:66, head, tok(2 * im + x)],
                                      qs[0:66, head, img(im)], True, True)
                        S.fill(last)

                def values(b):
                    g, im = b // 2, b % 2
                    if im == 0:
                        C.claim(pe, it, s + "_pv", g)
                    bank = C.banks[(C.first[s + "_pv"] + g) % 4]
                    va_in[s].wait(pe, it)
                    ones[s].wait(pe, it)
                    exps[s].wait(pe, it, 4 * b + 4)
                    for x in range(2):
                        for j in range(4):
                            last = mm(bank[32 * j:32 * j + 32, img(im)], va[:, 2 * im + x, 2 * g + j // 2, j % 2, :],
                                      probs[:, (4 * b + j) % P, TOK * x:TOK * x + TOK], x == 0, x == 1)
                    if im:
                        C.fill(last)
                    else:
                        last.then_inc(pvs[s].sem, 1)

                scores(0)
                for b in range(1, 6):
                    scores(b)
                    values(b - 1)
                values(5)
                project(it, s + "_out", group, 3, on_l[s], lambda g: g + 1)

            def body(it):
                attention(it, "a0", C_A0QK, C_A0QK + D, K_O0)

                turn_tokens(it, "f0")
                xl["f0"].wait(pe, it)
                for t in range(NT):
                    for k, (c, n) in enumerate(((C_F0V, NV0), (C_F0V + NV0, NV1))):
                        bank = S.claim(pe, it, "f0_v", 2 * t + k)
                        S.fill(rows(bank[0:HALF, 0:n], t, c, n))
                for s in range(2):
                    for i in range(6):
                        tile = 3 * s + i % 3 + (6 if i >= 3 else 0)
                        bank = S.claim(pe, it, f"f0_qk{s}", i)
                        S.fill(features(bank[:, 0:TT], C_F0QK + 128 * tile))
                    bank = S.claim(pe, it, f"f0_var{s}", 0)
                    for i in range(6):
                        f_sq.wait(pe, it, 6 * s + i + 1)
                        last = mm(bank[0:12, 0:TT], sumcol[:, 10 - 2 * i:22 - 2 * i], sa[:, i % 3, :], i == 0, i == 5)
                        if i < 5:
                            last.then_inc(f_squ.sem, 1)
                    S.fill(last)
                    f_rsr.wait(pe, it, 2 * s + 2)
                    for i in range(6):
                        bank = S.claim(pe, it, f"f0_rs{s}", i)
                        S.fill(mm(bank[:, 0:TT], sel[:, i, :], rowH[:, :], True, True))
                    f_l.wait(pe, it, 12 * s + 12)
                    for n in range(12):
                        head, im = n // 2, n % 2
                        bank = S.claim(pe, it, f"f0_S1{s}", n)
                        for x in range(2):
                            last = mm(bank[0:HALF, TOK * x:TOK * x + TOK], qs[0:65, head, tok(2 * im + x)],
                                      ks[0:65, head, img(im)], True, True)
                        S.fill(last)
                    f_max.wait(pe, it, 12 * s + 12)
                    turn_rows(it, f"f0_mx{s}", mx[:, :, 6 * s:6 * s + 6], 6)
                    pe.wait_ge(f_nmrow.sem, it * f_nmrow.per + 96 * (s + 1))

                    def scores(hd):
                        for im in range(IMS):
                            bank = S.claim(pe, it, f"f0_S2{s}", 2 * hd + im)
                            for x in range(2):
                                o = bank[0:HALF, TOK * x:TOK * x + TOK]
                                keys = tok(2 * im + x)
                                mm(o, ks[0:65, hd, keys], qs[0:65, hd, img(im)], True, False)
                                mm(o, ks[0:66, hd, keys], qs[0:66, 6 + hd, img(im)], False, False)
                                last = mm(o, ks[0:65, 6 + hd, keys], qs[0:65, hd, img(im)], False, True)
                            S.fill(last)

                    def values(hd):
                        head = 6 * s + hd
                        bank = C.claim(pe, it, f"f0_pv{s}", hd)
                        f_exp.wait(pe, it, 12 * s + 2 * hd + 2)
                        block_ = slice(0, 2) if head % 2 == 0 else slice(1, 3)
                        for im in range(IMS):
                            for x in range(2):
                                v = vf[:, 2 * im + x, head // 2, block_, :].rearrange("p a d -> p (a d)")
                                last = mm(bank[:, img(im)], v,
                                          probs[:, (2 * hd + im) % P, TOK * x:TOK * x + TOK], x == 0, x == 1)
                        C.fill(last)

                    scores(0)
                    for hd in range(1, 6):
                        scores(hd)
                        values(hd - 1)
                    values(5)
                    f_gate.wait(pe, it)
                    turn_rows(it, f"f0_g{s}", gm, NH)
                    f_row.wait(pe, it, 2 * s + 2)
                    for i in range(3):
                        bank = S.claim(pe, it, f"f0_gb{s}", i)
                        S.fill(mm(bank[:, 0:TT], sel[:, 3 * s + i, :], rowH[:, :], True, True))
                    project(it, f"f0_out{s}", K_PJ + 3 * s, 3, f_onl, lambda g: 3 * s + g + 1)

                attention(it, "a1", C_A1QK, C_A1V, K_O1)

                turn_tokens(it, "f1")
                xl["f1"].wait(pe, it)
                bank = S.claim(pe, it, "f1_r", 0)
                for t in range(NT):
                    last = rows(bank[0:HALF, 8 * t:8 * t + 8], t, C_RT, 8)
                S.fill(last)
                m_gate.wait(pe, it)
                turn_rows(it, "f1_c", cm, 28)
                m_row.wait(pe, it, 2)

                def hidden(m):
                    bank_ = S.claim(pe, it, f"f1_h{m}", 0)
                    S.fill(features(bank_[:, 0:TT], C_W1 + 128 * m))
                    bank_ = S.claim(pe, it, f"f1_cb{m}", 0)
                    S.fill(mm(bank_[:, 0:TT], sel[:, m, :], rowH[:, :], True, True))

                def outward(m):
                    m_l.wait(pe, it, m + 1)
                    c = slice((K_W2 + m) * D, (K_W2 + m + 1) * D)
                    for t in range(NT):
                        b = C.claim(pe, it, "f1_y", t) if m == 0 else C.banks[(C.first["f1_y"] + t) % 4]
                        o = b[0:HALF, 0:D]
                        mm(o, rh[:, m % 3, tok(t)], w["Kh"][:, c], m == 0, False)
                        mm(o, rh[:, m % 3, tok(t)], w["Kl"][:, c], False, False)
                        last = mm(o, rl[:, m % 3, tok(t)], w["Kh"][:, c], False, m == MOE_M - 1)
                        if m == MOE_M - 1:
                            C.fill(last)
                    if m < MOE_M - 1:
                        last.then_inc(m_used.sem, 1)

                hidden(0)
                hidden(1)
                for m in range(MOE_M):
                    if m + 2 < MOE_M:
                        hidden(m + 2)
                    outward(m)

            pe.wait_ge(ready, NREADY)
            with pe.Fori(0, STEPS) as it:
                body(it)


def vit_tower(nc, a, out):
    h0 = nc.dram_tensor("patch_tokens", (TOK * IMAGES, D), F32).ap()
    with ExitStack() as ctx:
        def sb(name, shape, dt=F32):
            return ctx.enter_context(nc.sbuf_tensor(name, shape, dt))

        w = {
            "A": sb("wA", [128, NCOL], F32R), "Al": sb("wAl", [128, NCOL], F32R), "B": sb("wB", [128, NCOL], F32R),
            "Kh": sb("wKh", [128, NK * D], F32R), "Kl": sb("wKl", [128, NK * D], F32R),
            "sel": sb("sel", [SELROWS, MOE_M, 128], F32R), "sumcol": sb("sumcol", [128, 22]),
            "ident": sb("ident", [128, 128]), "cos": sb("cos", [128, TOK]), "sin": sb("sin", [128, TOK]),
            "a1qkb": sb("a1qkb", [128, 3]), "f0n": sb("f0n", [128, 4]), "f0vb": sb("f0vb", [128, 6]),
            "f0qkb": sb("f0qkb", [128, 12]), "a1vb": sb("a1vb", [128, 3]), "f0pb": sb("f0pb", [HALF, D]),
            "bal": sb("bal", [HALF, 8]), "iota": sb("iota", [HALF, 10]),
        }
        setup_and_patches(nc, a, w, h0)
        layers(nc, a, w, h0, out)


def constants():
    import numpy as np

    p = np.arange(128)
    sel = np.zeros((SELROWS, MOE_M, 128), np.float32)
    for m in range(MOE_M):
        for half in range(2):
            for part in (0, 64):
                sel[part + 2 * m + half, m, 64 * half:64 * half + 64] = 1.0
    sumcol = np.zeros((128, 22), np.float32)
    sumcol[:64, 10] = sumcol[64:, 11] = 1.0 / 64
    position = np.array([i * GRID + j for i, j in token_classes()[1]], np.float32)
    inv = (1.0 / np.float32(10000.0) ** (np.arange(0, 16, 2, dtype=np.float32) / np.float32(16))).astype(np.float32)
    angle = inv[p % 8][:, None] * position[None, :]
    sign = np.where(p % 16 < 8, -1.0, 1.0).astype(np.float32)[:, None]
    return {
        "blockmean": ((p[:, None] // 64 == p[None, :] // 64) / 64).astype(np.float32),
        "sel": sel.reshape(SELROWS, -1), "sumcol": sumcol, "ident": np.eye(128, dtype=np.float32),
        "cos": np.cos(angle).astype(np.float32), "sin": (np.sin(angle) * sign).astype(np.float32),
        "iota": np.tile(np.arange(10, dtype=np.float32), (HALF, 1)),
    }


def lay_out(x, i):
    import numpy as np

    f = {k: np.asarray(v) for k, v in i.items()}
    x = np.asarray(x).reshape(IMAGES, GRID, 2, 8, GRID, 2, 8, 3)
    x = x.transpose(1, 4, 2, 5, 3, 6, 7, 0).reshape(GRID, GRID, 768, IMAGES)
    cls, _ = token_classes()
    tiles = []
    for c in cls:
        for n in range(0, len(c), 2):
            two = [x[i_, j] for i_, j in c[n:n + 2]]
            if len(two) == 1:
                two.append(np.zeros_like(two[0]))
            t = np.concatenate(two, axis=1)
            tiles.append(t.reshape(KC, 128, 128).transpose(1, 0, 2).reshape(128, KC * 128))
    tokW = f["L0_tok_W"].reshape(2, 8, 2, 8, 5, 3, D).transpose(4, 0, 2, 1, 3, 5, 6).reshape(5, KC, 128, D)

    def first(wt):
        return wt[:128]

    def rest(wt):
        return np.concatenate([wt[128:D], wt[128:D]], 0)

    w1 = np.concatenate(list(f["L1_ffn_w1"]) + [f["L1_ffn_w_fc_sh"], np.zeros((D, 64), np.float32)], 1)
    cols = np.concatenate([
        f["L0_attn_w_qkv"][:, :2 * D], f["L1_attn_w_qkv"].T, f["L0_ffn_qkv_w"],
        f["L0_ffn_wg_w"], f["L0_ffn_wg0_w"], f["L0_ffn_wg1_w"], f["L1_ffn_router_w"].T, w1], 1)
    assert cols.shape[1] == NCOL

    def spread(wo, bias=None):
        g = np.zeros((3, 4, 32, D), np.float32)
        g[:, :, :16] = wo.reshape(3, 4, 16, D)
        if bias is not None:
            g[0, 0, 16] = bias
        return g.reshape(3, 128, D)

    w2 = np.concatenate([f["L1_ffn_w2"].reshape(-1, D), f["L1_ffn_w_proj_sh"], np.zeros((64, D), np.float32)], 0)
    groups = np.concatenate([
        w2.reshape(MOE_M, 128, D), f["L0_ffn_proj_w"].reshape(6, 128, D), spread(f["L0_attn_w_out"]),
        spread(f["L1_attn_w_proj"].T, f["L1_attn_b_proj"])], 0)

    def per_head(b):
        g = np.zeros((3, 4, 32), np.float32)
        g[:, :, :16] = b.reshape(3, 4, 16)
        return g.reshape(3, 128).T

    a1b, f0b = f["L1_attn_b_qkv"], f["L0_ffn_qkv_b"]
    norm = [np.tile(f[f"L0_ffn_{k}"], 2) for k in ("q_norm_w", "q_norm_b", "k_norm_w", "k_norm_b")]
    return {
        "px": np.stack(tiles), "tokW": tokW.transpose(2, 0, 1, 3), "tokb": np.tile(f["L0_tok_b"], (128, 1)),
        "WA": first(cols), "WB": rest(cols), "WK": groups.transpose(1, 0, 2).reshape(128, NK * D),
        "qkb": f0b[:2 * 768].reshape(12, 128).T, "a1qkb": a1b[:2 * D].reshape(3, 128).T,
        "f0n": np.stack(norm, 1), "f0vb": f0b[2 * 768:].reshape(6, 128).T, "a1vb": per_head(a1b[2 * D:]),
        "f0pb": np.tile(f["L0_ffn_proj_b"], (HALF, 1)), "bal": np.tile(f["L1_ffn_balance_bias"], (HALF, 1)),
    }


def kernel(x, **inputs):
    import concourse.bacc as bacc
    import numpy as np
    from concourse.bass_utils import run_bass_kernel_spmd

    arrays = {**lay_out(x, inputs), **constants()}
    arrays = {"in_" + k: np.ascontiguousarray(v) for k, v in arrays.items()}
    nc = bacc.Bacc("TRN2", target_bir_lowering=False, num_devices=1)
    a = {k[3:]: nc.dram_tensor(k, v.shape, F32, kind="ExternalInput").ap() for k, v in arrays.items()}
    out = nc.dram_tensor("out", (IMAGES // IMS, HALF, NT, D), F32, kind="ExternalOutput").ap()
    vit_tower(nc, a, out)
    got = run_bass_kernel_spmd(nc, [arrays], core_ids=[0]).results[0]["out"]
    slots = got.reshape(-1, HALF, IMS, 2, D).transpose(0, 2, 3, 1, 4).reshape(IMAGES, TOK, D)
    at = [i * GRID + j for i, j in token_classes()[1]]
    full = np.empty_like(slots)
    full[:, at] = slots
    return full
```

```python
from contextlib import ExitStack

import concourse.bass as bass
from concourse import mybir

F32 = mybir.dt.float32
F32R = mybir.dt.float32r
U32 = mybir.dt.uint32
ALU = mybir.AluOpType
ACT = mybir.ActivationFunctionType
AX = mybir.AxisListType

IMAGES = 64
STEPS = 32
D = 192
TOK = 196
HALF = 98
IMS = 2
TT = IMS * TOK
NT = TT // HALF
NH = 12
EPS = 1e-5
GRID = 14
KC = 6

CLASSES = [("mid", "mid"), ("first", "mid"), ("last", "mid"), ("mid", "first"), ("mid", "last"),
           ("first", "first"), ("first", "last"), ("last", "first"), ("last", "last")]
MID_TILES = 72

C_A0QK, C_A1QK, C_A1V, C_F0QK = 0, 384, 768, 960
C_F0V = C_F0QK + 2 * NH * 64
NV0, NV1 = 384, 398
C_RT = C_F0V + NV0 + NV1
C_W1 = C_RT + 8
MOE_M = 14
NCOL = C_W1 + MOE_M * 128
K_W2, K_PJ, K_O0, K_O1 = 0, 14, 20, 23
NK = 26
SELROWS = 92


def token_classes():
    span = {"first": [0], "mid": list(range(1, GRID - 1)), "last": [GRID - 1]}
    cls = [[(i, j) for i in span[r] for j in span[c]] for r, c in CLASSES]
    return cls, sum(cls, [])


def edge_tiles():
    return [c for c in (1, 2, 3, 4) for k in range(6)] + [5, 6, 7, 8]


def crop_rows(c, k):
    r, q = CLASSES[c]
    quadrants = [[(0, 128, 0, 1), (0, 64, 1, 2)], [(64, 128, 1, 2), (0, 128, 2, 3)],
                 [(0, 128, 3, 4), (0, 64, 4, 5)], [(64, 128, 4, 5), (0, 128, 5, 6)]]
    kept = []
    for n, parts in enumerate(quadrants):
        low, right = n // 2, n % 2
        rows = not (low and r == "last") if k in (1, 3) else not (not low and r == "first")
        cols = not (right and q == "last") if k in (1, 2) else not (not right and q == "first")
        if rows and cols:
            kept += parts
    return [(0, 128, 0, KC)] if len(kept) == 8 else kept


def w32(ap):
    return ap.bitcast(F32)


class Signal:

    def __init__(self, sem, per):
        self.sem, self.per = sem, per

    def wait(self, e, it, k=None):
        e.wait_ge(self.sem, it * self.per + (self.per if k is None else k))


class Banks:

    def __init__(self, banks, filled, stages):
        self.banks, self.filled = banks, filled
        self.first, self.readers = {}, []
        for name, n, signal, count in stages:
            self.first[name] = len(self.readers)
            self.readers += [(signal, count(k)) for k in range(n)]
        self.total = len(self.readers)

    def claim(self, pe, it, stage, k):
        n = self.first[stage] + k
        if n >= len(self.banks):
            signal, count = self.readers[n - len(self.banks)]
            signal.wait(pe, it, count)
        return self.banks[n % len(self.banks)]

    def fill(self, ins):
        ins.then_inc(self.filled, 1)

    def wait(self, e, it, stage, k):
        e.wait_ge(self.filled, it * self.total + self.first[stage] + k + 1)
        return self.banks[(self.first[stage] + k) % len(self.banks)]


def setup_and_patches(nc, a, w, h0):
    with ExitStack() as ctx:
        def sb(name, shape, dt=F32):
            return ctx.enter_context(nc.sbuf_tensor(name, shape, dt))

        def sem(name):
            return ctx.enter_context(nc.semaphore(name))

        cuts = [0, 480, C_F0QK, C_F0QK + 768, C_F0V, C_RT, C_RT + 776, C_RT + 1544, NCOL]
        blocks = [("cols", c0, c1) for c0, c1 in zip(cuts, cuts[1:])]
        blocks += [("groups", g, min(g + 4, NK)) for g in range(0, NK, 4)]
        is_qk = [k == "cols" and C_F0QK <= c0 < C_F0V for k, c0, c1 in blocks]

        stage = sb("stage", [128, 2, 2, 784])
        headsum = sb("headsum", [128, 2, 12])
        wtok = sb("wtok", [128, 5, KC, D])
        weff = sb("weff", [128, KC, D])
        weffH = sb("weffH", [128, 2, KC, D], F32R)
        weffL = sb("weffL", [128, 2, KC, D], F32R)
        tokb = sb("tokb", [128, D])
        blockmean = sb("blockmean", [128, 128])
        qkb_in = sb("qkb_in", [128, 12])
        sel_in = sb("sel_in", [SELROWS, MOE_M * 128])
        px = sb("px", [128, 4, KC * 128])
        pxH = sb("pxH", [128, 2, KC * 128], F32R)
        pxL = sb("pxL", [128, 2, KC * 128], F32R)
        tok = sb("tok", [128, 2, D])
        ps = [ctx.enter_context(nc.psum_tensor(f"ps_tok{i}", [128, 512], F32)) for i in range(2)]
        ps_mean = ctx.enter_context(nc.psum_tensor("ps_mean", [128, 512], F32))

        wtok_in = sem("wtok_in")
        const_in = sem("const_in")
        stage_in = [sem("stage_in0"), sem("stage_in1")]
        centred = sem("centred")
        split_h = sem("split_h")
        split_l = sem("split_l")
        meaned = sem("meaned")
        small = sem("small")
        summed = sem("summed")
        weff_h = sem("weff_h")
        weff_l = sem("weff_l")
        px_in = [sem(f"px_in{i}") for i in range(4)]
        px_h = sem("px_h")
        px_l = sem("px_l")
        tok_ps = sem("tok_ps")
        tok_sb = sem("tok_sb")
        tok_out = [sem("tok_out0"), sem("tok_out1")]

        edges = edge_tiles()
        total = MID_TILES + len(edges)
        WHOLE = total - 4
        first_of = {c: MID_TILES + edges.index(c) for c in range(1, 9)}
        first_of[0] = 0
        ends, s = [], 0
        for c in range(len(CLASSES)):
            s += 1 + sum(len(crop_rows(c, k)) for k in range(1, 5))
            ends.append(s)

        block = ctx.enter_context(nc.Block())

        def since(e, sem_, v):
            if not isinstance(v, int) or v > 0:
                e.wait_ge(sem_, v)

        def all_tiles(e, body):
            for u in range(4):
                body(u, u)
            with e.Fori(1, MID_TILES // 4) as r:
                for u in range(4):
                    body(4 * r + u, u)
            for t in range(MID_TILES, total):
                body(t, t % 4)

        def rounds(t, u):
            return 4 * (t - u) + 16 if not isinstance(t, int) else 16 * (t // 4 + 1)

        @block.sync
        def _(sp):
            sp.dma_start(wtok[:, :, :, :], a["tokW"]).then_inc(wtok_in, 16)
            sp.dma_start(tokb[:, :], a["tokb"]).then_inc(wtok_in, 16)
            for t in range(4):
                sp.dma_start(px[:, t, :], a["px"][t]).then_inc(px_in[t], 16)
            for dst, name in ((blockmean, "blockmean"), (qkb_in, "qkb"), (sel_in, "sel"), (w["ident"], "ident"),
                              (w["sumcol"], "sumcol"), (w["cos"], "cos"), (w["sin"], "sin"),
                              (w["a1qkb"], "a1qkb"), (w["f0n"], "f0n"), (w["f0vb"], "f0vb"),
                              (w["a1vb"], "a1vb"), (w["f0pb"], "f0pb"), (w["bal"], "bal"), (w["iota"], "iota"), (w["parity"], "parity")):
                sp.dma_start(dst[:, :], a[name]).then_inc(const_in, 16)

            def load(t, u):
                sp.wait_ge(px_l, t - 3)
                sp.dma_start(px[:, u, :], a["px"][bass.ds(t, 1), :, :].rearrange("o p n -> (o p) n")
                             ).then_inc(px_in[u], 16)

            def store(t, u, rows):
                sp.wait_ge(tok_sb, t + 1)
                sp.dma_start(h0[bass.ds(128 * t if rows == 128 else 128 * WHOLE + 64 * (t - WHOLE), rows), :],
                             tok[0:rows, u % 2, :]).then_inc(tok_out[u % 2], 16)

            with sp.Fori(1, MID_TILES // 4) as r:
                for u in range(4):
                    load(4 * r + u, u)
                    store(4 * r + (u - 4), u, 128)
            for t in range(MID_TILES, total + 4):
                if t < total:
                    load(t, t % 4)
                store(t - 4, t % 4, 128 if t - 4 < WHOLE else 64)
            for u in range(2):
                sp.wait_ge(tok_out[u], 16 * (total // 2))
            sp.wait_ge(const_in, 16 * 15)

        @block.gpsimd
        def _(pool):
            def stage_block(i):
                if i < len(blocks):
                    kind, c0, c1 = blocks[i]
                    if kind == "cols":
                        for part, name in enumerate(("WA", "WB")):
                            pool.dma_start(stage[:, i % 2, part, 0:c1 - c0], a[name][:, c0:c1]
                                           ).then_inc(stage_in[i % 2], 16)
                    else:
                        pool.dma_start(stage[:, i % 2, 0, 0:(c1 - c0) * D], a["WK"][:, c0 * D:c1 * D]
                                       ).then_inc(stage_in[i % 2], 16)

            def class_weights(c):
                n = ends[c - 1] if c else 0
                if c:
                    pool.wait_ge(weff_h, c)
                    pool.wait_ge(weff_l, c)
                nc.gpsimd.tensor_copy(weff[:, :, :], wtok[:, 0, :, :]).then_inc(summed, 1)
                n += 1
                for k in range(1, 5):
                    for p0, p1, k0, k1 in crop_rows(c, k):
                        pool.wait_ge(summed, n)
                        nc.gpsimd.tensor_tensor(weff[p0:p1, k0:k1, :], weff[p0:p1, k0:k1, :],
                                                wtok[p0:p1, k, k0:k1, :], ALU.add).then_inc(summed, 1)
                        n += 1
                pool.wait_ge(weff_h, c + 1)
                nc.gpsimd.tensor_tensor(weffL[:, c % 2, :, :], weff[:, :, :],
                                        w32(weffH[:, c % 2, :, :]), ALU.subtract).then_inc(weff_l, 1)

            stage_block(0)
            stage_block(1)
            pool.wait_ge(wtok_in, 32)
            class_weights(0)
            for i, (kind, c0, c1) in enumerate(blocks):
                pool.wait_ge(split_h, i + 1)
                if kind == "cols":
                    n = c1 - c0
                    nc.gpsimd.tensor_tensor(w["Al"][:, c0:c1], stage[:, i % 2, 0, 0:n],
                                            w32(w["A"][:, c0:c1]), ALU.subtract).then_inc(split_l, 1)
                    pool.wait_ge(split_l, 2 * i + 1)
                    nc.gpsimd.tensor_tensor(w["B"][64:128, c0:c1], stage[64:128, i % 2, 1, 0:n],
                                            w32(w["B"][64:128, c0:c1]), ALU.subtract).then_inc(split_l, 1)
                else:
                    n = (c1 - c0) * D
                    nc.gpsimd.tensor_tensor(w["Kl"][:, c0 * D:c1 * D], stage[:, i % 2, 0, 0:n],
                                            w32(w["Kh"][:, c0 * D:c1 * D]), ALU.subtract).then_inc(split_l, 2)
                pool.wait_ge(split_l, 2 * i + 2)
                stage_block(i + 2)
            for c in range(1, len(CLASSES)):
                class_weights(c)

        @block.scalar
        def _(act):
            def weights_h(c):
                act.wait_ge(summed, ends[c])
                if c >= 2:
                    act.wait_ge(tok_ps, first_of[c - 1])
                nc.scalar.copy(weffH[:, c % 2, :, :], weff[:, :, :]).then_inc(weff_h, 1)

            def pixels_h(t, u):
                if isinstance(t, int) and t >= MID_TILES and t - 1 in [first_of[c] for c in range(1, 8)]:
                    weights_h(1 + [first_of[c] for c in range(1, 9)].index(t - 1) + 1)
                act.wait_ge(px_in[u], rounds(t, u))
                since(act, tok_ps, t - 1)
                nc.scalar.copy(pxH[:, u % 2, :], px[:, u, :]).then_inc(px_h, 1)

            weights_h(0)
            for i, (kind, c0, c1) in enumerate(blocks):
                if kind == "cols":
                    act.wait_ge(stage_in[i % 2], 32 * (i // 2 + 1))
                else:
                    n_cols = [len([b for b in blocks if b[0] == "cols"][p::2]) for p in range(2)][i % 2]
                    act.wait_ge(stage_in[i % 2], 32 * n_cols + 16 * (i // 2 + 1 - n_cols))
                if is_qk[i]:
                    act.wait_ge(centred, 3 * sum(is_qk[:i + 1]))
                n = c1 - c0
                if kind == "cols":
                    nc.scalar.copy(w["A"][:, c0:c1], stage[:, i % 2, 0, 0:n])
                    nc.scalar.copy(w["B"][:, c0:c1], stage[:, i % 2, 1, 0:n]).then_inc(split_h, 1)
                else:
                    nc.scalar.copy(w["Kh"][:, c0 * D:c1 * D], stage[:, i % 2, 0, 0:n * D]).then_inc(split_h, 1)
            weights_h(1)
            all_tiles(act, pixels_h)

        @block.vector
        def _(dve):
            n = 0
            for i in range(len(blocks)):
                if is_qk[i]:
                    part = stage[:, i % 2, :, 0:768].rearrange("p x (h d) -> p x h d", d=64)
                    dve.wait_ge(stage_in[i % 2], 32 * (i // 2 + 1))
                    since(dve, centred, n)
                    nc.vector.tensor_reduce(headsum[:, :, :], part, AX.X, ALU.add).then_inc(centred, 1)
                    dve.wait_ge(centred, n + 1)
                    nc.vector.tensor_scalar(headsum[:, :, :], headsum[:, :, :], 1.0 / 64, None,
                                            ALU.mult).then_inc(centred, 1)
                    dve.wait_ge(centred, n + 2)
                    nc.vector.tensor_tensor(part, part, headsum[:, :, :].unsqueeze(3).to_broadcast([128, 2, 12, 64]),
                                            ALU.subtract).then_inc(centred, 1)
                    n += 3
            dve.wait_ge(const_in, 16 * 15)
            nc.vector.tensor_copy(w["sel"][:, :, :].rearrange("p m n -> p (m n)"), sel_in[:, :]).then_inc(small, 1)
            nc.vector.tensor_copy(w["eye"][:, :], w["ident"][:, 0:72]).then_inc(small, 1)
            dve.wait_ge(meaned, 1)
            nc.vector.tensor_tensor(w["f0qkb"][:, :], qkb_in[:, :], ps_mean[:, 0:12], ALU.subtract).then_inc(small, 1)

            def tile(t, u):
                dve.wait_ge(px_h, t + 1)
                nc.vector.tensor_tensor(pxL[:, u % 2, :], px[:, u, :], w32(pxH[:, u % 2, :]),
                                        ALU.subtract).then_inc(px_l, 1)
                dve.wait_ge(tok_ps, t + 1)
                since(dve, tok_out[u % 2], 8 * t - 8 * (u % 2))
                nc.vector.tensor_tensor(tok[:, u % 2, :], ps[u % 2][:, 0:D], tokb[:, :], ALU.add).then_inc(tok_sb, 1)

            all_tiles(dve, tile)

        @block.tensor
        def _(pe):
            pe.wait_ge(const_in, 16 * 15)
            nc.tensor.matmul(ps_mean[:, 0:12], blockmean[:, :], qkb_in[:, :], start=True, stop=True).then_inc(meaned, 1)

            def tile(t, u):
                c = 0 if not isinstance(t, int) or t < MID_TILES else edges[t - MID_TILES]
                if isinstance(t, int) and t == first_of[c]:
                    pe.wait_ge(weff_l, c + 1)
                pe.wait_ge(px_h, t + 1)
                since(pe, tok_sb, t - 1)
                out = ps[u % 2][:, 0:D]
                for k in range(KC):
                    x = pxH[:, u % 2, 128 * k:128 * k + 128]
                    nc.tensor.matmul(out, x, weffH[:, c % 2, k, :], start=(k == 0), stop=False)
                    nc.tensor.matmul(out, x, weffL[:, c % 2, k, :], start=False, stop=False)
                pe.wait_ge(px_l, t + 1)
                for k in range(KC):
                    last = nc.tensor.matmul(out, pxL[:, u % 2, 128 * k:128 * k + 128], weffH[:, c % 2, k, :],
                                            start=False, stop=(k == KC - 1))
                last.then_inc(tok_ps, 1)

            all_tiles(pe, tile)


def layers(nc, a, w, h0, out):
    with ExitStack() as ctx:
        def sb(name, shape, dt=F32):
            return ctx.enter_context(nc.sbuf_tensor(name, shape, dt))

        def sem(name):
            return ctx.enter_context(nc.semaphore(name))

        def signal(name, per):
            return Signal(sem(name), per)

        hin = sb("hin", [HALF, NT, D])
        h = sb("h", [HALF, NT, D])
        bnst = sb("bnst", [HALF, NT, 6])
        bnmv = sb("bnmv", [HALF, NT, 2])
        vareps = sb("vareps", [HALF, NT])
        rstd = sb("rstd", [HALF, NT])
        mhalf = sb("mhalf", [HALF, 1])
        eps = sb("eps", [HALF, 1])
        xA = sb("xA", [128, 2, TT], F32R)
        xB = sb("xB", [128, 2, TT], F32R)
        qs = sb("qs", [128, NH, TT], F32R)
        ks = sb("ks", [128, NH, TT], F32R)
        q16 = qs[0:96, 0:8, :].rearrange("p (part t odd) n -> p part t odd n", part=2, t=2)
        k16 = ks[0:96, 0:4, :].rearrange("p (part t) n -> p part t n", part=2)
        vf = sb("vf", [HALF, NT, 6, 3, 64])
        va = vf[:, :, :, 0:3:2, 0:32]
        P = 6
        work = sb("work", [128, P, TT])
        probs = work[0:HALF, :, :]
        qc = work
        mx = sb("mx", [HALF, NT, 66])
        m16 = qs[:, 8:10, :]
        rh = sb("rh", [128, 3, TT], F32R)
        rl = sb("rl", [128, 3, TT], F32R)
        sa = sb("sa", [128, 3, TT])
        sc = sb("sc", [128, 3, TT])
        mx16 = [mx, sa[0:HALF, 1, 0:NT * 66].rearrange("p (t c) -> p t c", c=66)]
        qvar = sa[0:12, 0, :]
        xn = sa[0:HALF, :, :].rearrange("p a n -> p (a n)")[:, 0:NT * 256].rearrange("p (t c) -> p t c", c=256)
        rowH = sb("rowH", [SELROWS, TT], F32R)
        lg = sb("lg", [HALF, NT, 14])
        gmax = sb("gmax", [HALF, NT, 3])
        gsum = sb("gsum", [HALF, NT, 3])
        top8 = sb("top8", [HALF, NT, 8])
        idx8 = sb("idx8", [HALF, NT, 8], U32)
        idxf = sb("idxf", [HALF, NT, 8])
        hot = sb("hot", [HALF, NT, 10])
        hot2 = sb("hot2", [HALF, NT, 10])
        gm = sb("gm", [HALF, NT, NH])
        cm = mx[:, :, 34:62]

        banks = [ctx.enter_context(nc.psum_tensor(f"ps{i}", [128, 512], F32)) for i in range(8)]
        ready = sem("ready")
        held_pool = sem("held_pool")
        held = sem("held")
        h_in = sem("h_in")
        h_out = sem("h_out")
        subs = ("a0", "f0", "a1", "f1")
        stats = {s: signal(s + "_stats", 8) for s in subs}
        vare = {s: signal(s + "_vare", 1) for s in subs}
        rstds = {s: signal(s + "_rstd", 1) for s in subs}
        normed = {s: signal(s + "_normed", 8) for s in subs}
        xh = {s: signal(s + "_xh", 2) for s in subs}
        xl = {s: signal(s + "_xl", 2) for s in subs}
        resid = {"a0": signal("a0_resid", 4), "f0": signal("f0_resid", 8), "a1": signal("a1_resid", 4),
                 "f1": signal("f1_resid", 4)}
        at = ("a0", "a1")
        q_h = {s: signal(s + "_q_h", 4) for s in at}
        q_l = {s: signal(s + "_q_l", 4) for s in at}
        k_h = {s: signal(s + "_k_h", 2) for s in at}
        k_l = {s: signal(s + "_k_l", 2) for s in at}
        ones = {s: signal(s + "_ones", 1) for s in at}
        va_in = {s: signal(s + "_va", 2) for s in at}
        maxes = {s: signal(s + "_maxes", 24) for s in at}
        nm = {s: signal(s + "_nm", 2) for s in at}
        exps = {s: signal(s + "_exps", 24) for s in at}
        pvs = {s: signal(s + "_pvs", 3) for s in at}
        dens = {s: signal(s + "_dens", 6) for s in at}
        quot = {s: signal(s + "_quot", 3) for s in at}
        on_h = {s: signal(s + "_on_h", 3) for s in at}
        on_l = {s: signal(s + "_on_l", 3) for s in at}
        rope_b = signal("rope_b", 4)
        rope_s = signal("rope_s", 4)
        rope_p = signal("rope_p", 4)
        rope_c = signal("rope_c", 4)
        rope_u = signal("rope_u", 4)
        row64 = signal("row64", 2)
        a1_bias = signal("a1_bias", 3)
        h_bias = signal("h_bias", 4)
        f_v = signal("f_v", 12)
        f_gate = signal("f_gate", 28)
        f_gexp = signal("f_gexp", 1)
        f_row = signal("f_row", 4)
        f_qc = signal("f_qc", 12)
        f_sq = signal("f_sq", 12)
        f_squ = signal("f_squ", 10)
        f_dev = signal("f_dev", 2)
        f_rs = signal("f_rs", 2)
        f_rsr = signal("f_rsr", 4)
        f_t = signal("f_t", 12)
        f_u = signal("f_u", 12)
        f_h = signal("f_h", 36)
        f_l = signal("f_l", 24)
        f_max = signal("f_max", 24)
        f_nm = signal("f_nm", 2)
        f_exp = signal("f_exp", 24)
        f_den = signal("f_den", 12)
        f_quot = signal("f_quot", 12)
        f_on = signal("f_on", 6)
        f_onh = signal("f_onh", 6)
        f_onl = signal("f_onl", 6)
        m_exp = signal("m_exp", 1)
        m_gate = signal("m_gate", 21)
        m_row = signal("m_row", 2)
        m_relu = signal("m_relu", MOE_M)
        m_c = signal("m_c", MOE_M)
        m_hid = signal("m_hid", MOE_M)
        m_h = signal("m_h", MOE_M)
        m_l = signal("m_l", MOE_M)
        m_used = signal("m_used", MOE_M - 1)

        ident, eye, sel, sumcol = w["ident"], w["eye"], w["sel"], w["sumcol"]
        NREADY = 9

        def attention_fills(s):
            fills = [(s + "_x", 2, xl[s], after(0))]
            for m in range(2):
                if s == "a0":
                    fills += [(f"a0_q{m}", 1, q_l[s], after(2 * m + 1)), (f"a0_k{m}", 1, k_l[s], after(m))]
                else:
                    fills += [(f"a1_q{m}", 1, rope_b, after(2 * m)), (f"a1_k{m}", 1, rope_b, after(2 * m + 1))]
            fills += [(s + "_v", 2, va_in[s], after(0))]
            for stage, n in S1_S2:
                if stage == "S1":
                    fills += [(f"{s}_S1{n}", 4, maxes[s], after(4 * n))]
                elif stage == "mx":
                    fills += [(f"{s}_mx{n}", 1, nm[s], after(n))]
                else:
                    fills += [(f"{s}_S2{n}", 4, exps[s], after(4 * n))]
            return fills

        BY_PAIR = [0, 3, 1, 4, 2, 5]

        S1_S2 = [("S1", 0), ("S1", 1), ("S1", 2), ("S1", 3), ("mx", 0), ("S1", 4), ("S2", 0), ("S1", 5),
                 ("S2", 1), ("mx", 1), ("S2", 2), ("S2", 3), ("S2", 4), ("S2", 5)]

        def after(n):
            return lambda k: n + k + 1

        s_fills = attention_fills("a0")
        s_fills += [("f0_x", 2, xl["f0"], after(0)), ("f0_qk0", 6, f_sq, after(0)),
                    ("f0_v", 8, f_v, lambda k: 3 * (k // 2) + 1 + 2 * (k % 2))]
        for s in range(2):
            s_fills += [(f"f0_rs{s}", 6, f_t, after(6 * s)), (f"f0_S1{s}", 12, f_max, after(12 * s)),
                        (f"f0_mx{s}", 1, f_nm, after(s)), (f"f0_S2{s}", 12, f_exp, after(12 * s)),
                        (f"f0_g{s}", 1, f_row, after(2 * s + 1))]
            if s == 0:
                s_fills += [("f0_qk1", 6, f_sq, after(6))]
            s_fills += [(f"f0_gb{s}", 3, f_on, after(3 * s))]
        s_fills += attention_fills("a1")
        s_fills += [("f1_x", 2, xl["f1"], after(0)), ("f1_r", 1, m_exp, after(0)), ("f1_c", 1, m_row, after(1))]
        for m in range(MOE_M):
            s_fills += [(f"f1_h{m}", 1, m_relu, after(m)), (f"f1_cb{m}", 1, m_c, after(m))]
        c_fills = [("a0_pv", 3, quot["a0"], after(0)), ("a0_out", 4, resid["a0"], after(0))]
        c_fills += [("f0_var0", 1, f_dev, after(0)), ("f0_pv0", 6, f_quot, after(0)), ("f0_var1", 1, f_dev, after(1)),
                    ("f0_out0", 4, resid["f0"], after(0)), ("f0_pv1", 6, f_quot, after(6)),
                    ("f0_out1", 4, resid["f0"], after(4))]
        c_fills += [("a1_pv", 3, quot["a1"], after(0)), ("a1_out", 4, resid["a1"], after(0)),
                    ("f1_y", 4, resid["f1"], after(0))]
        S = Banks(banks[:4], sem("s_filled"), s_fills)
        C = Banks(banks[4:], sem("c_filled"), c_fills)

        def tok(t):
            return slice(HALF * t, HALF * t + HALF)

        def img(im):
            return slice(TOK * im, TOK * im + TOK)

        def images(tile):
            return tile.rearrange("p (i t) -> p i t", i=IMS)

        def turn(table):
            return table[0:96, :].unsqueeze(1).to_broadcast([96, IMS, TOK])

        block = ctx.enter_context(nc.Block())

        @block.sync
        def _(sp):
            def load(it):
                for half in range(2):
                    sp.dma_start(hin[:, half:NT:2, :],
                                 h0v[half][:, bass.ds(IMS * it, IMS), :]).then_inc(h_in, 16)

            h0v = [h0[IMAGES * HALF * half:IMAGES * HALF * (half + 1), :].rearrange("(p b) d -> p b d", b=IMAGES)
                   for half in range(2)]

            def body(it, more):
                if more:
                    resid["a0"].wait(sp, it)
                    load(it + 1)
                resid["f1"].wait(sp, it)
                sp.dma_start(out[bass.ds(it, 1)].rearrange("o p t d -> (o p) t d"), h[:, :, :]).then_inc(h_out, 16)

            load(0)
            if STEPS > 1:
                with sp.Fori(0, STEPS - 1) as it:
                    body(it, True)
            body(STEPS - 1, False)
            sp.wait_ge(h_out, 16 * STEPS)

        @block.gpsimd
        def _(pool):
            constant = [(mhalf[:, :], -0.5), (eps[:, :], EPS), (w32(qs[64:65, :, :]), 0.0), (w32(ks[64:65, :, :]), 1.0),
                        (vf[:, :, :, 1, :], 1.0), (mx[:, :, :], 0.0), (w32(rowH[:, :]), 0.0), (cm[:, :, 24:27], 1.0),
                        (cm[:, :, 27:28], 0.0)]
            for n, (to, value) in enumerate(constant):
                nc.gpsimd.memset(to, value).then_inc(ready, 1)
                pool.wait_ge(ready, n + 1)

            def rstd_of_tokens(it, s):
                stats[s].wait(pool, it)
                nc.gpsimd.tensor_tensor(vareps[:, :], bnmv[:, :, 1], eps[:, :].to_broadcast([HALF, NT]), ALU.add).then_inc(vare[s].sem, 1)
                vare[s].wait(pool, it)
                nc.gpsimd.tensor_tensor(rstd[:, :], vareps[:, :], mhalf[:, :].to_broadcast([HALF, NT]), ALU.pow).then_inc(rstds[s].sem, 1)

            def low(out_, full, high):
                return nc.gpsimd.tensor_tensor(out_, full, w32(high), ALU.subtract)

            def ones_beside_values(it, s):
                for t in range(NT):
                    ins = nc.gpsimd.memset(va[:, t, :, :, 16:32], 1.0)
                ins.then_inc(ones[s].sem, 1)

            def outputs(it, s):
                for g in range(3):
                    quot[s].wait(pool, it, g + 1)
                    if s == "a1":
                        nc.gpsimd.tensor_tensor(sc[:, g, :], sc[:, g, :], w["a1vb"][:, g:g + 1]
                                                .to_broadcast([128, TT]), ALU.add).then_inc(a1_bias.sem, 1)
                    on_h[s].wait(pool, it, g + 1)
                    low(rl[:, g, :], sc[:, g, :], rh[:, g, :]).then_inc(on_l[s].sem, 1)

            def body(it):
                rstd_of_tokens(it, "a0")
                ones_beside_values(it, "a0")
                outputs(it, "a0")
                on_l["a0"].wait(pool, it)
                pool.sem_inc(held_pool, 1)
                nc.gpsimd.memset(w32(qs[64:65, 0:10, :]), 0.0).then_inc(row64.sem, 1)
                nc.gpsimd.memset(w32(ks[64:65, 0:4, :]), 1.0).then_inc(row64.sem, 1)
                row64.wait(pool, it)

                rstd_of_tokens(it, "f0")
                normed["f0"].wait(pool, it)
                for t in range(NT):
                    nc.gpsimd.tensor_tensor(h[:, t, :], h[:, t, :], w["f0pb"][:, :], ALU.add).then_inc(h_bias.sem, 1)
                h_bias.wait(pool, it)
                for s in range(2):
                    for k, i in enumerate(BY_PAIR):
                        dst = qs if i < 3 else ks
                        for x in range(2):
                            hd = 2 * (i % 3) + x
                            f_h.wait(pool, it, 18 * s + 3 * k + 1 + 2 * x)
                            high = dst[0:64, hd, :] if x == 0 else rh[64:128, k % 3, :]
                            low(dst[0:64, 6 + hd, :], qc[64 * x:64 * x + 64, i, :], high).then_inc(f_l.sem, 1)
                    for i in range(3):
                        f_onh.wait(pool, it, 3 * s + i + 1)
                        low(rl[:, i, :], sc[:, i, :], rh[:, i, :]).then_inc(f_onl.sem, 1)

                rstd_of_tokens(it, "a1")
                ones_beside_values(it, "a1")
                for i in range(4):
                    rope_s.wait(pool, it, i + 1)
                    nc.gpsimd.tensor_tensor(images(sa[0:96, i % 3, :]), images(sa[0:96, i % 3, :]), turn(w["cos"]),
                                            ALU.mult).then_inc(rope_c.sem, 1)
                    if i % 2:
                        k_h["a1"].wait(pool, it, i // 2 + 1)
                        low(k16[:, 1, i // 2, :], sc[0:96, i % 3, :], k16[:, 0, i // 2, :]).then_inc(k_l["a1"].sem, 1)
                outputs(it, "a1")

                rstd_of_tokens(it, "f1")
                for m in range(MOE_M):
                    m_h.wait(pool, it, m + 1)
                    low(rl[:, m % 3, :], sc[:, m % 3, :], rh[:, m % 3, :]).then_inc(m_l.sem, 1)

            with pool.Fori(0, STEPS) as it:
                body(it)

        @block.scalar
        def _(act):
            def copy(out_, in_, scale=1.0):
                return nc.scalar.activation(out_, in_, ACT.Copy, scale=scale)

            def turned(it, s):
                for k, x in enumerate((xA, xB)):
                    bank = S.wait(act, it, s + "_x", k)
                    copy(x[:, 0, :], bank[:, 0:TT]).then_inc(xh[s].sem, 1)

            def attention(it, s, scale):
                def values_in():
                    for k in range(2):
                        bank = S.wait(act, it, s + "_v", k)
                        for x in range(2):
                            ins = copy(va[:, 2 * k + x, :, :, 0:16],
                                       bank[0:HALF, D * x:D * x + D].rearrange("p (a b d) -> p a b d", a=6, d=16))
                        ins.then_inc(va_in[s].sem, 1)

                def high(i, full):
                    if i % 2:
                        copy(k16[:, 0, i // 2, :], full).then_inc(k_h[s].sem, 1)
                    else:
                        for odd in range(2):
                            nc.scalar.activation(q16[:, 0, i // 2, odd, :], full, ACT.Identity,
                                                 scale=w["parity"][:, odd:odd + 1]).then_inc(q_h[s].sem, 1)

                if s == "a0":
                    for i in range(4):
                        bank = S.wait(act, it, "a0_" + "qk"[i % 2] + str(i // 2), 0)
                        high(i, bank[0:96, 0:TT])
                    values_in()
                else:
                    def with_bias(i):
                        bank = S.wait(act, it, "a1_" + "qk"[i % 2] + str(i // 2), 0)
                        nc.scalar.activation(sa[0:96, i % 3, :], bank[0:96, 0:TT], ACT.Identity,
                                             bias=w["a1qkb"][:, 2 * (i % 2) + i // 2:2 * (i % 2) + i // 2 + 1]
                                             ).then_inc(rope_b.sem, 1)

                    for i in range(3):
                        with_bias(i)
                    for i in range(4):
                        rope_u.wait(act, it, i + 1)
                        high(i, sc[0:96, i % 3, :])
                        if i == 0:
                            with_bias(3)
                        if i == 1:
                            values_in()

                def minus_max(t):
                    bank = S.wait(act, it, f"{s}_mx{t}", 0)
                    copy(m16[0:66, t, :], bank[0:66, 0:TT], scale=-1.0).then_inc(nm[s].sem, 1)

                def outputs_h(g):
                    if s == "a1":
                        a1_bias.wait(act, it, g + 1)
                    else:
                        quot[s].wait(act, it, g + 1)
                    copy(rh[:, g, :], sc[:, g, :]).then_inc(on_h[s].sem, 1)

                for n in range(24):
                    if n in (0, 8):
                        minus_max(n // 8)
                    bank = S.wait(act, it, f"{s}_S2{n // 4}", n % 4)
                    if n >= P:
                        b = (n - P) // 4
                        if b % 2:
                            C.wait(act, it, s + "_pv", b // 2)
                        else:
                            pvs[s].wait(act, it, b // 2 + 1)
                    ins = nc.scalar.activation(probs[:, n % P, :], bank[0:HALF, 0:TT], ACT.Exp, scale=scale)
                    ins.then_inc(exps[s].sem, 1)
                    if n in (15, 23):
                        outputs_h(n // 8 - 1)
                outputs_h(2)

            def body(it):
                turned(it, "a0")
                attention(it, "a0", float(D) ** -0.5)

                turned(it, "f0")

                def values_in(t):
                    for k in range(2):
                        bank = S.wait(act, it, "f0_v", 2 * t + k)
                        copy(vf[:, t, 3 * k:3 * k + 3, 0:3:2, :],
                             bank[0:HALF, 0:384].rearrange("p (a x d) -> p a x d", a=3, d=64)).then_inc(f_v.sem, 1)
                        if k == 1:
                            copy(lg[:, t, :], bank[0:HALF, 384:398]).then_inc(f_v.sem, 1)

                def q_and_k(s):
                    for i in range(6):
                        bank = S.wait(act, it, f"f0_qk{s}", i)
                        tile = 3 * s + i % 3 + (6 if i >= 3 else 0)
                        bias = w["f0qkb"][:, tile:tile + 1]
                        nc.scalar.activation(qc[:, i, :], bank[:, 0:TT], ACT.Identity, bias=bias).then_inc(f_qc.sem, 1)
                        if i >= 3:
                            f_squ.wait(act, it, 5 * s + i - 2)
                        elif s:
                            f_quot.wait(act, it, 2 * i + 2)
                        nc.scalar.activation(sa[:, i % 3, :], bank[:, 0:TT], ACT.Square, bias=bias).then_inc(f_sq.sem, 1)

                q_and_k(0)
                values_in(0)
                for s in range(2):
                    bank = C.wait(act, it, f"f0_var{s}", 0)
                    nc.scalar.activation(qvar, bank[0:12, 0:TT], ACT.Sqrt, bias=eps[0:12, :]).then_inc(f_dev.sem, 1)
                    if s == 0:
                        for t in range(1, NT):
                            values_in(t)
                    f_rs.wait(act, it, s + 1)
                    copy(rowH[0:12, :], qvar).then_inc(f_rsr.sem, 1)
                    if s == 0:
                        f_gate.wait(act, it, 4)
                        nc.scalar.activation(lg[:, :, :], lg[:, :, :], ACT.Exp).then_inc(f_gexp.sem, 1)
                    for k, i in enumerate(BY_PAIR):
                        f_u.wait(act, it, 6 * s + k + 1)
                        dst = qs if i < 3 else ks
                        for x in range(2):
                            copy(dst[0:64, 2 * (i % 3) + x, :], qc[64 * x:64 * x + 64, i, :]).then_inc(f_h.sem, 1)
                        if k >= 3:
                            f_l.wait(act, it, 12 * s + 2 * k - 4)
                        copy(rh[64:128, k % 3, :], qc[64:128, i, :]).then_inc(f_h.sem, 1)
                    bank = S.wait(act, it, f"f0_mx{s}", 0)
                    copy(rowH[0:6, :], bank[0:6, 0:TT], scale=-1.0).then_inc(f_nm.sem, 1)

                    for n in range(12):
                        bank = S.wait(act, it, f"f0_S2{s}", n)
                        if n >= P:
                            C.wait(act, it, f"f0_pv{s}", (n - P) // 2)
                        else:
                            f_l.wait(act, it, 12 * s + 2 * n + 2)
                        nc.scalar.activation(probs[:, BY_PAIR[n % P], :], bank[0:HALF, 0:TT], ACT.Exp, scale=0.125
                                             ).then_inc(f_exp.sem, 1)
                    bank = S.wait(act, it, f"f0_g{s}", 0)
                    copy(rowH[0:12, :], bank[0:12, 0:TT]).then_inc(f_row.sem, 1)
                    if s == 0:
                        q_and_k(1)
                    for i in range(3):
                        f_on.wait(act, it, 3 * s + i + 1)
                        copy(rh[:, i, :], sc[:, i, :]).then_inc(f_onh.sem, 1)

                turned(it, "a1")
                attention(it, "a1", 16.0 ** -0.5)

                turned(it, "f1")
                bank = S.wait(act, it, "f1_r", 0)
                nc.scalar.activation(lg[:, :, 0:8], bank[0:HALF, 0:NT * 8].rearrange("p (t e) -> p t e", e=8),
                                     ACT.Exp, scale=-1.0).then_inc(m_exp.sem, 1)
                bank = S.wait(act, it, "f1_c", 0)
                copy(rowH[0:28, :], bank[0:28, 0:TT]).then_inc(m_row.sem, 1)

                def relu(m):
                    bank_ = S.wait(act, it, f"f1_h{m}", 0)
                    if m >= 3:
                        m_hid.wait(act, it, m - 2)
                    nc.scalar.activation(sa[:, m % 3, :], bank_[:, 0:TT], ACT.Relu).then_inc(m_relu.sem, 1)

                relu(0)
                for m in range(MOE_M):
                    if m + 1 < MOE_M:
                        relu(m + 1)
                    m_hid.wait(act, it, m + 1)
                    if m >= 3:
                        m_used.wait(act, it, m - 2)
                    copy(rh[:, m % 3, :], sc[:, m % 3, :]).then_inc(m_h.sem, 1)

            with act.Fori(0, STEPS) as it:
                body(it)

        @block.vector
        def _(dve):
            tt = nc.vector.tensor_tensor

            def hold(e):
                e.sem_inc(held, 1)

            def low(out_, full, high):
                return tt(out_, full, w32(high), ALU.subtract)

            def normalise(it, s, src):
                for t in range(NT):
                    nc.vector.bn_stats(bnst[:, t, :], src[:, t, :]).then_inc(stats[s].sem, 1)
                for t in range(NT):
                    stats[s].wait(dve, it, t + 1)
                    hold(dve)
                    nc.vector.bn_aggr(bnmv[:, t, :], bnst[:, t, :]).then_inc(stats[s].sem, 1)
                rstds[s].wait(dve, it)
                for t in range(NT):
                    for d0, s0, n in ((0, 0, D), (D, 128, 256 - D)):
                        nc.vector.tensor_scalar(xn[:, t, d0:d0 + n], src[:, t, s0:s0 + n], bnmv[:, t, 0:1],
                                                rstd[:, t:t + 1], ALU.subtract, ALU.mult).then_inc(normed[s].sem, 1)
                for k, x in enumerate((xA, xB)):
                    bank = S.wait(dve, it, s + "_x", k)
                    xh[s].wait(dve, it, k + 1)
                    low(x[:, 1, :], bank[:, 0:TT], x[:, 0, :]).then_inc(xl[s].sem, 1)

            def largest(bank, t0, head, mx=mx):
                return nc.vector.tensor_reduce(mx[:, t0:t0 + 2, head], bank[0:HALF, 0:TT]
                                               .rearrange("p (t k) -> p t k", t=2), AX.X, ALU.max)

            def add_up(it, s, stage, src, n0=0):
                for t in range(NT):
                    bank = C.wait(dve, it, stage, t)
                    tt(h[:, t, :], src[:, t, :], bank[0:HALF, 0:D], ALU.add).then_inc(resid[s].sem, 1)

            def attention(it, s):
                def low_q(m, full):
                    q_h[s].wait(dve, it, 2 * m + 2)
                    for odd in range(2):
                        nc.vector.scalar_tensor_tensor(q16[:, 1, m, odd, :], full, w["parity"][:, odd:odd + 1],
                                                       w32(q16[:, 0, m, odd, :]), ALU.mult, ALU.subtract
                                                       ).then_inc(q_l[s].sem, 1)

                if s == "a0":
                    for m in range(2):
                        bank = S.wait(dve, it, f"a0_q{m}", 0)
                        low_q(m, bank[0:96, 0:TT])
                        bank = S.wait(dve, it, f"a0_k{m}", 0)
                        k_h[s].wait(dve, it, m + 1)
                        low(k16[:, 1, m, :], bank[0:96, 0:TT], k16[:, 0, m, :]).then_inc(k_l[s].sem, 1)
                else:
                    swap = [(i // 16) * 16 + (i + 8) % 16 for i in range(32)]

                    def shuffled(i):
                        rope_b.wait(dve, it, i + 1)
                        hold(dve)
                        nc.vector.stream_shuffle(sc[0:96, i % 3, :], sa[0:96, i % 3, :], swap).then_inc(rope_s.sem, 1)

                    shuffled(0)
                    for i in range(4):
                        tile = sc[0:96, i % 3, :]
                        rope_s.wait(dve, it, i + 1)
                        tt(images(tile), images(tile), turn(w["sin"]), ALU.mult).then_inc(rope_p.sem, 1)
                        if i < 3:
                            shuffled(i + 1)
                        rope_p.wait(dve, it, i + 1)
                        rope_c.wait(dve, it, i + 1)
                        tt(tile, sa[0:96, i % 3, :], tile, ALU.add).then_inc(rope_u.sem, 1)
                        if i % 2 == 0:
                            rope_u.wait(dve, it, i + 1)
                            low_q(i // 2, tile)
                            q_l[s].wait(dve, it, i + 2)
                for n in range(24):
                    bank = S.wait(dve, it, f"{s}_S1{n // 4}", n % 4)
                    t, pair, odd = n // 12, n // 4 % 3, n // 2 % 2
                    largest(bank, 2 * (n % 2), 32 * pair + odd, mx16[t]).then_inc(maxes[s].sem, 1)
                to_all = [16 + i % 16 for i in range(32)]
                for g in range(3):
                    bank = C.wait(dve, it, s + "_pv", g)
                    hold(dve)
                    nc.vector.stream_shuffle(sa[:, g, :], bank[:, 0:TT], to_all).then_inc(dens[s].sem, 1)
                    dens[s].wait(dve, it, 2 * g + 1)
                    nc.vector.reciprocal(sa[:, g, :], sa[:, g, :]).then_inc(dens[s].sem, 1)
                    dens[s].wait(dve, it, 2 * g + 2)
                    tt(sc[:, g, :], bank[:, 0:TT], sa[:, g, :], ALU.mult).then_inc(quot[s].sem, 1)

            def gates(it, n, first):

                def step(ins, last=True, alone=False):
                    n[0] += 1
                    ins.then_inc(f_gate.sem, 1)
                    if last:
                        f_gate.wait(dve, it, n[0])
                    if alone:
                        hold(dve)

                pairs = lg[:, :, 10:14].rearrange("p t (a b) -> p t a b", b=2)
                if first:
                    f_v.wait(dve, it)
                    step(nc.vector.tensor_reduce(gmax[:, :, 0], lg[:, :, 0:10], AX.X, ALU.max), False)
                    step(nc.vector.tensor_reduce(gmax[:, :, 1:3], pairs, AX.X, ALU.max))
                    step(tt(lg[:, :, 0:10], lg[:, :, 0:10], gmax[:, :, 0:1].to_broadcast([HALF, NT, 10]),
                            ALU.subtract), False)
                    step(tt(pairs, pairs, gmax[:, :, 1:3].unsqueeze(3).to_broadcast([HALF, NT, 2, 2]),
                            ALU.subtract))
                    return
                f_gexp.wait(dve, it)
                step(nc.vector.tensor_reduce(gsum[:, :, 0], lg[:, :, 0:10], AX.X, ALU.add), False)
                step(nc.vector.tensor_reduce(gsum[:, :, 1:3], pairs, AX.X, ALU.add))
                step(nc.vector.reciprocal(gsum[:, :, :], gsum[:, :, :]))
                step(tt(lg[:, :, 0:10], lg[:, :, 0:10], gsum[:, :, 0:1].to_broadcast([HALF, NT, 10]),
                        ALU.mult), False)
                step(tt(pairs, pairs, gsum[:, :, 1:3].unsqueeze(3).to_broadcast([HALF, NT, 2, 2]), ALU.mult),
                     alone=True)
                top_two(step, lg, 10)
                step(tt(hot[:, :, :], hot[:, :, :], lg[:, :, 0:10], ALU.mult))
                step(nc.vector.tensor_reduce(gsum[:, :, 0], hot[:, :, :], AX.X, ALU.add))
                step(nc.vector.tensor_scalar(gsum[:, :, 0], gsum[:, :, 0], 2.0 ** -23, None, ALU.max))
                step(nc.vector.reciprocal(gsum[:, :, 0], gsum[:, :, 0]))
                step(tt(hot[:, :, :], hot[:, :, :], gsum[:, :, 0:1].to_broadcast([HALF, NT, 10]), ALU.mult))
                step(nc.vector.scalar_tensor_tensor(gm[:, :, 2:12], hot[:, :, :], 4.0,
                                                    lg[:, :, 11:12].to_broadcast([HALF, NT, 10]),
                                                    ALU.mult, ALU.mult), False)
                step(nc.vector.scalar_tensor_tensor(gm[:, :, 0:2], lg[:, :, 12:14], 4.0,
                                                    lg[:, :, 10:11].to_broadcast([HALF, NT, 2]),
                                                    ALU.mult, ALU.mult), False)
                assert n[0] == f_gate.per, n

            def top_two(step, src, n):
                for t in range(NT):
                    step(nc.vector.max(top8[:, t, :], src[:, t, 0:n]), t == NT - 1, t == NT - 1)
                for t in range(NT):
                    step(nc.vector.max_index(idx8[:, t, :], top8[:, t, :], src[:, t, 0:n]), t == NT - 1)
                step(nc.vector.tensor_copy(idxf[:, :, 0:2], idx8[:, :, 0:2]))
                iota = w["iota"][:, 0:n].unsqueeze(1).to_broadcast([HALF, NT, n])
                for k, dst in enumerate((hot, hot2)):
                    step(tt(dst[:, :, 0:n], iota, idxf[:, :, k:k + 1].to_broadcast([HALF, NT, n]), ALU.is_equal),
                         k == 1)
                step(tt(hot[:, :, 0:n], hot[:, :, 0:n], hot2[:, :, 0:n], ALU.add))

            def router(it):
                n = [0]

                def step(ins, last=True, alone=False):
                    n[0] += 1
                    ins.then_inc(m_gate.sem, 1)
                    if last:
                        m_gate.wait(dve, it, n[0])
                    if alone:
                        hold(dve)

                m_exp.wait(dve, it)
                score = lg[:, :, 0:8]
                step(nc.vector.tensor_scalar(score, score, 1.0, None, ALU.add))
                step(nc.vector.reciprocal(score, score))
                step(tt(hot[:, :, 0:8], score, w["bal"][:, :].unsqueeze(1).to_broadcast([HALF, NT, 8]), ALU.add),
                     alone=True)
                top_two(step, hot, 8)
                step(tt(hot[:, :, 0:8], hot[:, :, 0:8], score, ALU.mult))
                step(nc.vector.tensor_reduce(gsum[:, :, 0], hot[:, :, 0:8], AX.X, ALU.add))
                step(nc.vector.tensor_scalar(gsum[:, :, 0], gsum[:, :, 0], 1e-20, None, ALU.add))
                step(nc.vector.reciprocal(gsum[:, :, 0], gsum[:, :, 0]))
                step(tt(hot[:, :, 0:8], hot[:, :, 0:8], gsum[:, :, 0:1].to_broadcast([HALF, NT, 8]), ALU.mult))
                step(nc.vector.tensor_copy(cm[:, :, 0:24].rearrange("p t (e r) -> p t e r", r=3),
                                           hot[:, :, 0:8].unsqueeze(3).to_broadcast([HALF, NT, 8, 3])), False)
                assert n[0] == m_gate.per, n

            def body(it):
                dve.wait_ge(h_in, 32 * it + 32)
                normalise(it, "a0", hin)
                attention(it, "a0")
                dve.wait_ge(h_out, 16 * it)
                add_up(it, "a0", "a0_out", hin)

                resid["a0"].wait(dve, it)
                normalise(it, "f0", h)
                steps = [0]
                for s in range(2):
                    f_dev.wait(dve, it, s + 1)
                    nc.vector.reciprocal(qvar, qvar).then_inc(f_rs.sem, 1)
                    f_rsr.wait(dve, it, 2 * s + 1)
                    low(rowH[64:76, :], qvar, rowH[0:12, :]).then_inc(f_rsr.sem, 1)
                    if s == 0:
                        gates(it, steps, True)
                    else:
                        add_up(it, "f0", "f0_out0", h)
                    f_qc.wait(dve, it, 6 * s + 6)
                    for k, i in enumerate(BY_PAIR):
                        bank = S.wait(dve, it, f"f0_rs{s}", k)
                        tt(qc[:, i, :], qc[:, i, :], bank[:, 0:TT], ALU.mult).then_inc(f_t.sem, 1)
                        f_t.wait(dve, it, 6 * s + k + 1)
                        c = 2 * (i // 3)
                        nc.vector.tensor_scalar(qc[:, i, :], qc[:, i, :], w["f0n"][:, c:c + 1],
                                                w["f0n"][:, c + 1:c + 2], ALU.mult, ALU.add).then_inc(f_u.sem, 1)
                    if s == 0:
                        gates(it, steps, False)
                    for n in range(12):
                        bank = S.wait(dve, it, f"f0_S1{s}", n)
                        largest(bank, 2 * (n % 2), 6 * s + n // 2).then_inc(f_max.sem, 1)
                    for hd in range(6):
                        x, i = hd % 2, hd // 2
                        bank = C.wait(dve, it, f"f0_pv{s}", hd)
                        r, other = slice(64 * x, 64 * x + 64), slice(64 - 64 * x, 128 - 64 * x)
                        nc.vector.reciprocal(sa[r, i, :], bank[other, 0:TT]).then_inc(f_den.sem, 1)
                        f_den.wait(dve, it, 6 * s + hd + 1)
                        tt(sc[r, i, :], bank[r, 0:TT], sa[r, i, :], ALU.mult).then_inc(f_quot.sem, 1)
                    bank = S.wait(dve, it, f"f0_g{s}", 0)
                    f_row.wait(dve, it, 2 * s + 1)
                    low(rowH[64:76, :], bank[0:12, 0:TT], rowH[0:12, :]).then_inc(f_row.sem, 1)
                    f_quot.wait(dve, it, 6 * s + 6)
                    for i in range(3):
                        bank = S.wait(dve, it, f"f0_gb{s}", i)
                        nc.vector.scalar_tensor_tensor(sc[:, i, :], sc[:, i, :], w["f0vb"][:, 3 * s + i:3 * s + i + 1],
                                                       bank[:, 0:TT], ALU.add, ALU.mult).then_inc(f_on.sem, 1)
                    if s == 0:
                        h_bias.wait(dve, it)
                resid["f0"].wait(dve, it, 4)
                add_up(it, "f0", "f0_out1", h)

                resid["f0"].wait(dve, it)
                normalise(it, "a1", h)
                attention(it, "a1")
                add_up(it, "a1", "a1_out", h)

                resid["a1"].wait(dve, it)
                normalise(it, "f1", h)
                router(it)
                bank = S.wait(dve, it, "f1_c", 0)
                m_row.wait(dve, it, 1)
                low(rowH[64:92, :], bank[0:28, 0:TT], rowH[0:28, :]).then_inc(m_row.sem, 1)
                for m in range(MOE_M):
                    bank = S.wait(dve, it, f"f1_cb{m}", 0)
                    m_relu.wait(dve, it, m + 1)
                    if m >= 3:
                        m_l.wait(dve, it, m - 2)
                    tt(sc[:, m % 3, :], sa[:, m % 3, :], bank[:, 0:TT], ALU.mult).then_inc(m_c.sem, 1)
                    m_c.wait(dve, it, m + 1)
                    tt(sc[:, m % 3, :], sc[:, m % 3, :], sa[:, m % 3, :], ALU.mult).then_inc(m_hid.sem, 1)
                add_up(it, "f1", "f1_y", h)

            dve.wait_ge(ready, NREADY)
            with dve.Fori(0, STEPS) as it:
                body(it)

        @block.tensor
        def _(pe):
            def mm(out_, lhs, rhs, first, last):
                return nc.tensor.matmul(out_, lhs, rhs, start=first, stop=last, skip_group_check=True)

            def features(out_, c0, n=128):
                c = slice(c0, c0 + n)
                mm(out_, w["A"][:, c], xA[:, 0, :], True, False)
                mm(out_, w["A"][:, c], xA[:, 1, :], False, False)
                mm(out_, w["Al"][:, c], xA[:, 0, :], False, False)
                mm(out_, w["B"][:, c], xB[:, 0, :], False, False)
                return mm(out_, w["B"][:, c], xB[:, 1, :], False, True)

            def rows(out_, t, c0, n):
                c = slice(c0, c0 + n)
                mm(out_, xA[:, 0, tok(t)], w["A"][:, c], True, False)
                mm(out_, xA[:, 0, tok(t)], w["Al"][:, c], False, False)
                mm(out_, xA[:, 1, tok(t)], w["A"][:, c], False, False)
                mm(out_, xB[:, 0, tok(t)], w["B"][:, c], False, False)
                return mm(out_, xB[:, 1, tok(t)], w["B"][:, c], False, True)

            def turn_tokens(it, s):
                normed[s].wait(pe, it)
                for k in range(2):
                    bank = S.claim(pe, it, s + "_x", k)
                    for t in range(NT):
                        last = nc.tensor.transpose(bank[:, tok(t)], xn[:, t, 128 * k:128 * k + 128],
                                                   ident[0:HALF, 0:HALF])
                    S.fill(last)

            def turn_rows(it, stage, src, n):
                bank = S.claim(pe, it, stage, 0)
                for t in range(NT):
                    last = nc.tensor.transpose(bank[0:n, tok(t)], src[:, t, :], ident[0:HALF, 0:HALF])
                S.fill(last)

            def project(it, stage, group, n, h_sig, h_of):
                for t in range(NT):
                    bank = C.claim(pe, it, stage, t)[0:HALF, 0:D]
                    for g in range(n):
                        if t == 0:
                            h_sig.wait(pe, it, h_of(g))
                        c = slice((group + g) * D, (group + g + 1) * D)
                        mm(bank, rh[:, g, tok(t)], w["Kh"][:, c], g == 0, False)
                        mm(bank, rh[:, g, tok(t)], w["Kl"][:, c], False, False)
                        last = mm(bank, rl[:, g, tok(t)], w["Kh"][:, c], False, g == n - 1)
                    C.fill(last)

            def attention(it, s, c_qk, c_v, group):
                turn_tokens(it, s)
                xl[s].wait(pe, it)
                for m in range(2):
                    for k in range(2):
                        bank = S.claim(pe, it, f"{s}_" + "qk"[k] + str(m), 0)
                        S.fill(features(bank[0:96, 0:TT], c_qk + D * k + 96 * m, 96))
                for k in range(2):
                    bank = S.claim(pe, it, s + "_v", k)
                    for x in range(2):
                        last = rows(bank[0:HALF, D * x:D * x + D], 2 * k + x, c_v, D)
                    S.fill(last)

                def largest_of(n):
                    if n % 3 == 0:
                        q_h[s].wait(pe, it, 2 * (n // 3) + 2)
                        k_h[s].wait(pe, it, n // 3 + 1)
                    for i in range(4):
                        odd, im = i // 2, i % 2
                        r = slice(32 * (n % 3), 32 * (n % 3) + 32)
                        bank = S.claim(pe, it, f"{s}_S1{n}", i)
                        for x in range(2):
                            last = mm(bank[0:HALF, TOK * x:TOK * x + TOK], q16[r, 0, n // 3, odd, tok(2 * im + x)],
                                      k16[r, 0, n // 3, img(im)], True, True)
                        S.fill(last)

                def minus_max(t):
                    maxes[s].wait(pe, it, 12 * t + 12)
                    turn_rows(it, f"{s}_mx{t}", mx16[t], 66)

                def scores(b):
                    g, im = b // 2, b % 2
                    if im == 0:
                        q_l[s].wait(pe, it, 2 if g == 0 else 4)
                        k_l[s].wait(pe, it, 1 if g == 0 else 2)
                        nm[s].wait(pe, it, 1 if g == 0 else 2)
                    for j in range(4):
                        t, pair, odd = (4 * g + j) // 6, (4 * g + j) % 6 // 2, j % 2
                        r, m, row = slice(32 * pair, 32 * pair + 32), slice(32 * pair, 32 * pair + 2), 32 * pair + odd
                        bank = S.claim(pe, it, f"{s}_S2{b}", j)
                        for x in range(2):
                            o = bank[0:HALF, TOK * x:TOK * x + TOK]
                            mm(o, k16[r, 0, t, tok(2 * im + x)], q16[r, 0, t, odd, img(im)], True, False)
                            mm(o, k16[r, 0, t, tok(2 * im + x)], q16[r, 1, t, odd, img(im)], False, False)
                            mm(o, k16[r, 1, t, tok(2 * im + x)], q16[r, 0, t, odd, img(im)], False, False)
                            last = mm(o, eye[m, row:row + 1].to_broadcast([2, HALF]), m16[m, t, img(im)], False, True)
                        S.fill(last)

                def values(b):
                    g, im = b // 2, b % 2
                    if im == 0:
                        C.claim(pe, it, s + "_pv", g)
                    bank = C.banks[(C.first[s + "_pv"] + g) % 4]
                    va_in[s].wait(pe, it)
                    ones[s].wait(pe, it)
                    exps[s].wait(pe, it, 4 * b + 4)
                    for x in range(2):
                        for j in range(4):
                            last = mm(bank[32 * j:32 * j + 32, img(im)], va[:, 2 * im + x, 2 * g + j // 2, j % 2, :],
                                      probs[:, (4 * b + j) % P, TOK * x:TOK * x + TOK], x == 0, x == 1)
                    if im:
                        C.fill(last)
                    else:
                        last.then_inc(pvs[s].sem, 1)

                for stage, n in S1_S2:
                    if stage == "S1":
                        largest_of(n)
                    elif stage == "mx":
                        minus_max(n)
                    else:
                        scores(n)
                        if n:
                            values(n - 1)
                values(5)
                project(it, s + "_out", group, 3, on_l[s], lambda g: g + 1)

            def body(it):
                attention(it, "a0", C_A0QK, C_A0QK + D, K_O0)

                turn_tokens(it, "f0")
                xl["f0"].wait(pe, it)

                def values_of(t):
                    for k, (c, n) in enumerate(((C_F0V, NV0), (C_F0V + NV0, NV1))):
                        bank = S.claim(pe, it, "f0_v", 2 * t + k)
                        S.fill(rows(bank[0:HALF, 0:n], t, c, n))

                def variance(s, i):
                    if i == 0:
                        C.claim(pe, it, f"f0_var{s}", 0)
                    bank = C.banks[C.first[f"f0_var{s}"] % 4]
                    f_sq.wait(pe, it, 6 * s + i + 1)
                    last = mm(bank[0:12, 0:TT], sumcol[:, 10 - 2 * i:22 - 2 * i], sa[:, i % 3, :], i == 0, i == 5)
                    if i < 5:
                        last.then_inc(f_squ.sem, 1)
                    else:
                        C.fill(last)

                def q_and_k(s):
                    for i in range(6):
                        tile = 3 * s + i % 3 + (6 if i >= 3 else 0)
                        bank = S.claim(pe, it, f"f0_qk{s}", i)
                        S.fill(features(bank[:, 0:TT], C_F0QK + 128 * tile))
                        if i >= 2:
                            variance(s, i - 2)

                q_and_k(0)
                values_of(0)
                variance(0, 4)
                variance(0, 5)
                for t in range(1, NT):
                    values_of(t)
                row64.wait(pe, it)
                for s in range(2):
                    f_rsr.wait(pe, it, 2 * s + 2)
                    for k, i in enumerate(BY_PAIR):
                        bank = S.claim(pe, it, f"f0_rs{s}", k)
                        S.fill(mm(bank[:, 0:TT], sel[:, i, :], rowH[:, :], True, True))
                    for n in range(12):
                        head, im = n // 2, n % 2
                        f_h.wait(pe, it, 18 * s + 6 * (head // 2) + 6)
                        bank = S.claim(pe, it, f"f0_S1{s}", n)
                        for x in range(2):
                            last = mm(bank[0:HALF, TOK * x:TOK * x + TOK], qs[0:65, head, tok(2 * im + x)],
                                      ks[0:65, head, img(im)], True, True)
                        S.fill(last)
                    f_max.wait(pe, it, 12 * s + 12)
                    turn_rows(it, f"f0_mx{s}", mx[:, :, 6 * s:6 * s + 6], 6)
                    f_nm.wait(pe, it, s + 1)

                    def scores(hd):
                        f_l.wait(pe, it, 12 * s + 4 * (hd // 2) + 4)
                        for im in range(IMS):
                            bank = S.claim(pe, it, f"f0_S2{s}", 2 * hd + im)
                            for x in range(2):
                                o = bank[0:HALF, TOK * x:TOK * x + TOK]
                                keys = tok(2 * im + x)
                                mm(o, ks[0:65, hd, keys], qs[0:65, hd, img(im)], True, False)
                                mm(o, ks[0:65, hd, keys], qs[0:65, 6 + hd, img(im)], False, False)
                                mm(o, ks[0:65, 6 + hd, keys], qs[0:65, hd, img(im)], False, False)
                                last = mm(o, eye[0:76, hd:hd + 1].to_broadcast([76, HALF]), rowH[0:76, img(im)],
                                          False, True)
                            S.fill(last)

                    def values(hd):
                        head = 6 * s + hd
                        bank = C.claim(pe, it, f"f0_pv{s}", hd)
                        f_exp.wait(pe, it, 12 * s + 2 * hd + 2)
                        block_ = slice(0, 2) if head % 2 == 0 else slice(1, 3)
                        for im in range(IMS):
                            for x in range(2):
                                v = vf[:, 2 * im + x, head // 2, block_, :].rearrange("p a d -> p (a d)")
                                last = mm(bank[:, img(im)], v,
                                          probs[:, BY_PAIR[(2 * hd + im) % P], TOK * x:TOK * x + TOK], x == 0, x == 1)
                        C.fill(last)

                    scores(0)
                    for hd in range(1, 6):
                        scores(hd)
                        values(hd - 1)
                    values(5)
                    f_gate.wait(pe, it)
                    turn_rows(it, f"f0_g{s}", gm, NH)
                    if s == 0:
                        q_and_k(1)
                    f_row.wait(pe, it, 2 * s + 2)
                    for i in range(3):
                        bank = S.claim(pe, it, f"f0_gb{s}", i)
                        S.fill(mm(bank[:, 0:TT], sel[:, 3 * s + i, :], rowH[:, :], True, True))
                    if s == 0:
                        variance(1, 4)
                        variance(1, 5)
                    project(it, f"f0_out{s}", K_PJ + 3 * s, 3, f_onl, lambda g: 3 * s + g + 1)

                attention(it, "a1", C_A1QK, C_A1V, K_O1)

                turn_tokens(it, "f1")
                xl["f1"].wait(pe, it)
                bank = S.claim(pe, it, "f1_r", 0)
                for t in range(NT):
                    last = rows(bank[0:HALF, 8 * t:8 * t + 8], t, C_RT, 8)
                S.fill(last)
                m_gate.wait(pe, it)
                turn_rows(it, "f1_c", cm, 28)
                m_row.wait(pe, it, 2)

                def hidden(m):
                    bank_ = S.claim(pe, it, f"f1_h{m}", 0)
                    S.fill(features(bank_[:, 0:TT], C_W1 + 128 * m))
                    bank_ = S.claim(pe, it, f"f1_cb{m}", 0)
                    S.fill(mm(bank_[:, 0:TT], sel[:, m, :], rowH[:, :], True, True))

                def outward(m):
                    m_l.wait(pe, it, m + 1)
                    c = slice((K_W2 + m) * D, (K_W2 + m + 1) * D)
                    for t in range(NT):
                        b = C.claim(pe, it, "f1_y", t) if m == 0 else C.banks[(C.first["f1_y"] + t) % 4]
                        o = b[0:HALF, 0:D]
                        mm(o, rh[:, m % 3, tok(t)], w["Kh"][:, c], m == 0, False)
                        mm(o, rh[:, m % 3, tok(t)], w["Kl"][:, c], False, False)
                        last = mm(o, rl[:, m % 3, tok(t)], w["Kh"][:, c], False, m == MOE_M - 1)
                        if m == MOE_M - 1:
                            C.fill(last)
                    if m < MOE_M - 1:
                        last.then_inc(m_used.sem, 1)

                hidden(0)
                hidden(1)
                for m in range(MOE_M):
                    if m + 2 < MOE_M:
                        hidden(m + 2)
                    outward(m)

            pe.wait_ge(ready, NREADY)
            with pe.Fori(0, STEPS) as it:
                body(it)


def vit_tower(nc, a, out):
    h0 = nc.dram_tensor("patch_tokens", (TOK * IMAGES, D), F32).ap()
    with ExitStack() as ctx:
        def sb(name, shape, dt=F32):
            return ctx.enter_context(nc.sbuf_tensor(name, shape, dt))

        w = {
            "A": sb("wA", [128, NCOL], F32R), "Al": sb("wAl", [128, NCOL], F32R), "B": sb("wB", [128, NCOL], F32R),
            "Kh": sb("wKh", [128, NK * D], F32R), "Kl": sb("wKl", [128, NK * D], F32R),
            "sel": sb("sel", [SELROWS, MOE_M, 128], F32R), "sumcol": sb("sumcol", [128, 22]),
            "ident": sb("ident", [128, 128]), "cos": sb("cos", [128, TOK]), "sin": sb("sin", [128, TOK]),
            "eye": sb("eye", [128, 72], F32R), "parity": sb("parity", [96, 2]), "a1qkb": sb("a1qkb", [96, 4]), "f0n": sb("f0n", [128, 4]), "f0vb": sb("f0vb", [128, 6]),
            "f0qkb": sb("f0qkb", [128, 12]), "a1vb": sb("a1vb", [128, 3]), "f0pb": sb("f0pb", [HALF, D]),
            "bal": sb("bal", [HALF, 8]), "iota": sb("iota", [HALF, 10]),
        }
        setup_and_patches(nc, a, w, h0)
        layers(nc, a, w, h0, out)


def constants():
    import numpy as np

    p = np.arange(128)
    sel = np.zeros((SELROWS, MOE_M, 128), np.float32)
    for m in range(MOE_M):
        for half in range(2):
            for part in (0, 64):
                sel[part + 2 * m + half, m, 64 * half:64 * half + 64] = 1.0
    sumcol = np.zeros((128, 22), np.float32)
    sumcol[:64, 10] = sumcol[64:, 11] = 1.0 / 64
    position = np.array([i * GRID + j for i, j in token_classes()[1]], np.float32)
    inv = (1.0 / np.float32(10000.0) ** (np.arange(0, 16, 2, dtype=np.float32) / np.float32(16))).astype(np.float32)
    angle = inv[p % 8][:, None] * position[None, :]
    sign = np.where(p % 16 < 8, -1.0, 1.0).astype(np.float32)[:, None]
    return {
        "blockmean": ((p[:, None] // 64 == p[None, :] // 64) / 64).astype(np.float32),
        "sel": sel.reshape(SELROWS, -1), "sumcol": sumcol, "ident": np.eye(128, dtype=np.float32),
        "cos": np.cos(angle).astype(np.float32), "sin": (np.sin(angle) * sign).astype(np.float32),
        "parity": np.stack([p % 32 < 16, p % 32 >= 16], 1)[:96].astype(np.float32),
        "iota": np.tile(np.arange(10, dtype=np.float32), (HALF, 1)),
    }


def lay_out(x, i):
    import numpy as np

    f = {k: np.asarray(v) for k, v in i.items()}
    x = np.asarray(x).reshape(IMAGES, GRID, 2, 8, GRID, 2, 8, 3)
    x = x.transpose(1, 4, 2, 5, 3, 6, 7, 0).reshape(GRID, GRID, 768, IMAGES)
    cls, _ = token_classes()
    tiles = []
    for c in cls:
        for n in range(0, len(c), 2):
            two = [x[i_, j] for i_, j in c[n:n + 2]]
            if len(two) == 1:
                two.append(np.zeros_like(two[0]))
            t = np.concatenate(two, axis=1)
            tiles.append(t.reshape(KC, 128, 128).transpose(1, 0, 2).reshape(128, KC * 128))
    tokW = f["L0_tok_W"].reshape(2, 8, 2, 8, 5, 3, D).transpose(4, 0, 2, 1, 3, 5, 6).reshape(5, KC, 128, D)

    def first(wt):
        return wt[:128]

    def rest(wt):
        return np.concatenate([wt[128:D], wt[128:D]], 0)

    w1 = np.concatenate(list(f["L1_ffn_w1"]) + [f["L1_ffn_w_fc_sh"], np.zeros((D, 64), np.float32)], 1)
    cols = np.concatenate([
        f["L0_attn_w_qkv"][:, :2 * D], f["L1_attn_w_qkv"].T, f["L0_ffn_qkv_w"],
        f["L0_ffn_wg_w"], f["L0_ffn_wg0_w"], f["L0_ffn_wg1_w"], f["L1_ffn_router_w"].T, w1], 1)
    assert cols.shape[1] == NCOL

    def spread(wo, bias=None):
        g = np.zeros((3, 4, 32, D), np.float32)
        g[:, :, :16] = wo.reshape(3, 4, 16, D)
        if bias is not None:
            g[0, 0, 16] = bias
        return g.reshape(3, 128, D)

    w2 = np.concatenate([f["L1_ffn_w2"].reshape(-1, D), f["L1_ffn_w_proj_sh"], np.zeros((64, D), np.float32)], 0)
    groups = np.concatenate([
        w2.reshape(MOE_M, 128, D), f["L0_ffn_proj_w"].reshape(6, 128, D), spread(f["L0_attn_w_out"]),
        spread(f["L1_attn_w_proj"].T, f["L1_attn_b_proj"])], 0)

    def per_head(b):
        g = np.zeros((3, 4, 32), np.float32)
        g[:, :, :16] = b.reshape(3, 4, 16)
        return g.reshape(3, 128).T

    a1b, f0b = f["L1_attn_b_qkv"], f["L0_ffn_qkv_b"]
    norm = [np.tile(f[f"L0_ffn_{k}"], 2) for k in ("q_norm_w", "q_norm_b", "k_norm_w", "k_norm_b")]
    return {
        "px": np.stack(tiles), "tokW": tokW.transpose(2, 0, 1, 3), "tokb": np.tile(f["L0_tok_b"], (128, 1)),
        "WA": first(cols), "WB": rest(cols), "WK": groups.transpose(1, 0, 2).reshape(128, NK * D),
        "qkb": f0b[:2 * 768].reshape(12, 128).T, "a1qkb": a1b[:2 * D].reshape(4, 96).T,
        "f0n": np.stack(norm, 1), "f0vb": f0b[2 * 768:].reshape(6, 128).T, "a1vb": per_head(a1b[2 * D:]),
        "f0pb": np.tile(f["L0_ffn_proj_b"], (HALF, 1)), "bal": np.tile(f["L1_ffn_balance_bias"], (HALF, 1)),
    }


def kernel(x, **inputs):
    import concourse.bacc as bacc
    import numpy as np
    from concourse.bass_utils import run_bass_kernel_spmd

    arrays = {**lay_out(x, inputs), **constants()}
    arrays = {"in_" + k: np.ascontiguousarray(v) for k, v in arrays.items()}
    nc = bacc.Bacc("TRN2", target_bir_lowering=False, num_devices=1)
    a = {k[3:]: nc.dram_tensor(k, v.shape, F32, kind="ExternalInput").ap() for k, v in arrays.items()}
    out = nc.dram_tensor("out", (IMAGES // IMS, HALF, NT, D), F32, kind="ExternalOutput").ap()
    vit_tower(nc, a, out)
    got = run_bass_kernel_spmd(nc, [arrays], core_ids=[0]).results[0]["out"]
    slots = got.reshape(-1, HALF, IMS, 2, D).transpose(0, 2, 3, 1, 4).reshape(IMAGES, TOK, D)
    at = [i * GRID + j for i, j in token_classes()[1]]
    full = np.empty_like(slots)
    full[:, at] = slots
    return full
```

```python
from contextlib import ExitStack

import concourse.bass as bass
from concourse import mybir

F32 = mybir.dt.float32
F32R = mybir.dt.float32r
U32 = mybir.dt.uint32
ALU = mybir.AluOpType
ACT = mybir.ActivationFunctionType
AX = mybir.AxisListType

IMAGES = 64
STEPS = 32
D = 192
TOK = 196
HALF = 98
IMS = 2
TT = IMS * TOK
NT = TT // HALF
NH = 12
EPS = 1e-5
GRID = 14
KC = 6

CLASSES = [("mid", "mid"), ("first", "mid"), ("last", "mid"), ("mid", "first"), ("mid", "last"),
           ("first", "first"), ("first", "last"), ("last", "first"), ("last", "last")]
MID_TILES = 72

C_A0QK, C_A1QK, C_A1V, C_F0QK = 0, 384, 768, 960
C_F0V = C_F0QK + 2 * NH * 64
NV0, NV1 = 384, 398
C_RT = C_F0V + NV0 + NV1
C_W1 = C_RT + 8
MOE_M = 14
NCOL = C_W1 + MOE_M * 128
K_W2, K_PJ, K_O0, K_O1 = 0, 14, 20, 23
NK = 26
SELROWS = 128


def token_classes():
    span = {"first": [0], "mid": list(range(1, GRID - 1)), "last": [GRID - 1]}
    cls = [[(i, j) for i in span[r] for j in span[c]] for r, c in CLASSES]
    return cls, sum(cls, [])


def edge_tiles():
    return [c for c in (1, 2, 3, 4) for k in range(6)] + [5, 6, 7, 8]


def crop_rows(c, k):
    r, q = CLASSES[c]
    quadrants = [[(0, 128, 0, 1), (0, 64, 1, 2)], [(64, 128, 1, 2), (0, 128, 2, 3)],
                 [(0, 128, 3, 4), (0, 64, 4, 5)], [(64, 128, 4, 5), (0, 128, 5, 6)]]
    kept = []
    for n, parts in enumerate(quadrants):
        low, right = n // 2, n % 2
        rows = not (low and r == "last") if k in (1, 3) else not (not low and r == "first")
        cols = not (right and q == "last") if k in (1, 2) else not (not right and q == "first")
        if rows and cols:
            kept += parts
    return [(0, 128, 0, KC)] if len(kept) == 8 else kept


def w32(ap):
    return ap.bitcast(F32)


class Signal:

    def __init__(self, sem, per, base=0, own=None):
        self.sem, self.per, self.base, self.own = sem, per, base, per if own is None else own

    def wait(self, e, it, k=None):
        e.wait_ge(self.sem, it * self.per + (self.base + (self.own if k is None else k)))


def before_all(it):
    return isinstance(it, int) and it < 0


class Banks:

    def __init__(self, banks, filled, stages, before=0):
        self.banks, self.filled, self.before = banks, filled, before
        self.first, self.readers = {}, []
        for name, n, signal, count in stages:
            self.first[name] = len(self.readers)
            self.readers += [(signal, count(k)) for k in range(n)]
        self.total = len(self.readers)

    def claim(self, pe, it, stage, k):
        n = self.first[stage] + k
        if n >= len(self.banks) and not before_all(it):
            signal, count = self.readers[n - len(self.banks)]
            signal.wait(pe, it, count)
        return self.banks[n % len(self.banks)]

    def fill(self, ins):
        ins.then_inc(self.filled, 1)

    def wait(self, e, it, stage, k):
        e.wait_ge(self.filled, it * self.total + (self.before + self.first[stage] + k + 1))
        return self.banks[(self.first[stage] + k) % len(self.banks)]


def setup_and_patches(nc, a, w, h0):
    with ExitStack() as ctx:
        def sb(name, shape, dt=F32):
            return ctx.enter_context(nc.sbuf_tensor(name, shape, dt))

        def sem(name):
            return ctx.enter_context(nc.semaphore(name))

        cuts = [0, 480, C_F0QK, C_F0QK + 768, C_F0V, C_RT, C_RT + 776, C_RT + 1544, NCOL]
        blocks = [("cols", c0, c1) for c0, c1 in zip(cuts, cuts[1:])]
        blocks += [("groups", g, min(g + 4, NK)) for g in range(0, NK, 4)]
        is_qk = [k == "cols" and C_F0QK <= c0 < C_F0V for k, c0, c1 in blocks]

        stage = sb("stage", [128, 2, 2, 784])
        headsum = sb("headsum", [128, 2, 12])
        wtok = sb("wtok", [128, 5, KC, D])
        weff = sb("weff", [128, KC, D])
        weffH = sb("weffH", [128, 2, KC, D], F32R)
        weffL = sb("weffL", [128, 2, KC, D], F32R)
        tokb = sb("tokb", [128, D])
        blockmean = sb("blockmean", [128, 128])
        qkb_in = sb("qkb_in", [128, 12])
        sel_in = sb("sel_in", [SELROWS, MOE_M * 128])
        px = sb("px", [128, 4, KC * 128])
        pxH = sb("pxH", [128, 2, KC * 128], F32R)
        pxL = sb("pxL", [128, 2, KC * 128], F32R)
        tok = sb("tok", [128, 2, D])
        ps = [ctx.enter_context(nc.psum_tensor(f"ps_tok{i}", [128, 512], F32)) for i in range(2)]
        ps_mean = ctx.enter_context(nc.psum_tensor("ps_mean", [128, 512], F32))

        wtok_in = sem("wtok_in")
        const_in = sem("const_in")
        stage_in = [sem("stage_in0"), sem("stage_in1")]
        centred = sem("centred")
        split_h = sem("split_h")
        split_l = sem("split_l")
        meaned = sem("meaned")
        small = sem("small")
        summed = sem("summed")
        weff_h = sem("weff_h")
        weff_l = sem("weff_l")
        px_in = [sem(f"px_in{i}") for i in range(4)]
        px_h = sem("px_h")
        px_l = sem("px_l")
        tok_ps = sem("tok_ps")
        tok_sb = sem("tok_sb")
        tok_out = [sem("tok_out0"), sem("tok_out1")]

        edges = edge_tiles()
        total = MID_TILES + len(edges)
        WHOLE = total - 4
        first_of = {c: MID_TILES + edges.index(c) for c in range(1, 9)}
        first_of[0] = 0
        ends, s = [], 0
        for c in range(len(CLASSES)):
            s += 1 + sum(len(crop_rows(c, k)) for k in range(1, 5))
            ends.append(s)

        block = ctx.enter_context(nc.Block())

        def since(e, sem_, v):
            if not isinstance(v, int) or v > 0:
                e.wait_ge(sem_, v)

        def all_tiles(e, body):
            for u in range(4):
                body(u, u)
            with e.Fori(1, MID_TILES // 4) as r:
                for u in range(4):
                    body(4 * r + u, u)
            for t in range(MID_TILES, total):
                body(t, t % 4)

        def rounds(t, u):
            return 4 * (t - u) + 16 if not isinstance(t, int) else 16 * (t // 4 + 1)

        @block.sync
        def _(sp):
            sp.dma_start(wtok[:, :, :, :], a["tokW"]).then_inc(wtok_in, 16)
            sp.dma_start(tokb[:, :], a["tokb"]).then_inc(wtok_in, 16)
            for t in range(4):
                sp.dma_start(px[:, t, :], a["px"][t]).then_inc(px_in[t], 16)
            for dst, name in ((blockmean, "blockmean"), (qkb_in, "qkb"), (sel_in, "sel"), (w["ident"], "ident"),
                              (w["sumcol"], "sumcol"), (w["cos"], "cos"), (w["sin"], "sin"),
                              (w["a1qkb"], "a1qkb"), (w["f0n"], "f0n"), (w["f0vb"], "f0vb"),
                              (w["a1vb"], "a1vb"), (w["f0pb"], "f0pb"), (w["bal"], "bal"), (w["iota"], "iota"),
                              (w["own"], "own")):
                sp.dma_start(dst[:, :], a[name]).then_inc(const_in, 16)

            def load(t, u):
                sp.wait_ge(px_l, t - 3)
                sp.dma_start(px[:, u, :], a["px"][bass.ds(t, 1), :, :].rearrange("o p n -> (o p) n")
                             ).then_inc(px_in[u], 16)

            def store(t, u, rows):
                sp.wait_ge(tok_sb, t + 1)
                sp.dma_start(h0[bass.ds(128 * t if rows == 128 else 128 * WHOLE + 64 * (t - WHOLE), rows), :],
                             tok[0:rows, u % 2, :]).then_inc(tok_out[u % 2], 16)

            with sp.Fori(1, MID_TILES // 4) as r:
                for u in range(4):
                    load(4 * r + u, u)
                    store(4 * r + (u - 4), u, 128)
            for t in range(MID_TILES, total + 4):
                if t < total:
                    load(t, t % 4)
                store(t - 4, t % 4, 128 if t - 4 < WHOLE else 64)
            for u in range(2):
                sp.wait_ge(tok_out[u], 16 * (total // 2))
            sp.wait_ge(const_in, 16 * 15)

        @block.gpsimd
        def _(pool):
            def stage_block(i):
                if i < len(blocks):
                    kind, c0, c1 = blocks[i]
                    if kind == "cols":
                        for part, name in enumerate(("WA", "WB")):
                            pool.dma_start(stage[:, i % 2, part, 0:c1 - c0], a[name][:, c0:c1]
                                           ).then_inc(stage_in[i % 2], 16)
                    else:
                        pool.dma_start(stage[:, i % 2, 0, 0:(c1 - c0) * D], a["WK"][:, c0 * D:c1 * D]
                                       ).then_inc(stage_in[i % 2], 16)

            def class_weights(c):
                n = ends[c - 1] if c else 0
                if c:
                    pool.wait_ge(weff_h, c)
                    pool.wait_ge(weff_l, c)
                nc.gpsimd.tensor_copy(weff[:, :, :], wtok[:, 0, :, :]).then_inc(summed, 1)
                n += 1
                for k in range(1, 5):
                    for p0, p1, k0, k1 in crop_rows(c, k):
                        pool.wait_ge(summed, n)
                        nc.gpsimd.tensor_tensor(weff[p0:p1, k0:k1, :], weff[p0:p1, k0:k1, :],
                                                wtok[p0:p1, k, k0:k1, :], ALU.add).then_inc(summed, 1)
                        n += 1
                pool.wait_ge(weff_h, c + 1)
                nc.gpsimd.tensor_tensor(weffL[:, c % 2, :, :], weff[:, :, :],
                                        w32(weffH[:, c % 2, :, :]), ALU.subtract).then_inc(weff_l, 1)

            stage_block(0)
            stage_block(1)
            pool.wait_ge(wtok_in, 32)
            class_weights(0)
            for i, (kind, c0, c1) in enumerate(blocks):
                pool.wait_ge(split_h, i + 1)
                if kind == "cols":
                    n = c1 - c0
                    nc.gpsimd.tensor_tensor(w["Al"][:, c0:c1], stage[:, i % 2, 0, 0:n],
                                            w32(w["A"][:, c0:c1]), ALU.subtract).then_inc(split_l, 1)
                    pool.wait_ge(split_l, 2 * i + 1)
                    nc.gpsimd.tensor_tensor(w["B"][64:128, c0:c1], stage[64:128, i % 2, 1, 0:n],
                                            w32(w["B"][64:128, c0:c1]), ALU.subtract).then_inc(split_l, 1)
                else:
                    n = (c1 - c0) * D
                    nc.gpsimd.tensor_tensor(w["Kl"][:, c0 * D:c1 * D], stage[:, i % 2, 0, 0:n],
                                            w32(w["Kh"][:, c0 * D:c1 * D]), ALU.subtract).then_inc(split_l, 2)
                pool.wait_ge(split_l, 2 * i + 2)
                stage_block(i + 2)
            for c in range(1, len(CLASSES)):
                class_weights(c)

        @block.scalar
        def _(act):
            def weights_h(c):
                act.wait_ge(summed, ends[c])
                if c >= 2:
                    act.wait_ge(tok_ps, first_of[c - 1])
                nc.scalar.copy(weffH[:, c % 2, :, :], weff[:, :, :]).then_inc(weff_h, 1)

            def pixels_h(t, u):
                if isinstance(t, int) and t >= MID_TILES and t - 1 in [first_of[c] for c in range(1, 8)]:
                    weights_h(1 + [first_of[c] for c in range(1, 9)].index(t - 1) + 1)
                act.wait_ge(px_in[u], rounds(t, u))
                since(act, tok_ps, t - 1)
                nc.scalar.copy(pxH[:, u % 2, :], px[:, u, :]).then_inc(px_h, 1)

            weights_h(0)
            for i, (kind, c0, c1) in enumerate(blocks):
                if kind == "cols":
                    act.wait_ge(stage_in[i % 2], 32 * (i // 2 + 1))
                else:
                    n_cols = [len([b for b in blocks if b[0] == "cols"][p::2]) for p in range(2)][i % 2]
                    act.wait_ge(stage_in[i % 2], 32 * n_cols + 16 * (i // 2 + 1 - n_cols))
                if is_qk[i]:
                    act.wait_ge(centred, 3 * sum(is_qk[:i + 1]))
                n = c1 - c0
                if kind == "cols":
                    nc.scalar.copy(w["A"][:, c0:c1], stage[:, i % 2, 0, 0:n])
                    nc.scalar.copy(w["B"][:, c0:c1], stage[:, i % 2, 1, 0:n]).then_inc(split_h, 1)
                else:
                    nc.scalar.copy(w["Kh"][:, c0 * D:c1 * D], stage[:, i % 2, 0, 0:n * D]).then_inc(split_h, 1)
            weights_h(1)
            all_tiles(act, pixels_h)

        @block.vector
        def _(dve):
            n = 0
            for i in range(len(blocks)):
                if is_qk[i]:
                    part = stage[:, i % 2, :, 0:768].rearrange("p x (h d) -> p x h d", d=64)
                    dve.wait_ge(stage_in[i % 2], 32 * (i // 2 + 1))
                    since(dve, centred, n)
                    nc.vector.tensor_reduce(headsum[:, :, :], part, AX.X, ALU.add).then_inc(centred, 1)
                    dve.wait_ge(centred, n + 1)
                    nc.vector.tensor_scalar(headsum[:, :, :], headsum[:, :, :], 1.0 / 64, None,
                                            ALU.mult).then_inc(centred, 1)
                    dve.wait_ge(centred, n + 2)
                    nc.vector.tensor_tensor(part, part, headsum[:, :, :].unsqueeze(3).to_broadcast([128, 2, 12, 64]),
                                            ALU.subtract).then_inc(centred, 1)
                    n += 3
            dve.wait_ge(const_in, 16 * 15)
            nc.vector.tensor_copy(w["sel"][:, :, :].rearrange("p m n -> p (m n)"), sel_in[:, :]).then_inc(small, 1)
            nc.vector.tensor_copy(w["eye"][:, :], w["ident"][:, 0:98]).then_inc(small, 1)
            dve.wait_ge(meaned, 1)
            nc.vector.tensor_tensor(w["f0qkb"][:, :], qkb_in[:, :], ps_mean[:, 0:12], ALU.subtract).then_inc(small, 1)

            def tile(t, u):
                dve.wait_ge(px_h, t + 1)
                nc.vector.tensor_tensor(pxL[:, u % 2, :], px[:, u, :], w32(pxH[:, u % 2, :]),
                                        ALU.subtract).then_inc(px_l, 1)
                dve.wait_ge(tok_ps, t + 1)
                since(dve, tok_out[u % 2], 8 * t - 8 * (u % 2))
                nc.vector.tensor_tensor(tok[:, u % 2, :], ps[u % 2][:, 0:D], tokb[:, :], ALU.add).then_inc(tok_sb, 1)

            all_tiles(dve, tile)

        @block.tensor
        def _(pe):
            pe.wait_ge(const_in, 16 * 15)
            nc.tensor.matmul(ps_mean[:, 0:12], blockmean[:, :], qkb_in[:, :], start=True, stop=True).then_inc(meaned, 1)

            def tile(t, u):
                c = 0 if not isinstance(t, int) or t < MID_TILES else edges[t - MID_TILES]
                if isinstance(t, int) and t == first_of[c]:
                    pe.wait_ge(weff_l, c + 1)
                pe.wait_ge(px_h, t + 1)
                since(pe, tok_sb, t - 1)
                out = ps[u % 2][:, 0:D]
                for k in range(KC):
                    x = pxH[:, u % 2, 128 * k:128 * k + 128]
                    nc.tensor.matmul(out, x, weffH[:, c % 2, k, :], start=(k == 0), stop=False)
                    nc.tensor.matmul(out, x, weffL[:, c % 2, k, :], start=False, stop=False)
                pe.wait_ge(px_l, t + 1)
                for k in range(KC):
                    last = nc.tensor.matmul(out, pxL[:, u % 2, 128 * k:128 * k + 128], weffH[:, c % 2, k, :],
                                            start=False, stop=(k == KC - 1))
                last.then_inc(tok_ps, 1)

            all_tiles(pe, tile)


def layers(nc, a, w, h0, out):
    with ExitStack() as ctx:
        def sb(name, shape, dt=F32):
            return ctx.enter_context(nc.sbuf_tensor(name, shape, dt))

        def sem(name):
            return ctx.enter_context(nc.semaphore(name))

        def signal(name, per):
            return Signal(sem(name), per)

        def signals(name, keys, per):
            one = sem(name)
            return {key: Signal(one, per * len(keys), per * n, per) for n, key in enumerate(keys)}

        hin = sb("hin", [HALF, NT, D])
        h = sb("h", [HALF, NT, D])
        bnst = sb("bnst", [HALF, NT, 6])
        bnmv = sb("bnmv", [HALF, NT, 2])
        vareps = sb("vareps", [HALF, NT])
        rstd = sb("rstd", [HALF, NT])
        mhalf = sb("mhalf", [HALF, 1])
        eps = sb("eps", [HALF, 1])
        xA = sb("xA", [128, 2, TT], F32R)
        xB = sb("xB", [128, 2, TT], F32R)
        qs = sb("qs", [128, NH, TT], F32R)
        ks = sb("ks", [128, NH, TT], F32R)
        q16, k16_h, k16_l = qs, ks[:, 0:3, :], ks[:, 3:6, :]
        m16 = ks[:, 6:9, :]
        m64 = ks[:, 0:3, :]
        vf = sb("vf", [HALF, NT, 6, 3, 64])
        va = vf[:, :, :, 0:3:2, 0:32]
        P = 6
        work = sb("work", [128, P, TT])
        probs = work[0:HALF, :, :]
        qc = work
        mx = sb("mx", [HALF, NT, NH])
        rh = sb("rh", [128, 3, TT], F32R)
        rl = sb("rl", [128, 3, TT], F32R)
        sa = sb("sa", [128, 3, TT])
        sc = sb("sc", [128, 3, TT])
        qvar = sa[0:12, 0, :]
        xn = sa[0:HALF, :, :].rearrange("p a n -> p (a n)")[:, 0:NT * 256].rearrange("p (t c) -> p t c", c=256)
        rowH = sb("rowH", [SELROWS, TT], F32R)
        lg = sb("lg", [HALF, NT, 14])
        gmax = sb("gmax", [HALF, NT, 3])
        gsum = sb("gsum", [HALF, NT, 3])
        top8 = sb("top8", [HALF, NT, 8])
        idx8 = sb("idx8", [HALF, NT, 8], U32)
        idxf = sb("idxf", [HALF, NT, 8])
        hot = sb("hot", [HALF, NT, 10])
        hot2 = sb("hot2", [HALF, NT, 10])
        gm = sb("gm", [HALF, NT, NH])
        cm = sb("cm", [HALF, NT, 28])

        banks = [ctx.enter_context(nc.psum_tensor(f"ps{i}", [128, 512], F32)) for i in range(8)]
        ready = sem("ready")
        held = sem("held")
        held_pool = sem("held_pool")
        h_in = sem("h_in")
        h_out = sem("h_out")
        subs = ("a0", "f0", "a1", "f1")
        stats = signals("stats", subs, 8)
        vare = signals("vare", subs, 2)
        rstds = signals("rstd", subs, 2)
        normed = signals("normed", subs, 8)
        xh = signals("xh", subs, 2)
        xl = signals("xl", subs, 2)
        resid = {"a0": signal("a0_resid", 4), "f0": signal("f0_resid", 8), "a1": signal("a1_resid", 4),
                 "f1": signal("f1_resid", 4)}
        at = ("a0", "a1")
        q_h = signals("q_h", at, 3)
        q_l = signals("q_l", at, 3)
        q_own = signals("q_own", at, 9)
        q_own3 = signals("q_own3", at, 3)
        k_h = signals("k_h", at, 6)
        k_l = signals("k_l", at, 6)
        ones = signals("ones", at, 1)
        va_in = signals("va", at, 2)
        maxes = signals("maxes", at, 24)
        nm = signals("nm", at, 3)
        exps = signals("exps", at, 24)
        dens = signals("dens", at, 12)
        quot = signals("quot", at, 6)
        on_h = signals("on_h", at, 6)
        on_l = signals("on_l", at, 6)
        rope_b = signal("rope_b", 3)
        rope_s = signal("rope_s", 3)
        rope_p = signal("rope_p", 3)
        rope_c = signal("rope_c", 3)
        rope_u = signal("rope_u", 3)
        zeroed = signal("zeroed", 1)
        h_bias = signal("h_bias", 4)
        f_v = signal("f_v", 12)
        f_gate = signal("f_gate", 28)
        f_gexp = signal("f_gexp", 1)
        f_row = signal("f_row", 4)
        f_qc = signal("f_qc", 12)
        f_sq = signal("f_sq", 12)
        f_squ = signal("f_squ", 10)
        f_dev = signal("f_dev", 2)
        f_rs = signal("f_rs", 2)
        f_rsr = signal("f_rsr", 4)
        f_t = signal("f_t", 12)
        f_u = signal("f_u", 12)
        f_h = signal("f_h", 36)
        f_l = signal("f_l", 24)
        f_max = signal("f_max", 24)
        f_nm = signal("f_nm", 6)
        f_exp = signal("f_exp", 24)
        f_sum = signal("f_sum", 12)
        f_den = signal("f_den", 6)
        f_quot = signal("f_quot", 12)
        f_on = signal("f_on", 6)
        f_onh = signal("f_onh", 6)
        f_onl = signal("f_onl", 6)
        m_exp = signal("m_exp", 1)
        m_gate = signal("m_gate", 21)
        m_row = signal("m_row", 2)
        m_relu = signal("m_relu", MOE_M)
        m_c = signal("m_c", MOE_M)
        m_hid = signal("m_hid", MOE_M)
        m_h = signal("m_h", MOE_M)
        m_l = signal("m_l", MOE_M)
        m_used = signal("m_used", MOE_M - 1)

        ident, eye, sel, sumcol = w["ident"], w["eye"], w["sel"], w["sumcol"]
        NREADY = 9

        def attention_fills(s):
            fills = [] if s == "a0" else [(s + "_x", 2, xl[s], after(0))]
            fills += [("a0_qk", 3, k_l[s], lambda k: 2 * k + 2) if s == "a0" else ("a1_qk", 3, rope_b, after(0))]
            fills += [(s + "_v", 2, va_in[s], after(0))]
            for stage, n in S1_S2:
                if stage == "S1":
                    fills += [(f"{s}_S1{n}", 4, maxes[s], after(4 * n))]
                elif stage == "mx":
                    fills += [(f"{s}_mx{n}", 1, nm[s], after(n))]
                else:
                    fills += [(f"{s}_S2{n}", 4, exps[s], after(4 * n))]
            return fills

        BY_PAIR = [0, 3, 1, 4, 2, 5]

        S1_S2 = [("S1", 0), ("S1", 1), ("S1", 2), ("mx", 0), ("S1", 3), ("S2", 0), ("S1", 4), ("S2", 1),
                 ("mx", 1), ("S1", 5), ("S2", 2), ("S2", 3), ("mx", 2), ("S2", 4), ("S2", 5)]

        LEAD = 4
        F0_S1_S2 = [("S1", 0), ("S1", 1), ("mx", 0), ("S2", 0), ("S1", 2), ("S2", 1), ("mx", 1), ("S2", 2),
                    ("mx", 2), ("S2", 3), ("S2", 4), ("S2", 5)]

        def after(n):
            return lambda k: n + k + 1

        s_fills = attention_fills("a0")
        s_fills += [("f0_x", 2, xl["f0"], after(0)), ("f0_qk0", 6, f_sq, after(0)),
                    ("f0_v", 8, f_v, lambda k: 3 * (k // 2) + 1 + 2 * (k % 2))]
        for s in range(2):
            s_fills += [(f"f0_rs{s}", 6, f_t, after(6 * s))]
            for stage, n in F0_S1_S2:
                if stage == "S1":
                    s_fills += [(f"f0_S1{s}{n}", 4, f_max, after(12 * s + 4 * n))]
                elif stage == "mx":
                    s_fills += [(f"f0_mx{s}{n}", 1, f_nm, after(3 * s + n))]
                else:
                    s_fills += [(f"f0_S2{s}{n}", 2, f_exp, after(12 * s + 2 * n))]
            s_fills += [(f"f0_g{s}", 1, f_row, after(2 * s + 1))]
            if s == 0:
                s_fills += [("f0_qk1", 6, f_sq, after(6))]
            s_fills += [(f"f0_gb{s}", 3, f_on, after(3 * s))]
        s_fills += attention_fills("a1")
        s_fills += [("f1_x", 2, xl["f1"], after(0)), ("f1_r", 1, m_exp, after(0))]
        s_fills += [(f"f1_h{m}", 1, m_relu, after(m)) for m in range(LEAD)]
        s_fills += [("f1_c", 1, m_row, after(1)), ("f1_cb0", 1, m_c, after(0)), ("f1_cb1", 1, m_c, after(1))]
        for m in range(MOE_M):
            s_fills += [(f"f1_h{m + LEAD}", 1, m_relu, after(m + LEAD))] if m + LEAD < MOE_M else []
            s_fills += [(f"f1_cb{m + 2}", 1, m_c, after(m + 2))] if m + 2 < MOE_M else []
        s_fills += [("a0_x", 2, xl["a0"], after(0))]
        c_fills = [("a0_pv", 6, quot["a0"], after(0)), ("a0_out", 4, resid["a0"], after(0))]
        c_fills += [("f0_var0", 1, f_dev, after(0)), ("f0_pv0", 6, f_quot, after(0)), ("f0_var1", 1, f_dev, after(1)),
                    ("f0_out0", 4, resid["f0"], after(0)), ("f0_pv1", 6, f_quot, after(6)),
                    ("f0_out1", 4, resid["f0"], after(4))]
        c_fills += [("a1_pv", 6, quot["a1"], after(0)), ("a1_out", 4, resid["a1"], after(0)),
                    ("f1_y", 4, resid["f1"], after(0))]
        S = Banks(banks[:4], sem("s_filled"), s_fills, 2)
        C = Banks(banks[4:], sem("c_filled"), c_fills)

        def tok(t):
            return slice(HALF * t, HALF * t + HALF)

        def img(im):
            return slice(TOK * im, TOK * im + TOK)

        def all_steps(e, body):
            if STEPS > 1:
                with e.Fori(0, STEPS - 1) as it:
                    body(it, True)
            body(STEPS - 1, False)

        NEXT_STATS, NEXT_NORMED = 6, 8

        def images(tile):
            return tile.rearrange("p (i t) -> p i t", i=IMS)

        def turn(table):
            return table[:, :].unsqueeze(1).to_broadcast([128, IMS, TOK])

        block = ctx.enter_context(nc.Block())

        @block.sync
        def _(sp):
            def load(it):
                for half in range(2):
                    sp.dma_start(hin[:, half:NT:2, :],
                                 h0v[half][:, bass.ds(IMS * it, IMS), :]).then_inc(h_in, 16)

            h0v = [h0[IMAGES * HALF * half:IMAGES * HALF * (half + 1), :].rearrange("(p b) d -> p b d", b=IMAGES)
                   for half in range(2)]

            def body(it, more):
                if more:
                    resid["a0"].wait(sp, it)
                    load(it + 1)
                resid["f1"].wait(sp, it)
                sp.dma_start(out[bass.ds(it, 1)].rearrange("o p t d -> (o p) t d"), h[:, :, :]).then_inc(h_out, 16)

            load(0)
            all_steps(sp, body)
            sp.wait_ge(h_out, 16 * STEPS)

        @block.gpsimd
        def _(pool):
            constant = [(w32(ks[:, :, :]), 0.0), (mhalf[:, :], -0.5), (eps[:, :], EPS), (w32(qs[:, :, :]), 0.0),
                        (vf[:, :, :, 1, :], 1.0), (mx[:, :, :], 0.0), (w32(rowH[:, :]), 0.0), (cm[:, :, 24:27], 1.0),
                        (cm[:, :, 27:28], 0.0)]
            for n, (to, value) in enumerate(constant):
                nc.gpsimd.memset(to, value).then_inc(ready, 1)
                pool.wait_ge(ready, n + 1)

            def rstd_of_tokens(it, s):
                for im in range(IMS):
                    two = slice(2 * im, 2 * im + 2)
                    stats[s].wait(pool, it, 4 * im + 4)
                    nc.gpsimd.tensor_tensor(vareps[:, two], bnmv[:, two, 1], eps[:, :].to_broadcast([HALF, 2]),
                                            ALU.add).then_inc(vare[s].sem, 1)
                    vare[s].wait(pool, it, im + 1)
                    nc.gpsimd.tensor_tensor(rstd[:, two], vareps[:, two], mhalf[:, :].to_broadcast([HALF, 2]),
                                            ALU.pow).then_inc(rstds[s].sem, 1)

            def low(out_, full, high):
                return nc.gpsimd.tensor_tensor(out_, full, w32(high), ALU.subtract)

            def ones_beside_values(it, s):
                for t in range(NT):
                    ins = nc.gpsimd.memset(va[:, t, :, :, 16:32], 1.0)
                ins.then_inc(ones[s].sem, 1)

            def last_alone(it, s):
                for g in range(3):
                    q_l[s].wait(pool, it, g + 1)
                    nc.gpsimd.tensor_tensor(q16[:, 4 * g + 3, :], w32(rh[:, g, :]), w["own"][:, 3:4]
                                            .to_broadcast([128, TT]), ALU.mult).then_inc(q_own3[s].sem, 1)

            def body(it, more):
                ones_beside_values(it, "a0")
                ones["a0"].wait(pool, it)
                last_alone(it, "a0")
                quot["a0"].wait(pool, it)
                pool.sem_inc(held_pool, 1)
                nc.gpsimd.memset(w32(qs[64:128, :, :]), 0.0).then_inc(zeroed.sem, 1)
                zeroed.wait(pool, it)

                rstd_of_tokens(it, "f0")
                normed["f0"].wait(pool, it)
                for t in range(NT):
                    nc.gpsimd.tensor_tensor(h[:, t, :], h[:, t, :], w["f0pb"][:, :], ALU.add).then_inc(h_bias.sem, 1)
                h_bias.wait(pool, it)
                for s in range(2):
                    for k, i in enumerate(BY_PAIR):
                        dst = qs if i < 3 else ks
                        for x in range(2):
                            hd = 2 * (i % 3) + x
                            f_h.wait(pool, it, 18 * s + 3 * k + 1 + 2 * x)
                            high = dst[0:64, hd, :] if x == 0 else rh[64:128, k % 3, :]
                            low(dst[0:64, 6 + hd, :], qc[64 * x:64 * x + 64, i, :], high).then_inc(f_l.sem, 1)

                rstd_of_tokens(it, "a1")
                ones_beside_values(it, "a1")
                for g in range(3):
                    rope_s.wait(pool, it, g + 1)
                    nc.gpsimd.tensor_tensor(images(sa[:, g, :]), images(sa[:, g, :]), turn(w["cos"]),
                                            ALU.mult).then_inc(rope_c.sem, 1)
                last_alone(it, "a1")

                rstd_of_tokens(it, "f1")
                for m in range(MOE_M):
                    m_h.wait(pool, it, m + 1)
                    low(rl[:, m % 3, :], sc[:, m % 3, :], rh[:, m % 3, :]).then_inc(m_l.sem, 1)
                    if m == NEXT_STATS and more:
                        rstd_of_tokens(it + 1, "a0")

            rstd_of_tokens(0, "a0")
            all_steps(pool, body)

        @block.scalar
        def _(act):
            def copy(out_, in_, scale=1.0):
                return nc.scalar.activation(out_, in_, ACT.Copy, scale=scale)

            def turned(it, s):
                for k, x in enumerate((xA, xB)):
                    bank = S.wait(act, it - 1 if s == "a0" else it, s + "_x", k)
                    copy(x[:, 0, :], bank[:, 0:TT]).then_inc(xh[s].sem, 1)

            def attention(it, s, scale):
                def values_in():
                    for k in range(2):
                        bank = S.wait(act, it, s + "_v", k)
                        for x in range(2):
                            ins = copy(va[:, 2 * k + x, :, :, 0:16],
                                       bank[0:HALF, D * x:D * x + D].rearrange("p (a b d) -> p a b d", a=6, d=16))
                        ins.then_inc(va_in[s].sem, 1)

                def high(g, full):
                    copy(rh[0:64, g, :], full[0:64]).then_inc(q_h[s].sem, 1)
                    for rows_ in (slice(0, 64), slice(64, 128)):
                        copy(k16_h[rows_, g, :], full[64:128]).then_inc(k_h[s].sem, 1)

                def alone(g):
                    q_l[s].wait(act, it, g + 1)
                    for j in range(3):
                        nc.scalar.activation(q16[:, 4 * g + j, :], w32(rh[:, g, :]), ACT.Identity,
                                             scale=w["own"][:, j:j + 1]).then_inc(q_own[s].sem, 1)

                if s == "a0":
                    def high_of(g):
                        bank = S.wait(act, it, "a0_qk", g)
                        high(g, bank[:, 0:TT])
                else:
                    for g in range(3):
                        bank = S.wait(act, it, "a1_qk", g)
                        nc.scalar.activation(sa[:, g, :], bank[:, 0:TT], ACT.Identity, bias=w["a1qkb"][:, g:g + 1]
                                             ).then_inc(rope_b.sem, 1)

                    def high_of(g):
                        rope_u.wait(act, it, g + 1)
                        high(g, sc[:, g, :])

                high_of(0)
                high_of(1)
                alone(0)
                if s == "a0":
                    high_of(2)
                values_in()
                alone(1)
                if s == "a1":
                    high_of(2)
                alone(2)

                def minus_max(g):
                    bank = S.wait(act, it, f"{s}_mx{g}", 0)
                    copy(m16[0:4, g, :], bank[0:4, 0:TT], scale=-1.0).then_inc(nm[s].sem, 1)

                def outputs_h(b):
                    quot[s].wait(act, it, b + 1)
                    o = slice(TOK * (b % 2), TOK * (b % 2) + TOK)
                    if s == "a1":
                        nc.scalar.activation(rh[:, b // 2, o], sc[:, b // 2, o], ACT.Identity,
                                             bias=w["a1vb"][:, b // 2:b // 2 + 1]).then_inc(on_h[s].sem, 1)
                    else:
                        copy(rh[:, b // 2, o], sc[:, b // 2, o]).then_inc(on_h[s].sem, 1)

                for n in range(24):
                    if n % 8 == 0:
                        minus_max(n // 8)
                    bank = S.wait(act, it, f"{s}_S2{n // 4}", n % 4)
                    if n >= P:
                        C.wait(act, it, s + "_pv", (n - P) // 4)
                    ins = nc.scalar.activation(probs[:, n % P, :], bank[0:HALF, 0:TT], ACT.Exp, scale=scale)
                    ins.then_inc(exps[s].sem, 1)
                    if n in (11, 15, 19, 23):
                        outputs_h(n // 4 - 2)
                outputs_h(4)
                outputs_h(5)

            def body(it, more):
                attention(it, "a0", float(D) ** -0.5)

                turned(it, "f0")

                def values_in(t):
                    for k in range(2):
                        bank = S.wait(act, it, "f0_v", 2 * t + k)
                        copy(vf[:, t, 3 * k:3 * k + 3, 0:3:2, :],
                             bank[0:HALF, 0:384].rearrange("p (a x d) -> p a x d", a=3, d=64)).then_inc(f_v.sem, 1)
                        if k == 1:
                            copy(lg[:, t, :], bank[0:HALF, 384:398]).then_inc(f_v.sem, 1)

                def q_and_k(s):
                    for i in range(6):
                        bank = S.wait(act, it, f"f0_qk{s}", i)
                        tile = 3 * s + i % 3 + (6 if i >= 3 else 0)
                        bias = w["f0qkb"][:, tile:tile + 1]
                        nc.scalar.activation(qc[:, i, :], bank[:, 0:TT], ACT.Identity, bias=bias).then_inc(f_qc.sem, 1)
                        if i >= 3:
                            f_squ.wait(act, it, 5 * s + i - 2)
                        elif s:
                            f_quot.wait(act, it, 2 * i + 2)
                        nc.scalar.activation(sa[:, i % 3, :], bank[:, 0:TT], ACT.Square, bias=bias
                                             ).then_inc(f_sq.sem, 1)

                def denominators(s, hd):
                    x = hd % 2
                    bank = C.wait(act, it, f"f0_pv{s}", hd)
                    copy(sa[64 * x:64 * x + 64, hd // 2, :], bank[64 - 64 * x:128 - 64 * x, 0:TT]
                         ).then_inc(f_sum.sem, 1)

                q_and_k(0)
                values_in(0)
                for s in range(2):
                    bank = C.wait(act, it, f"f0_var{s}", 0)
                    nc.scalar.activation(qvar, bank[0:12, 0:TT], ACT.Sqrt, bias=eps[0:12, :]).then_inc(f_dev.sem, 1)
                    if s == 0:
                        values_in(1)
                    f_rs.wait(act, it, s + 1)
                    copy(rowH[0:12, :], qvar).then_inc(f_rsr.sem, 1)
                    if s == 0:
                        values_in(2)
                        values_in(3)
                    for k, i in enumerate(BY_PAIR):
                        f_u.wait(act, it, 6 * s + k + 1)
                        dst = qs if i < 3 else ks
                        for x in range(2):
                            copy(dst[0:64, 2 * (i % 3) + x, :], qc[64 * x:64 * x + 64, i, :]).then_inc(f_h.sem, 1)
                        if k >= 3:
                            f_l.wait(act, it, 12 * s + 2 * k - 4)
                        copy(rh[64:128, k % 3, :], qc[64:128, i, :]).then_inc(f_h.sem, 1)
                    if s == 0:
                        f_gate.wait(act, it, 4)
                        nc.scalar.activation(lg[:, :, :], lg[:, :, :], ACT.Exp).then_inc(f_gexp.sem, 1)
                    for n in range(12):
                        if n % 4 == 0:
                            bank = S.wait(act, it, f"f0_mx{s}{n // 4}", 0)
                            copy(m64[96:98, n // 4, :], bank[0:2, 0:TT], scale=-1.0).then_inc(f_nm.sem, 1)
                        bank = S.wait(act, it, f"f0_S2{s}{n // 2}", n % 2)
                        if n >= P:
                            C.wait(act, it, f"f0_pv{s}", (n - P) // 2)
                        else:
                            f_l.wait(act, it, 12 * s + 2 * n + 2)
                        nc.scalar.activation(probs[:, BY_PAIR[n % P], :], bank[0:HALF, 0:TT], ACT.Exp, scale=0.125
                                             ).then_inc(f_exp.sem, 1)
                        if n >= 3 and n % 2:
                            denominators(s, n // 2 - 1)
                    denominators(s, 5)
                    bank = S.wait(act, it, f"f0_g{s}", 0)
                    copy(rowH[0:12, :], bank[0:12, 0:TT]).then_inc(f_row.sem, 1)
                    if s == 0:
                        q_and_k(1)
                    for i in range(3):
                        f_on.wait(act, it, 3 * s + i + 1)
                        copy(rh[:, i, :], sc[:, i, :]).then_inc(f_onh.sem, 1)

                turned(it, "a1")
                attention(it, "a1", 16.0 ** -0.5)

                turned(it, "f1")
                bank = S.wait(act, it, "f1_r", 0)
                nc.scalar.activation(lg[:, :, 0:8], bank[0:HALF, 0:NT * 8].rearrange("p (t e) -> p t e", e=8),
                                     ACT.Exp, scale=-1.0).then_inc(m_exp.sem, 1)

                def relu(m):
                    bank_ = S.wait(act, it, f"f1_h{m}", 0)
                    if m >= P:
                        m_hid.wait(act, it, m - P + 1)
                    nc.scalar.activation(work[:, m % P, :], bank_[:, 0:TT], ACT.Relu).then_inc(m_relu.sem, 1)

                for m in range(LEAD):
                    relu(m)
                bank = S.wait(act, it, "f1_c", 0)
                copy(rowH[0:28, :], bank[0:28, 0:TT]).then_inc(m_row.sem, 1)
                for m in range(MOE_M):
                    m_hid.wait(act, it, m + 1)
                    if m >= 3:
                        m_used.wait(act, it, m - 2)
                    copy(rh[:, m % 3, :], sc[:, m % 3, :]).then_inc(m_h.sem, 1)
                    if m + LEAD < MOE_M:
                        relu(m + LEAD)
                if more:
                    turned(it + 1, "a0")

            turned(0, "a0")
            all_steps(act, body)

        @block.vector
        def _(dve):
            tt = nc.vector.tensor_tensor

            def hold(e):
                e.sem_inc(held, 1)

            def low(out_, full, high):
                return tt(out_, full, w32(high), ALU.subtract)

            def add_up(it, s, stage, src, t):
                bank = C.wait(dve, it, stage, t)
                tt(h[:, t, :], src[:, t, :], bank[0:HALF, 0:D], ALU.add).then_inc(resid[s].sem, 1)

            def measure(it, s, src, before=None):
                for im in range(IMS):
                    tiles = range(2 * im, 2 * im + 2)
                    for t in tiles:
                        if before:
                            before(t)
                    for t in tiles:
                        nc.vector.bn_stats(bnst[:, t, :], src[:, t, :]).then_inc(stats[s].sem, 1)
                    stats[s].wait(dve, it, 4 * im + 2)
                    hold(dve)
                    for t in tiles:
                        nc.vector.bn_aggr(bnmv[:, t, :], bnst[:, t, :]).then_inc(stats[s].sem, 1)

            def scale(it, s, src):
                for t in range(NT):
                    if t % 2 == 0:
                        rstds[s].wait(dve, it, t // 2 + 1)
                    for d0, s0, n in ((0, 0, D), (D, 128, 256 - D)):
                        nc.vector.tensor_scalar(xn[:, t, d0:d0 + n], src[:, t, s0:s0 + n], bnmv[:, t, 0:1],
                                                rstd[:, t:t + 1], ALU.subtract, ALU.mult).then_inc(normed[s].sem, 1)

            def turned(it, s):
                for k, x in enumerate((xA, xB)):
                    bank = S.wait(dve, it - 1 if s == "a0" else it, s + "_x", k)
                    xh[s].wait(dve, it, k + 1)
                    low(x[:, 1, :], bank[:, 0:TT], x[:, 0, :]).then_inc(xl[s].sem, 1)

            def normalise(it, s, src, before):
                measure(it, s, src, before)
                scale(it, s, src)
                turned(it, s)

            def measure_next(it):
                dve.wait_ge(h_in, 32 * it + 32)
                measure(it, "a0", hin)

            def largest(bank, t0, head):
                return nc.vector.tensor_reduce(mx[:, t0:t0 + 2, head], bank[0:HALF, 0:TT]
                                               .rearrange("p (t k) -> p t k", t=2), AX.X, ALU.max)

            def attention(it, s):
                def cut_group(g, full):
                    q_h[s].wait(dve, it, g + 1)
                    k_h[s].wait(dve, it, 2 * g + 2)
                    low(rh[64:128, g, :], full[0:64], rh[0:64, g, :]).then_inc(q_l[s].sem, 1)
                    for rows_ in (slice(0, 64), slice(64, 128)):
                        low(k16_l[rows_, g, :], full[64:128], k16_h[64:128, g, :]).then_inc(k_l[s].sem, 1)

                def maxima(g):
                    for n in range(8 * g, 8 * g + 8):
                        bank = S.wait(dve, it, f"{s}_S1{n // 4}", n % 4)
                        largest(bank, 2 * (n % 2), n // 2).then_inc(maxes[s].sem, 1)

                if s == "a0":
                    for g in range(3):
                        bank = S.wait(dve, it, "a0_qk", g)
                        cut_group(g, bank[:, 0:TT])
                    maxima(0)
                else:
                    swap = [(i // 16) * 16 + (i + 8) % 16 for i in range(32)]

                    def shuffled(g):
                        rope_b.wait(dve, it, g + 1)
                        hold(dve)
                        nc.vector.stream_shuffle(sc[:, g, :], sa[:, g, :], swap).then_inc(rope_s.sem, 1)

                    def rotated(g):
                        rope_s.wait(dve, it, g + 1)
                        tt(images(sc[:, g, :]), images(sc[:, g, :]), turn(w["sin"]), ALU.mult).then_inc(rope_p.sem, 1)
                        rope_p.wait(dve, it, g + 1)
                        rope_c.wait(dve, it, g + 1)
                        tt(sc[:, g, :], sa[:, g, :], sc[:, g, :], ALU.add).then_inc(rope_u.sem, 1)

                    for g in range(3):
                        shuffled(g)
                    rotated(0)
                    rotated(1)
                    cut_group(0, sc[:, 0, :])
                    cut_group(1, sc[:, 1, :])
                    rotated(2)
                    maxima(0)
                    cut_group(2, sc[:, 2, :])
                maxima(1)
                maxima(2)
                def outputs_l(b):
                    g, o = b // 2, slice(TOK * (b % 2), TOK * (b % 2) + TOK)
                    on_h[s].wait(dve, it, b + 1)
                    if s == "a1":
                        nc.vector.scalar_tensor_tensor(rl[:, g, o], sc[:, g, o], w["a1vb"][:, g:g + 1],
                                                       w32(rh[:, g, o]), ALU.add, ALU.subtract
                                                       ).then_inc(on_l[s].sem, 1)
                    else:
                        low(rl[:, g, o], sc[:, g, o], rh[:, g, o]).then_inc(on_l[s].sem, 1)

                to_all = [16 + i % 16 for i in range(32)]
                if s == "a1":
                    k_l[s].wait(dve, it)
                for b in range(6):
                    g, o = b // 2, slice(TOK * (b % 2), TOK * (b % 2) + TOK)
                    bank = C.wait(dve, it, s + "_pv", b)
                    hold(dve)
                    nc.vector.stream_shuffle(sa[:, g, o], bank[:, 0:TOK], to_all).then_inc(dens[s].sem, 1)
                    dens[s].wait(dve, it, 2 * b + 1)
                    nc.vector.reciprocal(sa[:, g, o], sa[:, g, o]).then_inc(dens[s].sem, 1)
                    dens[s].wait(dve, it, 2 * b + 2)
                    tt(sc[:, g, o], bank[:, 0:TOK], sa[:, g, o], ALU.mult).then_inc(quot[s].sem, 1)
                    if b:
                        outputs_l(b - 1)
                outputs_l(5)

            def gates(it, n, first):

                def step(ins, last=True, alone=False):
                    n[0] += 1
                    ins.then_inc(f_gate.sem, 1)
                    if last:
                        f_gate.wait(dve, it, n[0])
                    if alone:
                        hold(dve)

                pairs = lg[:, :, 10:14].rearrange("p t (a b) -> p t a b", b=2)
                if first:
                    f_v.wait(dve, it)
                    step(nc.vector.tensor_reduce(gmax[:, :, 0], lg[:, :, 0:10], AX.X, ALU.max), False)
                    step(nc.vector.tensor_reduce(gmax[:, :, 1:3], pairs, AX.X, ALU.max))
                    step(tt(lg[:, :, 0:10], lg[:, :, 0:10], gmax[:, :, 0:1].to_broadcast([HALF, NT, 10]),
                            ALU.subtract), False)
                    step(tt(pairs, pairs, gmax[:, :, 1:3].unsqueeze(3).to_broadcast([HALF, NT, 2, 2]),
                            ALU.subtract))
                    return
                f_gexp.wait(dve, it)
                step(nc.vector.tensor_reduce(gsum[:, :, 0], lg[:, :, 0:10], AX.X, ALU.add), False)
                step(nc.vector.tensor_reduce(gsum[:, :, 1:3], pairs, AX.X, ALU.add))
                step(nc.vector.reciprocal(gsum[:, :, :], gsum[:, :, :]))
                step(tt(lg[:, :, 0:10], lg[:, :, 0:10], gsum[:, :, 0:1].to_broadcast([HALF, NT, 10]),
                        ALU.mult), False)
                step(tt(pairs, pairs, gsum[:, :, 1:3].unsqueeze(3).to_broadcast([HALF, NT, 2, 2]), ALU.mult),
                     alone=True)
                top_two(step, lg, 10)
                step(tt(hot[:, :, :], hot[:, :, :], lg[:, :, 0:10], ALU.mult))
                step(nc.vector.tensor_reduce(gsum[:, :, 0], hot[:, :, :], AX.X, ALU.add))
                step(nc.vector.tensor_scalar(gsum[:, :, 0], gsum[:, :, 0], 2.0 ** -23, None, ALU.max))
                step(nc.vector.reciprocal(gsum[:, :, 0], gsum[:, :, 0]))
                step(tt(hot[:, :, :], hot[:, :, :], gsum[:, :, 0:1].to_broadcast([HALF, NT, 10]), ALU.mult))
                step(nc.vector.scalar_tensor_tensor(gm[:, :, 2:12], hot[:, :, :], 4.0,
                                                    lg[:, :, 11:12].to_broadcast([HALF, NT, 10]),
                                                    ALU.mult, ALU.mult), False)
                step(nc.vector.scalar_tensor_tensor(gm[:, :, 0:2], lg[:, :, 12:14], 4.0,
                                                    lg[:, :, 10:11].to_broadcast([HALF, NT, 2]),
                                                    ALU.mult, ALU.mult), False)
                assert n[0] == f_gate.per, n

            def top_two(step, src, n):
                for t in range(NT):
                    step(nc.vector.max(top8[:, t, :], src[:, t, 0:n]), t == NT - 1, t == NT - 1)
                for t in range(NT):
                    step(nc.vector.max_index(idx8[:, t, :], top8[:, t, :], src[:, t, 0:n]), t == NT - 1)
                step(nc.vector.tensor_copy(idxf[:, :, 0:2], idx8[:, :, 0:2]))
                iota = w["iota"][:, 0:n].unsqueeze(1).to_broadcast([HALF, NT, n])
                for k, dst in enumerate((hot, hot2)):
                    step(tt(dst[:, :, 0:n], iota, idxf[:, :, k:k + 1].to_broadcast([HALF, NT, n]), ALU.is_equal),
                         k == 1)
                step(tt(hot[:, :, 0:n], hot[:, :, 0:n], hot2[:, :, 0:n], ALU.add))

            def router(it):
                n = [0]

                def step(ins, last=True, alone=False):
                    n[0] += 1
                    ins.then_inc(m_gate.sem, 1)
                    if last:
                        m_gate.wait(dve, it, n[0])
                    if alone:
                        hold(dve)

                m_exp.wait(dve, it)
                score = lg[:, :, 0:8]
                step(nc.vector.tensor_scalar(score, score, 1.0, None, ALU.add))
                step(nc.vector.reciprocal(score, score))
                step(tt(hot[:, :, 0:8], score, w["bal"][:, :].unsqueeze(1).to_broadcast([HALF, NT, 8]), ALU.add),
                     alone=True)
                top_two(step, hot, 8)
                step(tt(hot[:, :, 0:8], hot[:, :, 0:8], score, ALU.mult))
                step(nc.vector.tensor_reduce(gsum[:, :, 0], hot[:, :, 0:8], AX.X, ALU.add))
                step(nc.vector.tensor_scalar(gsum[:, :, 0], gsum[:, :, 0], 1e-20, None, ALU.add))
                step(nc.vector.reciprocal(gsum[:, :, 0], gsum[:, :, 0]))
                step(tt(hot[:, :, 0:8], hot[:, :, 0:8], gsum[:, :, 0:1].to_broadcast([HALF, NT, 8]), ALU.mult))
                step(nc.vector.tensor_copy(cm[:, :, 0:24].rearrange("p t (e r) -> p t e r", r=3),
                                           hot[:, :, 0:8].unsqueeze(3).to_broadcast([HALF, NT, 8, 3])), False)
                assert n[0] == m_gate.per, n

            def body(it, more):
                attention(it, "a0")
                dve.wait_ge(h_out, 16 * it)

                def behind_a0(t):
                    add_up(it, "a0", "a0_out", hin, t)
                    resid["a0"].wait(dve, it, t + 1)

                normalise(it, "f0", h, behind_a0)
                steps = [0]
                for s in range(2):
                    f_dev.wait(dve, it, s + 1)
                    nc.vector.reciprocal(qvar, qvar).then_inc(f_rs.sem, 1)
                    f_rsr.wait(dve, it, 2 * s + 1)
                    low(rowH[64:76, :], qvar, rowH[0:12, :]).then_inc(f_rsr.sem, 1)
                    if s:
                        h_bias.wait(dve, it)
                        for t in range(NT):
                            add_up(it, "f0", "f0_out0", h, t)
                    f_qc.wait(dve, it, 6 * s + 6)
                    for k, i in enumerate(BY_PAIR):
                        bank = S.wait(dve, it, f"f0_rs{s}", k)
                        tt(qc[:, i, :], qc[:, i, :], bank[:, 0:TT], ALU.mult).then_inc(f_t.sem, 1)
                        f_t.wait(dve, it, 6 * s + k + 1)
                        c = 2 * (i // 3)
                        nc.vector.tensor_scalar(qc[:, i, :], qc[:, i, :], w["f0n"][:, c:c + 1],
                                                w["f0n"][:, c + 1:c + 2], ALU.mult, ALU.add).then_inc(f_u.sem, 1)
                    if s == 0:
                        gates(it, steps, True)
                    for n in range(12):
                        bank = S.wait(dve, it, f"f0_S1{s}{n // 4}", n % 4)
                        largest(bank, 2 * (n % 2), 6 * s + n // 2).then_inc(f_max.sem, 1)
                    for i in range(3):
                        f_sum.wait(dve, it, 6 * s + 2 * i + 2)
                        nc.vector.reciprocal(sa[:, i, :], sa[:, i, :]).then_inc(f_den.sem, 1)
                        f_den.wait(dve, it, 3 * s + i + 1)
                        for x in range(2):
                            bank = C.wait(dve, it, f"f0_pv{s}", 2 * i + x)
                            r = slice(64 * x, 64 * x + 64)
                            tt(sc[r, i, :], bank[r, 0:TT], sa[r, i, :], ALU.mult).then_inc(f_quot.sem, 1)
                        if s == 0 and i == 0:
                            gates(it, steps, False)
                    bank = S.wait(dve, it, f"f0_g{s}", 0)
                    f_row.wait(dve, it, 2 * s + 1)
                    low(rowH[64:76, :], bank[0:12, 0:TT], rowH[0:12, :]).then_inc(f_row.sem, 1)
                    f_quot.wait(dve, it, 6 * s + 6)
                    for i in range(3):
                        bank = S.wait(dve, it, f"f0_gb{s}", i)
                        nc.vector.scalar_tensor_tensor(sc[:, i, :], sc[:, i, :], w["f0vb"][:, 3 * s + i:3 * s + i + 1],
                                                       bank[:, 0:TT], ALU.add, ALU.mult).then_inc(f_on.sem, 1)
                    for i in range(3):
                        f_onh.wait(dve, it, 3 * s + i + 1)
                        low(rl[:, i, :], sc[:, i, :], rh[:, i, :]).then_inc(f_onl.sem, 1)

                def behind_f0(t):
                    add_up(it, "f0", "f0_out1", h, t)
                    resid["f0"].wait(dve, it, 5 + t)

                resid["f0"].wait(dve, it, 4)
                normalise(it, "a1", h, behind_f0)
                attention(it, "a1")

                def behind_a1(t):
                    add_up(it, "a1", "a1_out", h, t)
                    resid["a1"].wait(dve, it, t + 1)

                normalise(it, "f1", h, behind_a1)
                router(it)
                bank = S.wait(dve, it, "f1_c", 0)
                m_row.wait(dve, it, 1)
                low(rowH[64:92, :], bank[0:28, 0:TT], rowH[0:28, :]).then_inc(m_row.sem, 1)
                for m in range(MOE_M):
                    bank = S.wait(dve, it, f"f1_cb{m}", 0)
                    m_relu.wait(dve, it, m + 1)
                    if m >= 3:
                        m_l.wait(dve, it, m - 2)
                    tt(sc[:, m % 3, :], work[:, m % P, :], bank[:, 0:TT], ALU.mult).then_inc(m_c.sem, 1)
                    m_c.wait(dve, it, m + 1)
                    tt(sc[:, m % 3, :], sc[:, m % 3, :], work[:, m % P, :], ALU.mult).then_inc(m_hid.sem, 1)
                    if m == NEXT_STATS and more:
                        measure_next(it + 1)
                    if m == NEXT_NORMED and more:
                        scale(it + 1, "a0", hin)
                if more:
                    turned(it + 1, "a0")
                for t in range(NT):
                    add_up(it, "f1", "f1_y", h, t)

            dve.wait_ge(ready, NREADY)
            measure_next(0)
            scale(0, "a0", hin)
            turned(0, "a0")
            all_steps(dve, body)

        @block.tensor
        def _(pe):
            def mm(out_, lhs, rhs, first, last):
                return nc.tensor.matmul(out_, lhs, rhs, start=first, stop=last, skip_group_check=True)

            def features(out_, c0, n=128, low_of=None):
                c = slice(c0, c0 + n)
                mm(out_, w["A"][:, c], xA[:, 0, :], True, False)
                mm(out_, w["Al"][:, c], xA[:, 0, :], False, False)
                mm(out_, w["B"][:, c], xB[:, 0, :], False, False)
                if low_of:
                    xl[low_of[1]].wait(pe, low_of[0])
                mm(out_, w["A"][:, c], xA[:, 1, :], False, False)
                return mm(out_, w["B"][:, c], xB[:, 1, :], False, True)

            def rows(out_, t, c0, n, every_other=False):
                def c(part):
                    if not every_other:
                        return w[part][:, c0:c0 + n]
                    return w[part][:, c0:c0 + 2 * n].rearrange("p (g x d) -> p g x d", x=2, d=64)[:, :, 0, :]

                if every_other:
                    out_ = out_.rearrange("p (g d) -> p g d", d=64)
                mm(out_, xA[:, 0, tok(t)], c("A"), True, False)
                mm(out_, xA[:, 0, tok(t)], c("Al"), False, False)
                mm(out_, xA[:, 1, tok(t)], c("A"), False, False)
                mm(out_, xB[:, 0, tok(t)], c("B"), False, False)
                return mm(out_, xB[:, 1, tok(t)], c("B"), False, True)

            def turn_tokens(it, s):
                two = [S.claim(pe, it - 1 if s == "a0" else it, s + "_x", k) for k in range(2)]
                for im in range(IMS):
                    normed[s].wait(pe, it, 4 * im + 4)
                    for k, bank in enumerate(two):
                        for t in (2 * im, 2 * im + 1):
                            last = nc.tensor.transpose(bank[:, tok(t)], xn[:, t, 128 * k:128 * k + 128],
                                                       ident[0:HALF, 0:HALF])
                        if im:
                            S.fill(last)

            def turn_rows(it, stage, src, n):
                bank = S.claim(pe, it, stage, 0)
                for t in range(NT):
                    last = nc.tensor.transpose(bank[0:n, tok(t)], src[:, t, :], ident[0:HALF, 0:HALF])
                S.fill(last)

            def project(it, stage, group, n, l_sig, l_of):
                for t in range(NT):
                    bank = C.claim(pe, it, stage, t)[0:HALF, 0:D]
                    for g in range(n):
                        if t % 2 == 0:
                            l_sig.wait(pe, it, l_of(g, t // 2))
                        c = slice((group + g) * D, (group + g + 1) * D)
                        mm(bank, rh[:, g, tok(t)], w["Kh"][:, c], g == 0, False)
                        mm(bank, rh[:, g, tok(t)], w["Kl"][:, c], False, False)
                        last = mm(bank, rl[:, g, tok(t)], w["Kh"][:, c], False, g == n - 1)
                    C.fill(last)

            def attention(it, s, c_qk, c_v, group):
                if s == "a0":
                    xl[s].wait(pe, it)
                else:
                    turn_tokens(it, s)
                    xh[s].wait(pe, it)
                for g in range(3):
                    bank = S.claim(pe, it, s + "_qk", g)
                    S.fill(features(bank[:, 0:TT], c_qk + 128 * g, 128, (it, s) if g == 0 and s == "a1" else None))
                for k in range(2):
                    bank = S.claim(pe, it, s + "_v", k)
                    for x in range(2):
                        last = rows(bank[0:HALF, D * x:D * x + D], 2 * k + x, c_v, D, s == "a0")
                    S.fill(last)

                def largest_of(n):
                    g = n // 2
                    if n % 2 == 0:
                        q_own[s].wait(pe, it, 3 * g + 3)
                        q_own3[s].wait(pe, it, g + 1)
                        k_h[s].wait(pe, it, 2 * g + 2)
                    for i in range(4):
                        head, im = 2 * n + i // 2, i % 2
                        bank = S.claim(pe, it, f"{s}_S1{n}", i)
                        for x in range(2):
                            last = mm(bank[0:HALF, TOK * x:TOK * x + TOK], q16[:, head, tok(2 * im + x)],
                                      k16_h[:, g, img(im)], True, True)
                        S.fill(last)

                def minus_max(g):
                    maxes[s].wait(pe, it, 8 * g + 8)
                    turn_rows(it, f"{s}_mx{g}", mx[:, :, 4 * g:4 * g + 4], 4)

                def scores(b):
                    g, im = b // 2, b % 2
                    if im == 0:
                        k_l[s].wait(pe, it, 2 * g + 2)
                        nm[s].wait(pe, it, g + 1)
                    for j in range(4):
                        bank = S.claim(pe, it, f"{s}_S2{b}", j)
                        for x in range(2):
                            o = bank[0:HALF, TOK * x:TOK * x + TOK]
                            q = q16[:, 4 * g + j, img(im)]
                            mm(o, k16_h[:, g, tok(2 * im + x)], q, True, False)
                            mm(o, k16_l[:, g, tok(2 * im + x)], q, False, False)
                            last = mm(o, eye[:, j:j + 1].to_broadcast([128, HALF]), m16[:, g, img(im)], False, True)
                        S.fill(last)

                def values(b):
                    g, im = b // 2, b % 2
                    bank = C.claim(pe, it, s + "_pv", b)
                    if b == 0:
                        va_in[s].wait(pe, it)
                        ones[s].wait(pe, it)
                    exps[s].wait(pe, it, 4 * b + 4)
                    for x in range(2):
                        for j in range(4):
                            last = mm(bank[32 * j:32 * j + 32, 0:TOK], va[:, 2 * im + x, 2 * g + j // 2, j % 2, :],
                                      probs[:, (4 * b + j) % P, TOK * x:TOK * x + TOK], x == 0, x == 1)
                    C.fill(last)

                for stage, n in S1_S2:
                    if stage == "S1":
                        largest_of(n)
                    elif stage == "mx":
                        minus_max(n)
                    else:
                        scores(n)
                        if n:
                            values(n - 1)
                values(5)
                project(it, s + "_out", group, 3, on_l[s], lambda g, im: 2 * g + im + 1)

            def body(it, more):
                attention(it, "a0", C_A0QK, C_A0QK + 64, K_O0)

                turn_tokens(it, "f0")
                xh["f0"].wait(pe, it)

                def values_of(t):
                    for k, (c, n) in enumerate(((C_F0V, NV0), (C_F0V + NV0, NV1))):
                        bank = S.claim(pe, it, "f0_v", 2 * t + k)
                        S.fill(rows(bank[0:HALF, 0:n], t, c, n))

                def variance(s, i):
                    if i == 0:
                        C.claim(pe, it, f"f0_var{s}", 0)
                    bank = C.banks[C.first[f"f0_var{s}"] % 4]
                    f_sq.wait(pe, it, 6 * s + i + 1)
                    last = mm(bank[0:12, 0:TT], sumcol[:, 10 - 2 * i:22 - 2 * i], sa[:, i % 3, :], i == 0, i == 5)
                    if i < 5:
                        last.then_inc(f_squ.sem, 1)
                    else:
                        C.fill(last)

                def q_and_k(s):
                    for i in range(6):
                        tile = 3 * s + i % 3 + (6 if i >= 3 else 0)
                        bank = S.claim(pe, it, f"f0_qk{s}", i)
                        S.fill(features(bank[:, 0:TT], C_F0QK + 128 * tile, 128, (it, "f0") if s + i == 0 else None))
                        if i >= 2:
                            variance(s, i - 2)

                q_and_k(0)
                values_of(0)
                variance(0, 4)
                variance(0, 5)
                for t in range(1, NT):
                    values_of(t)
                zeroed.wait(pe, it)
                for s in range(2):
                    f_rsr.wait(pe, it, 2 * s + 2)
                    for k, i in enumerate(BY_PAIR):
                        bank = S.claim(pe, it, f"f0_rs{s}", k)
                        S.fill(mm(bank[:, 0:TT], sel[:, i, :], rowH[:, :], True, True))

                    def largest_of(p):
                        f_h.wait(pe, it, 18 * s + 6 * p + 6)
                        for i in range(4):
                            hd, im = 2 * p + i // 2, i % 2
                            bank = S.claim(pe, it, f"f0_S1{s}{p}", i)
                            for x in range(2):
                                last = mm(bank[0:HALF, TOK * x:TOK * x + TOK], qs[:, hd, tok(2 * im + x)],
                                          ks[:, hd, img(im)], True, True)
                            S.fill(last)

                    def minus_max(p):
                        f_max.wait(pe, it, 12 * s + 4 * p + 4)
                        turn_rows(it, f"f0_mx{s}{p}", mx[:, :, 6 * s + 2 * p:6 * s + 2 * p + 2], 2)

                    def scores(hd):
                        if hd % 2 == 0:
                            f_l.wait(pe, it, 12 * s + 2 * hd + 4)
                            f_nm.wait(pe, it, 3 * s + hd // 2 + 1)
                        for im in range(IMS):
                            bank = S.claim(pe, it, f"f0_S2{s}{hd}", im)
                            for x in range(2):
                                o = bank[0:HALF, TOK * x:TOK * x + TOK]
                                keys = tok(2 * im + x)
                                mm(o, ks[:, hd, keys], qs[:, hd, img(im)], True, False)
                                mm(o, ks[:, hd, keys], qs[:, 6 + hd, img(im)], False, False)
                                mm(o, ks[:, 6 + hd, keys], qs[:, hd, img(im)], False, False)
                                row = 96 + hd % 2
                                last = mm(o, eye[:, row:row + 1].to_broadcast([128, HALF]), m64[:, hd // 2, img(im)],
                                          False, True)
                            S.fill(last)

                    def values(hd):
                        head = 6 * s + hd
                        bank = C.claim(pe, it, f"f0_pv{s}", hd)
                        f_exp.wait(pe, it, 12 * s + 2 * hd + 2)
                        block_ = slice(0, 2) if head % 2 == 0 else slice(1, 3)
                        for im in range(IMS):
                            for x in range(2):
                                v = vf[:, 2 * im + x, head // 2, block_, :].rearrange("p a d -> p (a d)")
                                last = mm(bank[:, img(im)], v,
                                          probs[:, BY_PAIR[(2 * hd + im) % P], TOK * x:TOK * x + TOK], x == 0, x == 1)
                        C.fill(last)

                    for stage, n in F0_S1_S2:
                        if stage == "S1":
                            largest_of(n)
                        elif stage == "mx":
                            minus_max(n)
                        else:
                            scores(n)
                            if n:
                                values(n - 1)
                    values(5)
                    f_gate.wait(pe, it)
                    turn_rows(it, f"f0_g{s}", gm, NH)
                    if s == 0:
                        q_and_k(1)
                    f_row.wait(pe, it, 2 * s + 2)
                    for i in range(3):
                        bank = S.claim(pe, it, f"f0_gb{s}", i)
                        S.fill(mm(bank[:, 0:TT], sel[:, 3 * s + i, :], rowH[:, :], True, True))
                    if s == 0:
                        variance(1, 4)
                        variance(1, 5)
                    project(it, f"f0_out{s}", K_PJ + 3 * s, 3, f_onl, lambda g, im: 3 * s + g + 1)

                attention(it, "a1", C_A1QK, C_A1V, K_O1)

                turn_tokens(it, "f1")
                xl["f1"].wait(pe, it)
                bank = S.claim(pe, it, "f1_r", 0)
                for t in range(NT):
                    last = rows(bank[0:HALF, 8 * t:8 * t + 8], t, C_RT, 8)
                S.fill(last)
                def hidden(m):
                    bank_ = S.claim(pe, it, f"f1_h{m}", 0)
                    S.fill(features(bank_[:, 0:TT], C_W1 + 128 * m))

                for m in range(LEAD):
                    hidden(m)
                m_gate.wait(pe, it)
                turn_rows(it, "f1_c", cm, 28)
                m_row.wait(pe, it, 2)

                def weight(m):
                    bank_ = S.claim(pe, it, f"f1_cb{m}", 0)
                    S.fill(mm(bank_[:, 0:TT], sel[:, m, :], rowH[:, :], True, True))

                def outward(m):
                    m_l.wait(pe, it, m + 1)
                    c = slice((K_W2 + m) * D, (K_W2 + m + 1) * D)
                    for t in range(NT):
                        b = C.claim(pe, it, "f1_y", t) if m == 0 else C.banks[(C.first["f1_y"] + t) % 4]
                        o = b[0:HALF, 0:D]
                        mm(o, rh[:, m % 3, tok(t)], w["Kh"][:, c], m == 0, False)
                        mm(o, rh[:, m % 3, tok(t)], w["Kl"][:, c], False, False)
                        last = mm(o, rl[:, m % 3, tok(t)], w["Kh"][:, c], False, m == MOE_M - 1)
                        if m == MOE_M - 1:
                            C.fill(last)
                    if m < MOE_M - 1:
                        last.then_inc(m_used.sem, 1)

                weight(0)
                weight(1)
                for m in range(MOE_M):
                    if m + LEAD < MOE_M:
                        hidden(m + LEAD)
                    if m + 2 < MOE_M:
                        weight(m + 2)
                    if m == MOE_M - 2 and more:
                        turn_tokens(it + 1, "a0")
                    outward(m)

            pe.wait_ge(ready, NREADY)
            turn_tokens(0, "a0")
            all_steps(pe, body)


def vit_tower(nc, a, out):
    h0 = nc.dram_tensor("patch_tokens", (TOK * IMAGES, D), F32).ap()
    with ExitStack() as ctx:
        def sb(name, shape, dt=F32):
            return ctx.enter_context(nc.sbuf_tensor(name, shape, dt))

        w = {
            "A": sb("wA", [128, NCOL], F32R), "Al": sb("wAl", [128, NCOL], F32R), "B": sb("wB", [128, NCOL], F32R),
            "Kh": sb("wKh", [128, NK * D], F32R), "Kl": sb("wKl", [128, NK * D], F32R),
            "sel": sb("sel", [SELROWS, MOE_M, 128], F32R), "sumcol": sb("sumcol", [128, 22]),
            "ident": sb("ident", [128, 128]), "cos": sb("cos", [128, TOK]), "sin": sb("sin", [128, TOK]),
            "eye": sb("eye", [128, 98], F32R), "own": sb("own", [128, 4]),
            "a1qkb": sb("a1qkb", [128, 3]), "f0n": sb("f0n", [128, 4]), "f0vb": sb("f0vb", [128, 6]),
            "f0qkb": sb("f0qkb", [128, 12]), "a1vb": sb("a1vb", [128, 3]), "f0pb": sb("f0pb", [HALF, D]),
            "bal": sb("bal", [HALF, 8]), "iota": sb("iota", [HALF, 10]),
        }
        setup_and_patches(nc, a, w, h0)
        layers(nc, a, w, h0, out)


def constants():
    import numpy as np

    p = np.arange(128)
    sel = np.zeros((SELROWS, MOE_M, 128), np.float32)
    for m in range(MOE_M):
        for half in range(2):
            for part in (0, 64):
                sel[part + 2 * m + half, m, 64 * half:64 * half + 64] = 1.0
    sumcol = np.zeros((128, 22), np.float32)
    sumcol[:64, 10] = sumcol[64:, 11] = 1.0 / 64
    position = np.array([i * GRID + j for i, j in token_classes()[1]], np.float32)
    inv = (1.0 / np.float32(10000.0) ** (np.arange(0, 16, 2, dtype=np.float32) / np.float32(16))).astype(np.float32)
    angle = inv[p % 8][:, None] * position[None, :]
    sign = np.where(p % 16 < 8, -1.0, 1.0).astype(np.float32)[:, None]
    return {
        "blockmean": ((p[:, None] // 64 == p[None, :] // 64) / 64).astype(np.float32),
        "sel": sel.reshape(SELROWS, -1), "sumcol": sumcol, "ident": np.eye(128, dtype=np.float32),
        "cos": np.cos(angle).astype(np.float32), "sin": (np.sin(angle) * sign).astype(np.float32),
        "own": (p[:, None] % 64 // 16 == np.arange(4)).astype(np.float32),
        "iota": np.tile(np.arange(10, dtype=np.float32), (HALF, 1)),
    }


def lay_out(x, i):
    import numpy as np

    f = {k: np.asarray(v) for k, v in i.items()}
    x = np.asarray(x).reshape(IMAGES, GRID, 2, 8, GRID, 2, 8, 3)
    x = x.transpose(1, 4, 2, 5, 3, 6, 7, 0).reshape(GRID, GRID, 768, IMAGES)
    cls, _ = token_classes()
    tiles = []
    for c in cls:
        for n in range(0, len(c), 2):
            two = [x[i_, j] for i_, j in c[n:n + 2]]
            if len(two) == 1:
                two.append(np.zeros_like(two[0]))
            t = np.concatenate(two, axis=1)
            tiles.append(t.reshape(KC, 128, 128).transpose(1, 0, 2).reshape(128, KC * 128))
    tokW = f["L0_tok_W"].reshape(2, 8, 2, 8, 5, 3, D).transpose(4, 0, 2, 1, 3, 5, 6).reshape(5, KC, 128, D)

    def first(wt):
        return wt[:128]

    def rest(wt):
        return np.concatenate([wt[128:D], wt[128:D]], 0)

    def in_groups(qk):
        return qk.reshape(-1, 2, 3, 64).transpose(0, 2, 1, 3).reshape(-1, 2 * D)

    w1 = np.concatenate(list(f["L1_ffn_w1"]) + [f["L1_ffn_w_fc_sh"], np.zeros((D, 64), np.float32)], 1)
    cols = np.concatenate([
        in_groups(f["L0_attn_w_qkv"][:, :2 * D]), in_groups(f["L1_attn_w_qkv"].T[:, :2 * D]),
        f["L1_attn_w_qkv"].T[:, 2 * D:], f["L0_ffn_qkv_w"],
        f["L0_ffn_wg_w"], f["L0_ffn_wg0_w"], f["L0_ffn_wg1_w"], f["L1_ffn_router_w"].T, w1], 1)
    assert cols.shape[1] == NCOL

    def spread(wo, bias=None):
        g = np.zeros((3, 4, 32, D), np.float32)
        g[:, :, :16] = wo.reshape(3, 4, 16, D)
        if bias is not None:
            g[0, 0, 16] = bias
        return g.reshape(3, 128, D)

    w2 = np.concatenate([f["L1_ffn_w2"].reshape(-1, D), f["L1_ffn_w_proj_sh"], np.zeros((64, D), np.float32)], 0)
    groups = np.concatenate([
        w2.reshape(MOE_M, 128, D), f["L0_ffn_proj_w"].reshape(6, 128, D), spread(f["L0_attn_w_out"]),
        spread(f["L1_attn_w_proj"].T, f["L1_attn_b_proj"])], 0)

    def per_head(b):
        g = np.zeros((3, 4, 32), np.float32)
        g[:, :, :16] = b.reshape(3, 4, 16)
        return g.reshape(3, 128).T

    a1b, f0b = f["L1_attn_b_qkv"], f["L0_ffn_qkv_b"]
    norm = [np.tile(f[f"L0_ffn_{k}"], 2) for k in ("q_norm_w", "q_norm_b", "k_norm_w", "k_norm_b")]
    return {
        "px": np.stack(tiles), "tokW": tokW.transpose(2, 0, 1, 3), "tokb": np.tile(f["L0_tok_b"], (128, 1)),
        "WA": first(cols), "WB": rest(cols), "WK": groups.transpose(1, 0, 2).reshape(128, NK * D),
        "qkb": f0b[:2 * 768].reshape(12, 128).T, "a1qkb": in_groups(a1b[None, :2 * D]).reshape(3, 128).T,
        "f0n": np.stack(norm, 1), "f0vb": f0b[2 * 768:].reshape(6, 128).T, "a1vb": per_head(a1b[2 * D:]),
        "f0pb": np.tile(f["L0_ffn_proj_b"], (HALF, 1)), "bal": np.tile(f["L1_ffn_balance_bias"], (HALF, 1)),
    }


def kernel(x, **inputs):
    import concourse.bacc as bacc
    import numpy as np
    from concourse.bass_utils import run_bass_kernel_spmd

    arrays = {**lay_out(x, inputs), **constants()}
    arrays = {"in_" + k: np.ascontiguousarray(v) for k, v in arrays.items()}
    nc = bacc.Bacc("TRN2", target_bir_lowering=False, num_devices=1)
    a = {k[3:]: nc.dram_tensor(k, v.shape, F32, kind="ExternalInput").ap() for k, v in arrays.items()}
    out = nc.dram_tensor("out", (IMAGES // IMS, HALF, NT, D), F32, kind="ExternalOutput").ap()
    vit_tower(nc, a, out)
    got = run_bass_kernel_spmd(nc, [arrays], core_ids=[0]).results[0]["out"]
    slots = got.reshape(-1, HALF, IMS, 2, D).transpose(0, 2, 3, 1, 4).reshape(IMAGES, TOK, D)
    at = [i * GRID + j for i, j in token_classes()[1]]
    full = np.empty_like(slots)
    full[:, at] = slots
    return full
```
